# Optimizing a Trainium2 kernel written in Bass

```python
import numpy as np
import jax
import jax.numpy as jnp

def _softmax(x, axis=-1):
    return jax.nn.softmax(x, axis=axis)

def _gelu(x):
    return jax.nn.gelu(x, approximate=True)

def _silu(x):
    return jax.nn.silu(x)

def _sigmoid(x):
    return jax.nn.sigmoid(x)

def _layernorm(x, axis=-1, eps=1e-05):
    m = jnp.mean(x, axis=axis, keepdims=True)
    v = jnp.var(x, axis=axis, keepdims=True)
    return (x - m) / jnp.sqrt(v + eps)

def _scatter_add(tgt, idx, src, axis=0):
    return tgt.at[idx].add(src)

def _segment_sum(src, seg, n):
    return jax.ops.segment_sum(src, seg, n)
kernel_name = 'mk_hybrid_d1_jaxref_r8_45168e'

def setup_inputs(seed: int=0):
    np.random.seed(seed)
    _w = jnp.asarray

    def _L0_attn_a_setup():
        import jax, jax.numpy as jnp
        import numpy as np
        D_MODEL = 128
        D_STATE = 16
        DT_RANK = 64
        DT_MIN = 0.001
        DT_MAX = 0.1
        key = jax.random.key(seed)
        ks = jax.random.split(key, 7)
        B, S = (2, 256)
        return {'x': jax.random.normal(ks[0], (B, S, D_MODEL), jnp.float32), 'w_in': jax.random.normal(ks[1], (D_MODEL, D_MODEL), jnp.float32) / np.sqrt(D_MODEL).astype(np.float32), 'w_x': jax.random.normal(ks[2], (D_MODEL, DT_RANK + 2 * D_STATE), jnp.float32) / np.sqrt(D_MODEL).astype(np.float32), 'w_dt': jax.random.normal(ks[3], (DT_RANK, D_MODEL), jnp.float32) / np.sqrt(DT_RANK).astype(np.float32), 'b_dt': jnp.zeros((D_MODEL,), jnp.float32), 'A_log': jax.random.normal(ks[5], (D_MODEL, D_STATE), jnp.float32) * 0.5, 'Dp': jax.random.normal(ks[6], (D_MODEL,), jnp.float32)}
    _L0_attn_a_in = _L0_attn_a_setup()

    def _L0_attn_b_setup():
        import jax, jax.numpy as jnp
        import numpy as np
        D = 128
        FW = 64
        DEPTH = 2
        E = D * (DEPTH + 1)
        B, L = (2, 512)

        def _fftconv(x_bdl, h, bias_d):
            Lq = x_bdl.shape[-1]
            n = 2 * Lq
            Xf = jnp.fft.rfft(x_bdl, n=n)
            Hf = jnp.fft.rfft(h, n=n) / n
            y = jnp.fft.irfft(Xf * Hf, n=n, norm='forward')[..., :Lq]
            return y + x_bdl * bias_d[:, None]
        key = jax.random.key(seed)
        ks = jax.random.split(key, 12)
        s = lambda k, shape, scale: jax.random.normal(k, shape, dtype=jnp.float32) * scale
        return {'x': jax.random.normal(ks[0], (B, L, D), dtype=jnp.float32), 'w_in': s(ks[1], (D, E), 0.02), 'b_in': jnp.zeros((E,), jnp.float32), 'w_conv': s(ks[2], (E, 1, 3), 0.5), 'b_conv': jnp.zeros((E,), jnp.float32), 'w1': s(ks[3], (3, FW), 0.5), 'b1': jnp.zeros((FW,), jnp.float32), 'w2': s(ks[4], (FW, FW), 0.1), 'b2': jnp.zeros((FW,), jnp.float32), 'w3': s(ks[5], (FW, D), 0.1), 'filt_bias': jax.random.normal(ks[6], (D,), dtype=jnp.float32), 'w_out': s(ks[7], (D, D), 0.02), 'b_out': jnp.zeros((D,), jnp.float32)}
    _L0_attn_b_in = _L0_attn_b_setup()

    def _L0_ffn_setup():
        import jax, jax.numpy as jnp
        import numpy as np
        key = jax.random.key(seed)
        ks = jax.random.split(key, 5)
        B, T, D, E = (4, 256, 128, 8)
        inputs = jax.random.normal(ks[0], (B, T, D), dtype=jnp.float32)
        Wr = jax.random.normal(ks[1], (D, E), dtype=jnp.float32) * 0.02
        br = jnp.zeros((E,), dtype=jnp.float32)
        W1 = jax.random.normal(ks[2], (E, D, D), dtype=jnp.float32) * 0.02
        b1 = jnp.zeros((E, D), dtype=jnp.float32)
        W2 = jax.random.normal(ks[3], (E, D, D), dtype=jnp.float32) * 0.02
        b2 = jnp.zeros((E, D), dtype=jnp.float32)
        return {'inputs': inputs, 'Wr': Wr, 'br': br, 'W1': W1, 'b1': b1, 'W2': W2, 'b2': b2}
    _L0_ffn_in = _L0_ffn_setup()
    _d = {'L0_attn_a_x': _L0_attn_a_in['x'], 'L0_attn_a_w_in': _L0_attn_a_in['w_in'], 'L0_attn_a_w_x': _L0_attn_a_in['w_x'], 'L0_attn_a_w_dt': _L0_attn_a_in['w_dt'], 'L0_attn_a_b_dt': _L0_attn_a_in['b_dt'], 'L0_attn_a_A_log': _L0_attn_a_in['A_log'], 'L0_attn_a_Dp': _L0_attn_a_in['Dp'], 'L0_attn_b_w_in': _L0_attn_b_in['w_in'], 'L0_attn_b_b_in': _L0_attn_b_in['b_in'], 'L0_attn_b_w_conv': _L0_attn_b_in['w_conv'], 'L0_attn_b_b_conv': _L0_attn_b_in['b_conv'], 'L0_attn_b_w1': _L0_attn_b_in['w1'], 'L0_attn_b_b1': _L0_attn_b_in['b1'], 'L0_attn_b_w2': _L0_attn_b_in['w2'], 'L0_attn_b_b2': _L0_attn_b_in['b2'], 'L0_attn_b_w3': _L0_attn_b_in['w3'], 'L0_attn_b_filt_bias': _L0_attn_b_in['filt_bias'], 'L0_attn_b_w_out': _L0_attn_b_in['w_out'], 'L0_attn_b_b_out': _L0_attn_b_in['b_out'], 'L0_ffn_Wr': _L0_ffn_in['Wr'], 'L0_ffn_br': _L0_ffn_in['br'], 'L0_ffn_W1': _L0_ffn_in['W1'], 'L0_ffn_b1': _L0_ffn_in['b1'], 'L0_ffn_W2': _L0_ffn_in['W2'], 'L0_ffn_b2': _L0_ffn_in['b2']}
    _x0 = _d['L0_attn_a_x']
    _d['L0_attn_a_x'] = jax.random.normal(jax.random.fold_in(jax.random.key(seed), 1), (4, 1024, 128), dtype=_x0.dtype)
    del _x0
    return _d

def reference(L0_attn_a_x, L0_attn_a_w_in, L0_attn_a_w_x, L0_attn_a_w_dt, L0_attn_a_b_dt, L0_attn_a_A_log, L0_attn_a_Dp, L0_attn_b_w_in, L0_attn_b_b_in, L0_attn_b_w_conv, L0_attn_b_b_conv, L0_attn_b_w1, L0_attn_b_b1, L0_attn_b_w2, L0_attn_b_b2, L0_attn_b_w3, L0_attn_b_filt_bias, L0_attn_b_w_out, L0_attn_b_b_out, L0_ffn_Wr, L0_ffn_br, L0_ffn_W1, L0_ffn_b1, L0_ffn_W2, L0_ffn_b2):

    def _L0_attn_a_ref(x, w_in, w_x, w_dt, b_dt, A_log, Dp):
        import jax, jax.numpy as jnp
        import numpy as np
        D_MODEL = 128
        D_STATE = 16
        DT_RANK = 64
        DT_MIN = 0.001
        DT_MAX = 0.1
        x_in = jnp.einsum('bsd,de->bse', x, w_in)
        proj = jnp.einsum('bsd,dp->bsp', x_in, w_x)
        dt_low, Bm, Cm = jnp.split(proj, [DT_RANK, DT_RANK + D_STATE], axis=-1)
        dt = jax.nn.softplus(jnp.einsum('bsr,rd->bsd', dt_low, w_dt) + b_dt) * (DT_MAX - DT_MIN) + DT_MIN
        A = -jnp.exp(A_log)
        b, s, d = x.shape
        h0 = jnp.zeros((b, d, D_STATE), x.dtype)
        dt_tm = jnp.swapaxes(dt, 0, 1)
        u_tm = jnp.swapaxes(x_in, 0, 1)
        B_tm = jnp.swapaxes(Bm, 0, 1)
        C_tm = jnp.swapaxes(Cm, 0, 1)

        def step(h, inp):
            dtt, ut, bt, ct = inp
            dA = dtt[:, :, None] * A
            barA = jnp.exp(dA)
            inp_term = jnp.einsum('bdn,bn,bd->bn', dA, bt, ut)
            h = barA * h + inp_term[:, None, :]
            y = jnp.einsum('bdn,bn->bd', h, ct) + Dp * ut
            return (h, y)
        _, ys = jax.lax.scan(step, h0, (dt_tm, u_tm, B_tm, C_tm))
        return jnp.swapaxes(ys, 0, 1)

    def _L0_attn_b_ref(x, w_in, b_in, w_conv, b_conv, w1, b1, w2, b2, w3, filt_bias, w_out, b_out):
        import jax, jax.numpy as jnp
        import numpy as np
        D = 128
        FW = 64
        DEPTH = 2
        E = D * (DEPTH + 1)
        B, L = (2, 512)

        def _fftconv(x_bdl, h, bias_d):
            Lq = x_bdl.shape[-1]
            n = 2 * Lq
            Xf = jnp.fft.rfft(x_bdl, n=n)
            Hf = jnp.fft.rfft(h, n=n) / n
            y = jnp.fft.irfft(Xf * Hf, n=n, norm='forward')[..., :Lq]
            return y + x_bdl * bias_d[:, None]
        _, Lx, Dm = x.shape
        u = (x @ w_in + b_in).transpose(0, 2, 1)
        u = jax.lax.conv_general_dilated(u, w_conv, window_strides=(1,), padding=[(2, 2)], feature_group_count=u.shape[1], dimension_numbers=('NCH', 'OIH', 'NCH'))
        u = (u + b_conv[None, :, None])[..., :Lx]
        streams = [u[:, i * Dm:(i + 1) * Dm, :] for i in range(DEPTH + 1)]
        t = jnp.linspace(0.0, 1.0, Lx)
        pos = jnp.tile(t[:, None], (1, 3))
        hmlp = jax.nn.silu(pos @ w1 + b1)
        hmlp = jax.nn.silu(hmlp @ w2 + b2)
        filters = hmlp @ w3 * jnp.exp(-t[:, None] * jnp.abs(filt_bias)[None, :])
        v = streams[-1]
        for i in range(DEPTH - 1):
            v = v * streams[i]
            v = _fftconv(v, filters[i], filt_bias)
        out = (v * streams[0]).transpose(0, 2, 1) @ w_out + b_out
        return out

    def _L0_ffn_ref(inputs, Wr, br, W1, b1, W2, b2):
        import jax, jax.numpy as jnp
        import numpy as np
        B, T, D = inputs.shape
        E = Wr.shape[1]
        x = inputs.reshape(B * T, D)
        N = x.shape[0]
        C = N // E
        logits = x @ Wr + br
        probs = jax.nn.softmax(logits, axis=-1)
        gate = jnp.max(probs, axis=-1, keepdims=True)
        idx = jnp.argmax(probs, axis=-1)
        mask = jax.nn.one_hot(idx, E, dtype=jnp.float32)
        pos = (jnp.cumsum(mask, axis=0) * mask).astype(jnp.int32)
        mask = mask * (pos < C).astype(jnp.float32)
        mask_flat = jnp.sum(mask, axis=-1, keepdims=True)
        gate = gate * mask_flat
        combine = (gate * mask_flat * jax.nn.one_hot(idx, E, dtype=jnp.float32))[..., None] * jax.nn.one_hot(pos, C, dtype=jnp.float32)
        dispatch = combine
        expert_in = jnp.einsum('nd,nec->ecd', x, dispatch)
        h = jax.nn.relu(jnp.einsum('ecd,edf->ecf', expert_in, W1) + b1[:, None, :])
        eo = jnp.einsum('ecf,efd->ecd', h, W2) + b2[:, None, :]
        out = jnp.einsum('ecd,nec->nd', eo, combine)
        return out.reshape(B, T, D)
    x = L0_attn_a_x
    x = x + _L0_attn_a_ref(_layernorm(x, axis=-1), L0_attn_a_w_in, L0_attn_a_w_x, L0_attn_a_w_dt, L0_attn_a_b_dt, L0_attn_a_A_log, L0_attn_a_Dp)
    x = x + _L0_ffn_ref(_layernorm(x, axis=-1), L0_ffn_Wr, L0_ffn_br, L0_ffn_W1, L0_ffn_b1, L0_ffn_W2, L0_ffn_b2)
    x = x + _L0_attn_b_ref(_layernorm(x, axis=-1), L0_attn_b_w_in, L0_attn_b_b_in, L0_attn_b_w_conv, L0_attn_b_b_conv, L0_attn_b_w1, L0_attn_b_b1, L0_attn_b_w2, L0_attn_b_b2, L0_attn_b_w3, L0_attn_b_filt_bias, L0_attn_b_w_out, L0_attn_b_b_out)
    x = x + _L0_ffn_ref(_layernorm(x, axis=-1), L0_ffn_Wr, L0_ffn_br, L0_ffn_W1, L0_ffn_b1, L0_ffn_W2, L0_ffn_b2)
    return x

_drawn_inputs = setup_inputs


def setup_inputs(seed=0):
    import zlib

    import numpy as np

    out = dict(_drawn_inputs(seed))
    spreads = {'L0_attn_a_b_dt': (0.0, 0.1),
     'L0_attn_b_b_in': (0.0, 0.1),
     'L0_attn_b_b_conv': (0.0, 0.1),
     'L0_attn_b_b1': (0.0, 0.1),
     'L0_attn_b_b2': (0.0, 0.1),
     'L0_attn_b_b_out': (0.0, 0.1),
     'L0_ffn_br': (0.0, 0.1),
     'L0_ffn_b1': (0.0, 0.1),
     'L0_ffn_b2': (0.0, 0.1)}
    factors = {}
    for name, (base, spread) in spreads.items():
        noise = np.random.default_rng([zlib.crc32(name.encode()), seed]).standard_normal(out[name].shape)
        drawn = base * np.exp(spread * noise) if base else spread * noise
        out[name] = jnp.asarray(drawn.astype(out[name].dtype))
    for name, factor in factors.items():
        out[name] = (out[name] * factor).astype(out[name].dtype)
    return out
```

```python
from contextlib import ExitStack

import numpy as np

import concourse.bass as bass
from concourse import mybir

F32 = mybir.dt.float32
BF16 = mybir.dt.bfloat16
I32 = mybir.dt.int32
ALU = mybir.AluOpType
ACT = mybir.ActivationFunctionType
AX = mybir.AxisListType.X

P = 128
BATCH, SEQ, D = 4, 1024, 128
TOKENS = BATCH * SEQ
TILES = TOKENS // P
BT = SEQ // P
HALF = SEQ // 2
HT = HALF // P
STATES = 16
RANK = 64
GROUP = P // STATES
GROUPS = D // GROUP
PARTS = 3
QUARTER = 32
QG = QUARTER // GROUP
EXPERTS = 8
CAP = TOKENS // EXPERTS
TAPS = 3
FW = 64
DT_MIN, DT_MAX = 0.001, 0.1
EPS = 1e-5

C_ID, C_FLIP, C_TRI = 0, P, 2 * P
C_SEL = 3 * P
C_RED = C_SEL + QG * P
C_RANK = C_RED + GROUP
C_TOKEN = C_RANK + EXPERTS
C_END = C_TOKEN + TILES


def constant_table():
    t = np.zeros((P, C_END), np.float32)
    r = np.arange(P)
    t[r, C_ID + r] = 1.0
    t[r, C_FLIP + P - 1 - r] = 1.0
    t[:, C_TRI:C_TRI + P] = r[:, None] <= r[None, :]
    for s in range(QG):
        for part in range(PARTS):
            for p in range(P):
                t[part * QUARTER + s * GROUP + p % GROUP, C_SEL + s * P + p] = 1.0
    t[r, C_RED + r % GROUP] = 1.0
    t[:, C_RANK:C_RANK + EXPERTS] = EXPERTS - np.arange(EXPERTS)
    t[:, C_TOKEN:C_TOKEN + TILES] = TOKENS + np.arange(TILES)[None, :] * P + r[:, None]
    return t


class Kit:

    def __init__(self, nc, ctx, memory=None):
        self.nc, self.ctx, self.memory = nc, ctx, memory or ctx

    def sb(self, name, shape, dt=F32):
        return self.memory.enter_context(self.nc.sbuf_tensor(name, shape, dt))

    def sem(self, name):
        return self.ctx.enter_context(self.nc.semaphore(name))


def build(nc, t):
    with ExitStack() as ctx:
        k = Kit(nc, ctx)
        ps = ctx.enter_context(nc.psum_tensor("ps", [P, 8 * HALF], F32))
        m = {}
        m["x"] = k.sb("x", [P, TOKENS])
        m["const"] = k.sb("const", [P, C_END])
        m["tri"] = k.sb("tri", [P, P], BF16)
        m["neg_half"] = k.sb("neg_half", [P, BT])
        m["ones"] = k.sb("ones", [P, P], BF16)
        m["zero"] = k.sb("zero", [P, 1024])
        m["big"] = [k.sb(f"big{i}", [P, TOKENS]) for i in range(5)]
        m["w_out"] = k.sb("w_out", [P, D])
        m["b_out"] = k.sb("b_out", [1, D])
        slots = nc.dram_tensor("slots", (2 * TOKENS, D), F32).ap()
        answers = nc.dram_tensor("answers", (TOKENS, D), F32).ap()
        steps = nc.dram_tensor("steps", (P, BATCH * PARTS * SEQ), BF16).ap()
        taps = nc.dram_tensor("taps", (1, 4 * P), F32).ap()
        zeroed = k.sem("zeroed")
        m["passed"] = {e.engine: k.sem(f"passed_{n}") for n, e in (("pool", nc.gpsimd), ("dve", nc.vector), ("sp", nc.sync))}
        with ExitStack() as early:
            ke = Kit(nc, ctx, early)
            project(nc, ke, ps, m, t, slots, taps, zeroed)
            step(nc, ke, ps, m, t, steps)
            scan(nc, ke, ps, m, t)
        experts(nc, k, ps, m, t, slots, answers, zeroed, "f", None)
        conv(nc, k, ps, m, t, taps)
        experts(nc, k, ps, m, t, slots, answers, zeroed, "g", t["out"])


def due(count):
    return count + 1


def prime(eng, *sems):
    for s in sems:
        eng.sem_inc(s, 1)


def standalone(eng, passed):
    eng.sem_inc(passed[eng.engine], 1)


def bank(ps, i, n=1):
    return ps[:, i * HALF:(i + n) * HALF]


def project(nc, k, ps, m, t, slots, taps, zeroed):
    x, const, zero = m["x"], m["const"], m["zero"]
    relu_z, exp_z, inp, c_rows, u = m["big"]
    ident = const[:, C_ID:C_ID + P]
    w_in = k.sb("w_in", [P, D])
    w_x = k.sb("w_x", [P, RANK + 2 * STATES])
    w_dt = k.sb("w_dt", [RANK, D])
    b_dt = k.sb("b_dt", [P, 1])
    skip = k.sb("skip", [P, D])
    w_skip = k.sb("w_skip", [P, D])
    w_in_t = k.sb("w_in_t", [P, D])
    w_low = k.sb("w_low", [RANK, D])
    w_z = k.sb("w_z", [P, D])
    w_b = k.sb("w_b", [P, P])
    w_c = k.sb("w_c", [P, P])
    stats = k.sb("stats", [P, 2, HT, 6])
    moments = k.sb("moments", [P, 2, HT, 2])
    spread = k.sb("spread", [P, 2, HT])
    rstd = k.sb("rstd", [P, 2, HT])
    xn = k.sb("xn", [P, 2, HALF])
    xn_t = k.sb("xn_t", [P, 2, HALF])
    abs_z = k.sb("abs_z", [P, 2, HALF])
    m["xn"], m["xn_t"], m["stats"], m["moments"], m["rstd"] = xn, xn_t, stats, moments, rstd

    x_in, weights_in, consts_in = k.sem("x_in"), k.sem("weights_in"), k.sem("consts_in")
    half_made = k.sem("half_made")
    m["consts_in"] = consts_in
    zero_made, tri_made = k.sem("zero_made"), k.sem("tri_made")
    skip_made, fold_psum, fold_done = k.sem("skip_made"), k.sem("fold_psum"), k.sem("fold_done")
    moments_done, rstd_done = k.sem("moments_done"), k.sem("rstd_done")
    xn_ready, xt_psum, xt_ready = k.sem("xn_ready"), k.sem("xt_psum"), k.sem("xt_ready")
    z_psum, ubc_psum, skip_psum = k.sem("z_psum"), k.sem("ubc_psum"), k.sem("skip_psum")
    abs_done = k.sem("abs_done")
    z_taken, ubc_taken, skip_taken, exp_done = k.sem("z_taken"), k.sem("ubc_taken"), k.sem("skip_taken"), k.sem("exp_done")

    with nc.Block() as block:

        @block.sync
        def _(sp):
            sp.dma_start(x[:, :].rearrange("p (i d) -> p i d", d=D),
                         t["x"].rearrange("b (i p) d -> p (b i) d", p=P)).then_inc(x_in, 16)
            sp.wait_ge(zero_made, 1)
            for i in range(4):
                sp.dma_start(slots[i * 1024:(i + 1) * 1024, :].rearrange("(p j) d -> p (j d)", p=P),
                             zero[:, :]).then_inc(zeroed, 16)
            sp.dma_start(taps[:, :], zero[0:1, 0:4 * P]).then_inc(zeroed, 16)

        @block.gpsimd
        def _(pool):
            pool.memset(zero[:, :], 0.0).then_inc(zero_made, 1)
            pool.memset(m["ones"][:, :], 1.0)
            pool.memset(m["neg_half"][:, :], -0.5).then_inc(half_made, 1)
            pool.wait_ge(half_made, 1)
            with pool.Fori(0, BATCH) as b:
                for q in range(2):
                    pool.wait_ge(moments_done, b * 2 + (q + 1))
                    pool.tensor_tensor(rstd[:, q, :], spread[:, q, :], m["neg_half"][:, 0:HT], ALU.pow).then_inc(rstd_done, 1)

        @block.scalar
        def _(act):
            prime(act, xt_ready, ubc_taken, exp_done)
            act.dma_start(const[:, :], t["table"]).then_inc(consts_in, 16)
            act.dma_start(w_in[:, :], t["a_w_in"]).then_inc(weights_in, 16)
            act.dma_start(w_x[:, :], t["a_w_x"]).then_inc(weights_in, 16)
            act.dma_start(w_dt[:, :], t["a_w_dt"]).then_inc(weights_in, 16)
            act.dma_start(b_dt[:, :], t["a_b_dt"].rearrange("(d o) -> d o", o=1)).then_inc(weights_in, 16)
            act.dma_start(skip[:, :], t["a_Dp"].rearrange("(o d) -> o d", o=1).broadcast_to([P, D])).then_inc(weights_in, 16)
            act.wait_ge(fold_psum, 1)
            act.copy(w_in_t[:, :], ps[:, 0:D]).then_inc(fold_done, 1)
            act.wait_ge(fold_psum, 2)
            act.copy(w_low[:, :], ps[0:RANK, HALF:HALF + D])
            act.copy(w_b[:, :], ps[:, 2 * HALF:2 * HALF + P])
            act.copy(w_c[:, :], ps[:, 3 * HALF:3 * HALF + P]).then_inc(fold_done, 1)
            act.wait_ge(fold_psum, 3)
            act.copy(w_z[:, :], ps[:, 4 * HALF:4 * HALF + D]).then_inc(fold_done, 1)
            with act.Fori(0, BATCH) as b:
                for q in range(2):
                    act.wait_ge(xt_psum, due(b * 2 + (q + 1)))
                    act.wait_ge(ubc_psum, due(b * 2))
                    act.wait_ge(skip_psum, due(b * 2))
                    act.copy(xn_t[:, q, :], bank(ps, q)).then_inc(xt_ready, 1)
                for q in range(2):
                    col = b * SEQ + q * HALF
                    act.wait_ge(z_psum, b * 2 + (q + 1))
                    act.activation(abs_z[:, q, :], bank(ps, 5), ACT.Abs, bias=b_dt[:, 0:1]).then_inc(abs_done, 1)
                    act.wait_ge(ubc_psum, due(b * 2 + (q + 1)))
                    act.copy(u[:, bass.ds(col, HALF)], bank(ps, 2))
                    act.copy(inp[:, bass.ds(col, HALF)], bank(ps, 3))
                    act.copy(c_rows[:, bass.ds(col, HALF)], bank(ps, 4)).then_inc(ubc_taken, 1)
                for q in range(2):
                    act.wait_ge(abs_done, b * 2 + (q + 1))
                    act.activation(exp_z[:, bass.ds(b * SEQ + q * HALF, HALF)], abs_z[:, q, :], ACT.Exp,
                                   scale=-1.0).then_inc(exp_done, 1)

        @block.vector
        def _(dve):
            prime(dve, z_taken, skip_taken)
            dve.wait_ge(consts_in, 16)
            dve.tensor_copy(m["tri"][:, :], const[:, C_TRI:C_TRI + P]).then_inc(tri_made, 1)
            dve.wait_ge(weights_in, 16 * 5)
            dve.tensor_tensor(w_skip[:, :], w_in[:, :], skip[:, :], ALU.mult).then_inc(skip_made, 1)
            dve.wait_ge(x_in, 16)
            with dve.Fori(0, BATCH) as b:
                for q in range(2):
                    for i in range(HT):
                        last = dve.bn_stats(stats[:, q, i, :], x[:, bass.ds(b * SEQ + (q * HT + i) * D, D)])
                    dve.drain()
                    for i in range(HT):
                        last = dve.bn_aggr(moments[:, q, i, :], stats[:, q, i, :])
                    dve.drain()
                    dve.tensor_scalar(spread[:, q, :], moments[:, q, :, 1], EPS, None, ALU.add).then_inc(moments_done, 1)
                    dve.wait_ge(rstd_done, b * 2 + (q + 1))
                    dve.wait_ge(xt_psum, due(b * 2))
                    for i in range(HT):
                        last = dve.tensor_scalar(xn[:, q, i * D:(i + 1) * D], x[:, bass.ds(b * SEQ + (q * HT + i) * D, D)],
                                                 moments[:, q, i, 0:1], rstd[:, q, i:i + 1], ALU.subtract, ALU.mult)
                    last.then_inc(xn_ready, 1)
                for q in range(2):
                    col = b * SEQ + q * HALF
                    dve.wait_ge(abs_done, b * 2 + (q + 1))
                    dve.tensor_scalar(relu_z[:, bass.ds(col, HALF)], bank(ps, 5), b_dt[:, 0:1], 0.0,
                                      ALU.add, ALU.max).then_inc(z_taken, 1)
                    dve.wait_ge(skip_psum, due(b * 2 + (q + 1)))
                    dve.tensor_tensor(x[:, bass.ds(col, HALF)], x[:, bass.ds(col, HALF)], bank(ps, 6),
                                      ALU.add).then_inc(skip_taken, 1)

        @block.tensor
        def _(pe):
            prime(pe, xt_psum, ubc_psum, skip_psum)
            pe.wait_ge(consts_in, 16)
            pe.wait_ge(weights_in, 16 * 5)
            pe.transpose(ps[:, 0:D], w_in[:, :], ident).then_inc(fold_psum, 1)
            pe.wait_ge(fold_done, 1)
            rep = lambda a: a.rearrange("p (n o) -> p n o", o=1).broadcast_to([P, STATES, GROUP])
            pe.matmul(ps[0:RANK, HALF:HALF + D], w_x[:, 0:RANK], w_in_t[:, :], start=True, stop=True)
            pe.matmul(ps[:, 2 * HALF:2 * HALF + P], w_in_t[:, :], rep(w_x[:, RANK:RANK + STATES]), start=True, stop=True)
            pe.matmul(ps[:, 3 * HALF:3 * HALF + P], w_in_t[:, :], rep(w_x[:, RANK + STATES:]), start=True,
                      stop=True).then_inc(fold_psum, 1)
            pe.wait_ge(fold_done, 2)
            pe.matmul(ps[:, 4 * HALF:4 * HALF + D], w_low[:, :], w_dt[:, :], start=True, stop=True).then_inc(fold_psum, 1)
            pe.wait_ge(fold_done, 3)
            pe.wait_ge(skip_made, 1)
            with pe.Fori(0, BATCH) as b:
                for q in range(2):
                    pe.wait_ge(xn_ready, b * 2 + (q + 1))
                    pe.wait_ge(xt_ready, due(b * 2))
                    for i in range(HT):
                        last = pe.transpose(ps[:, q * HALF + i * P:q * HALF + (i + 1) * P], xn[:, q, i * D:(i + 1) * D], ident)
                    last.then_inc(xt_psum, 1)
                for q in range(2):
                    pe.wait_ge(xt_ready, due(b * 2 + (q + 1)))
                    pe.wait_ge(z_taken, due(b * 2 + q))
                    pe.matmul(bank(ps, 5), w_z[:, :], xn_t[:, q, :], start=True, stop=True).then_inc(z_psum, 1)
                    pe.wait_ge(ubc_taken, due(b * 2 + q))
                    pe.matmul(bank(ps, 2), w_in[:, :], xn_t[:, q, :], start=True, stop=True)
                    pe.matmul(bank(ps, 3), w_b[:, :], xn_t[:, q, :], start=True, stop=True)
                    pe.matmul(bank(ps, 4), w_c[:, :], xn_t[:, q, :], start=True, stop=True).then_inc(ubc_psum, 1)
                    pe.wait_ge(skip_taken, due(b * 2 + q))
                    for i in range(HT):
                        last = pe.matmul(ps[:, 6 * HALF + i * D:6 * HALF + (i + 1) * D], xn_t[:, q, i * P:(i + 1) * P],
                                         w_skip[:, :], start=True, stop=True)
                    last.then_inc(skip_psum, 1)


def step(nc, k, ps, m, t, steps):
    relu_z, exp_z, inp, c_rows, u = m["big"]
    const = m["const"]
    a_neg = k.sb("a_neg", [P, STATES])
    a_rep = k.sb("a_rep", [P, P])
    a_p = k.sb("a_p", [P, GROUPS])
    sel = k.sb("sel", [P, QG * P], BF16)
    part = k.sb("part", [P, PARTS, SEQ], BF16)
    rest = k.sb("rest", [P, SEQ])
    dtu = k.sb("dtu", [P, SEQ])
    stack = k.sb("stack", [PARTS * QUARTER, QUARTER // GROUP, TOKENS], BF16)
    m["a_p"], m["sel"], m["stack"] = a_p, sel, stack
    a_in, a_exp, a_made, a_reped = k.sem("a_in"), k.sem("a_exp"), k.sem("a_made"), k.sem("a_reped")
    ln_done, sp_done, dt_done, hi_done = k.sem("ln_done"), k.sem("sp_done"), k.sem("dt_done"), k.sem("hi_done")
    rest_done, mid_done, lo_done, dtu_done = k.sem("rest_done"), k.sem("mid_done"), k.sem("lo_done"), k.sem("dtu_done")
    q_psum, inp_done, parts_free, steps_out, stacked = k.sem("q_psum"), k.sem("inp_done"), k.sem("parts_free"), k.sem("steps_out"), k.sem("stacked")

    with nc.Block() as block:

        @block.sync
        def _(sp):
            prime(sp, parts_free)
            with sp.Fori(0, BATCH) as b:
                sp.wait_ge(lo_done, due(b + 1))
                standalone(sp, m["passed"])
                sp.dma_start(steps[:, bass.ds(b * (PARTS * SEQ), PARTS * SEQ)],
                             part[:, :, :].rearrange("p a s -> p (a s)")).then_inc(steps_out, 16)
                sp.wait_ge(steps_out, b * 16 + 16)
                sp.sem_inc(parts_free, 1)
                for a in range(PARTS):
                    sp.dma_start(stack[a * QUARTER:(a + 1) * QUARTER, :, bass.ds(b * SEQ, SEQ)],
                                 steps[:, bass.ds(b * (PARTS * SEQ) + a * SEQ, SEQ)].rearrange(
                                     "(q r) s -> r q s", r=QUARTER)).then_inc(stacked, 16)
            sp.wait_ge(stacked, 16 * PARTS * BATCH)

        @block.scalar
        def _(act):
            act.dma_start(a_neg[:, :], t["a_A_log"]).then_inc(a_in, 16)
            act.dma_start(a_p[:, :], t["a_A_log_p"]).then_inc(a_in, 16)
            act.wait_ge(a_in, 32)
            act.activation(a_neg[:, :], a_neg[:, :], ACT.Exp)
            act.activation(a_p[:, :], a_p[:, :], ACT.Exp).then_inc(a_exp, 1)
            with act.Fori(0, BATCH) as b:
                act.activation(exp_z[:, bass.ds(b * SEQ, SEQ)], exp_z[:, bass.ds(b * SEQ, SEQ)], ACT.Ln,
                               bias=1.0).then_inc(ln_done, 1)

        @block.vector
        def _(dve):
            prime(dve, inp_done)
            dve.tensor_copy(sel[:, :], const[:, C_SEL:C_SEL + QG * P])
            dve.wait_ge(a_exp, 1)
            dve.tensor_scalar(a_neg[:, :], a_neg[:, :], -1.0, None, ALU.mult)
            dve.tensor_scalar(a_p[:, :], a_p[:, :], -1.0, None, ALU.mult).then_inc(a_made, 1)
            dve.wait_ge(a_made, 1)
            dve.tensor_copy(a_rep[:, :].rearrange("p (n j) -> p n j", j=GROUP),
                            a_neg[:, :].rearrange("p (n o) -> p n o", o=1).broadcast_to([P, STATES, GROUP])).then_inc(a_reped, 1)
            with dve.Fori(0, BATCH) as b:
                cols = bass.ds(b * SEQ, SEQ)
                dve.wait_ge(ln_done, b + 1)
                dve.tensor_tensor(relu_z[:, cols], relu_z[:, cols], exp_z[:, cols], ALU.add).then_inc(sp_done, 1)
                dve.wait_ge(sp_done, b + 1)
                dve.tensor_scalar(relu_z[:, cols], relu_z[:, cols], DT_MAX - DT_MIN, DT_MIN, ALU.mult, ALU.add).then_inc(dt_done, 1)
                dve.wait_ge(dt_done, b + 1)
                dve.wait_ge(parts_free, due(b))
                standalone(dve, m["passed"])
                dve.tensor_copy(part[:, 0, :], relu_z[:, cols]).then_inc(hi_done, 1)
                dve.wait_ge(rest_done, b + 1)
                dve.tensor_copy(part[:, 1, :], rest[:, :]).then_inc(mid_done, 1)
                dve.wait_ge(q_psum, due(b + 1))
                dve.tensor_tensor(inp[:, cols], inp[:, cols], bank(ps, 0, 2), ALU.mult).then_inc(inp_done, 1)

        @block.gpsimd
        def _(pool):
            prime(pool, lo_done)
            with pool.Fori(0, BATCH) as b:
                cols = bass.ds(b * SEQ, SEQ)
                pool.wait_ge(hi_done, b + 1)
                pool.wait_ge(lo_done, due(b))
                standalone(pool, m["passed"])
                pool.tensor_tensor(rest[:, :], relu_z[:, cols], part[:, 0, :], ALU.subtract).then_inc(rest_done, 1)
                pool.wait_ge(q_psum, due(b))
                standalone(pool, m["passed"])
                pool.tensor_tensor(dtu[:, :], relu_z[:, cols], u[:, cols], ALU.mult).then_inc(dtu_done, 1)
                pool.wait_ge(mid_done, b + 1)
                pool.tensor_tensor(part[:, 2, :], rest[:, :], part[:, 1, :], ALU.subtract).then_inc(lo_done, 1)

        @block.tensor
        def _(pe):
            prime(pe, q_psum)
            pe.wait_ge(a_reped, 1)
            with pe.Fori(0, BATCH) as b:
                pe.wait_ge(dtu_done, b + 1)
                pe.wait_ge(inp_done, due(b))
                for q in range(2):
                    last = pe.matmul(bank(ps, q), a_rep[:, :], dtu[:, q * HALF:(q + 1) * HALF], start=True, stop=True)
                last.then_inc(q_psum, 1)


ON_DVE = (2, 5, 8, 11, 14)
RING = 3
STATE_BUFS = 4


def scan(nc, k, ps, m, t):
    x, const = m["x"], m["const"]
    _, _, inp, c_rows, _ = m["big"]
    a_p, sel, stack = m["a_p"], m["sel"], m["stack"]
    h = k.sb("h", [P, STATE_BUFS, SEQ])
    prod = k.sb("prod", [P, STATE_BUFS, SEQ])
    dt_psum, decay_ready, scanned = k.sem("dt_psum"), k.sem("decay_ready"), k.sem("scanned")
    prod_dve, prod_pool, summed, y_taken = k.sem("prod_dve"), k.sem("prod_pool"), k.sem("summed"), k.sem("y_taken")
    n_dve, n_pool = len(ON_DVE), GROUPS - len(ON_DVE)

    def upto(g, on_dve):
        return sum(1 for j in range(g + 1) if (j in ON_DVE) == on_dve)

    def wait_prod(eng, b, g):
        if g in ON_DVE:
            eng.wait_ge(prod_dve, due(b * n_dve + upto(g, True)))
        else:
            eng.wait_ge(prod_pool, due(b * n_pool + upto(g, False)))

    slot = lambda g: bank(ps, 2 * (g % RING), 2)

    with nc.Block() as block:

        @block.tensor
        def _(pe):
            prime(pe, summed)
            def broadcast(b, g):
                pe.wait_ge(scanned, due(b * GROUPS + (g - RING + 1 if g >= RING else 0)))
                for q in range(2):
                    last = pe.matmul(bank(ps, 2 * (g % RING) + q), sel[0:PARTS * QUARTER, (g % QG) * P:(g % QG + 1) * P],
                                     stack[:, g // QG, bass.ds(b * SEQ + q * HALF, HALF)], start=True, stop=True)
                last.then_inc(dt_psum, 1)

            def reduce(b, g):
                wait_prod(pe, b, g)
                for i in range(BT):
                    last = pe.matmul(ps[:, 6 * HALF + i * D + g * GROUP:6 * HALF + i * D + (g + 1) * GROUP],
                                     prod[:, g % STATE_BUFS, i * P:(i + 1) * P], const[:, C_RED:C_RED + GROUP],
                                     start=True, stop=True)
                last.then_inc(summed, 1)

            with pe.Fori(0, BATCH) as b:
                for g in range(RING):
                    broadcast(b, g)
                pe.wait_ge(y_taken, due(b))
                for g in range(GROUPS):
                    if g + RING < GROUPS:
                        broadcast(b, g + RING)
                    if g >= 2:
                        reduce(b, g - 2)
                for g in range(GROUPS - 2, GROUPS):
                    reduce(b, g)

        @block.scalar
        def _(act):
            with act.Fori(0, BATCH) as b:
                for g in range(GROUPS):
                    act.wait_ge(dt_psum, b * GROUPS + (g + 1))
                    act.activation(slot(g), slot(g), ACT.Exp, scale=a_p[:, g:g + 1]).then_inc(decay_ready, 1)

        @block.vector
        def _(dve):
            prime(dve, scanned, prod_dve, y_taken)
            def multiply(b, g):
                dve.wait_ge(scanned, due(b * GROUPS + (g + 1)))
                dve.wait_ge(summed, due(b * GROUPS + (g - STATE_BUFS + 1 if g >= STATE_BUFS else 0)))
                dve.tensor_tensor(prod[:, g % STATE_BUFS, :], h[:, g % STATE_BUFS, :], c_rows[:, bass.ds(b * SEQ, SEQ)],
                                  ALU.mult).then_inc(prod_dve, 1)

            with dve.Fori(0, BATCH) as b:
                for g in range(GROUPS):
                    dve.wait_ge(decay_ready, b * GROUPS + (g + 1))
                    if g >= STATE_BUFS:
                        wait_prod(dve, b, g - STATE_BUFS)
                    elif g == 0:
                        dve.wait_ge(prod_pool, due(b * n_pool))
                        dve.wait_ge(prod_dve, due(b * n_dve))
                    dve.tensor_tensor_scan(h[:, g % STATE_BUFS, :], slot(g), inp[:, bass.ds(b * SEQ, SEQ)], 0.0,
                                           ALU.mult, ALU.add).then_inc(scanned, 1)
                    if g - 1 in ON_DVE:
                        multiply(b, g - 1)
                if GROUPS - 1 in ON_DVE:
                    multiply(b, GROUPS - 1)
                dve.wait_ge(summed, due(b * GROUPS + GROUPS))
                dve.tensor_tensor(x[:, bass.ds(b * SEQ, SEQ)], x[:, bass.ds(b * SEQ, SEQ)], bank(ps, 6, 2),
                                  ALU.add).then_inc(y_taken, 1)

        @block.gpsimd
        def _(pool):
            prime(pool, prod_pool)
            with pool.Fori(0, BATCH) as b:
                for g in range(GROUPS):
                    if g not in ON_DVE:
                        pool.wait_ge(scanned, due(b * GROUPS + (g + 1)))
                        pool.wait_ge(summed, due(b * GROUPS + (g - STATE_BUFS + 1 if g >= STATE_BUFS else 0)))
                        standalone(pool, m["passed"])
                        pool.tensor_tensor(prod[:, g % STATE_BUFS, :], h[:, g % STATE_BUFS, :],
                                           c_rows[:, bass.ds(b * SEQ, SEQ)], ALU.mult).then_inc(prod_pool, 1)


def experts(nc, k, ps, m, t, slots, answers, zeroed, tag, out):
    x, const = m["x"], m["const"]
    ident = const[:, C_ID:C_ID + P]
    xn_all = m["big"][0]
    gated = [m["big"][1][:, 0:SEQ], m["big"][1][:, SEQ:2 * SEQ]]
    back = [m["big"][1][:, 2 * SEQ:3 * SEQ], m["big"][1][:, 3 * SEQ:4 * SEQ]]
    xt = [m["big"][2][:, 0:SEQ], m["big"][2][:, SEQ:2 * SEQ]]
    rows = [m["big"][3][:, q * HALF:(q + 1) * HALF] for q in range(2)]
    rows_t = [m["big"][3][:, (2 + q) * HALF:(3 + q) * HALF] for q in range(2)]
    hidden = [m["big"][3][:, (4 + q) * HALF:(5 + q) * HALF] for q in range(2)]
    reply = [m["big"][3][:, (6 + q) * HALF:(7 + q) * HALF] for q in range(2)]
    sb, sem = lambda n, s, d=F32: k.sb(n + tag, s, d), lambda n: k.sem(n + tag)
    if tag == "f":
        for n, s, d in (("w_r", [P, EXPERTS], F32), ("b_r", [P, EXPERTS], F32), ("b1", [P, EXPERTS], F32),
                        ("b2", [P, EXPERTS * D], F32), ("w1", [P, 2, D], F32), ("w2", [P, 2, D], F32),
                        ("onehot", [P, TILES, EXPERTS], BF16), ("logit", [P, BT, EXPERTS], F32),
                        ("top", [P, BT], F32), ("eq", [P, BT, EXPERTS], F32), ("dif", [P, BT, EXPERTS], F32),
                        ("prob", [P, BT, EXPERTS], F32), ("total", [P, BT], F32), ("gate", [P, BT], F32),
                        ("first", [P, BT], F32), ("base", [P, BT], F32), ("cum", [P, BT, EXPERTS], F32),
                        ("pos", [P, BT], F32), ("kept", [P, BT], F32), ("row", [P, BT], F32),
                        ("away", [P, BT], F32), ("trash", [P, BT], F32), ("weight", [P, TILES], F32),
                        ("prior", [P, EXPERTS], F32), ("prior_b", [P, EXPERTS], BF16), ("sum8", [P, EXPERTS], F32),
                        ("put", [P, 2, BT], I32), ("get", [P, TILES], I32),
                        ("est", [P, BT, 6], F32), ("emo", [P, BT, 2], F32), ("ers", [P, BT], F32), ("spread", [P, BT], F32)):
            m[n] = k.sb("e_" + n, s, d)
    g = lambda n: m[n]
    w_in = sem("router_in")
    s_st, s_mo, s_rs, s_xn, s_xtp, s_xt, s_lgp = (sem(n) for n in ("stats", "moments", "rstd", "xn", "xt_psum", "xt", "logit_psum"))
    link, exp_done, hot, cum_psum = sem("link"), sem("exp"), sem("hot"), sem("cum_psum")
    put_ready, put_done, w_loaded = sem("put_ready"), [sem("put0"), sem("put1")], [sem("loaded0"), sem("loaded1")]
    put_issued = sem("diff")
    put_free, store_free = sem("put_free"), sem("store_free")
    r_tp, r_t, h_psum, h_done, y_psum, y_done = (sem(n) for n in (
        "rows_psum", "rows_t", "hidden_psum", "hidden", "reply_psum", "reply"))
    stored = [sem("stored0"), sem("stored1")]
    got, added = [sem("got0"), sem("got1")], sem("added")
    out_done = sem("out_done")

    with nc.Block() as block:

        @block.sync
        def _(sp):
            prime(sp, put_free)
            if tag == "f":
                sp.dma_start(g("w_r")[:, :], t["f_Wr"]).then_inc(w_in, 16)
                sp.dma_start(g("b_r")[:, :], t["f_br"].rearrange("(o e) -> o e", o=1).broadcast_to([P, EXPERTS])).then_inc(w_in, 16)
                sp.dma_start(g("b1")[:, :], t["f_b1_t"]).then_inc(w_in, 16)
                sp.dma_start(g("b2")[:, :], t["f_b2"].rearrange("(o e) d -> o (e d)", o=1).broadcast_to([P, EXPERTS * D])).then_inc(w_in, 16)
            with sp.Fori(0, BATCH // 2) as bb:
                for q in range(2):
                    sp.wait_ge(put_done[q], bb * (16 * BT) + 16 * BT)
                    sp.sem_inc(put_free, 1)
            with sp.Fori(0, EXPERTS // 2) as ee:
                for q in range(2):
                    e = ee * 2 + q
                    sp.wait_ge(r_tp, due(ee * 2))
                    sp.wait_ge(y_psum, due(ee * 2))
                    sp.dma_start(rows[q], slots[bass.ds(e * CAP, CAP), :].rearrange("(p j) d -> p (j d)", p=P)).then_inc(w_loaded[q], 16)
                    sp.dma_start(g("w1")[:, q, :], t["f_W1"][bass.ds(e, 1), :, :].rearrange("o d f -> (o d) f")).then_inc(w_loaded[q], 16)
                    sp.dma_start(g("w2")[:, q, :], t["f_W2"][bass.ds(e, 1), :, :].rearrange("o d f -> (o d) f")).then_inc(w_loaded[q], 16)
            if out is not None:
                for b in range(BATCH):
                    sp.wait_ge(added, b + 1)
                    sp.dma_start(out[b:b + 1, :, :].rearrange("b (i p) d -> p (b i) d", p=P),
                                 x[:, b * SEQ:(b + 1) * SEQ].rearrange("p (i d) -> p i d", d=D)).then_inc(out_done, 16)
                sp.wait_ge(out_done, 16 * BATCH)

        @block.tensor
        def _(pe):
            prime(pe, s_lgp, y_psum, r_tp, h_psum)
            if tag == "f":
                pe.wait_ge(w_in, 64)
            with pe.Fori(0, BATCH // 2) as bb:
                for q in range(2):
                    b = bb * 2 + q
                    for i in range(BT):
                        if i == 0:
                            pe.wait_ge(s_xt, due(bb * 2))
                        pe.wait_ge(s_xn, b * BT + (i + 1))
                        last = pe.transpose(ps[:, 2 * q * HALF + i * P:2 * q * HALF + (i + 1) * P],
                                            gated[q][:, i * D:(i + 1) * D], ident)
                    last.then_inc(s_xtp, 1)
                    pe.wait_ge(s_xt, due(b + 1))
                    pe.wait_ge(link, due(b))
                    for i in range(BT):
                        last = pe.matmul(ps[:, 4 * HALF + i * EXPERTS:4 * HALF + (i + 1) * EXPERTS],
                                         xt[q][:, i * P:(i + 1) * P], g("w_r")[:, :], start=True, stop=True)
                    last.then_inc(s_lgp, 1)
                    pe.wait_ge(hot, b + 1)
                    counts = ps[:, 5 * HALF:5 * HALF + BT * EXPERTS]
                    pe.matmul(counts, m["tri"][:, :], g("onehot")[:, bass.ds(b * BT, BT), :].rearrange("p i e -> p (i e)"), start=True, stop=False)
                    for i in range(BT - 1):
                        last = pe.matmul(ps[:, 5 * HALF + (i + 1) * EXPERTS:5 * HALF + BT * EXPERTS], m["ones"][:, :],
                                         g("onehot")[:, bass.ds(b * BT + i, 1), :].broadcast_to([P, BT - 1 - i, EXPERTS]),
                                         start=False, stop=False)
                    pe.matmul(counts, m["ones"][:, :], g("prior_b")[:, :].rearrange("p (o e) -> p o e", o=1).broadcast_to([P, BT, EXPERTS]),
                              start=False, stop=True).then_inc(cum_psum, 1)
            with pe.Fori(0, EXPERTS // 2) as ee:
                for q in range(2):
                    pe.wait_ge(w_loaded[q], ee * 48 + 48)
                    pe.wait_ge(r_t, due(ee * 2 + q))
                    for j in range(HT):
                        last = pe.transpose(ps[:, 6 * HALF + j * P:6 * HALF + (j + 1) * P], rows[q][:, j * D:(j + 1) * D], ident)
                    last.then_inc(r_tp, 1)
                    pe.wait_ge(r_t, due(ee * 2 + (q + 1)))
                    pe.matmul(bank(ps, 0 + q), g("w1")[:, q, :], rows_t[q], start=True, stop=True).then_inc(h_psum, 1)
                    pe.wait_ge(h_done, ee * 2 + (q + 1))
                    pe.wait_ge(y_done, due(ee * 2))
                    for j in range(HT):
                        last = pe.matmul(ps[:, (2 + q) * HALF + j * D:(2 + q) * HALF + (j + 1) * D], hidden[q][:, j * P:(j + 1) * P],
                                         g("w2")[:, q, :], start=True, stop=True)
                    last.then_inc(y_psum, 1)

        @block.scalar
        def _(act):
            prime(act, s_xt, r_t)
            with act.Fori(0, BATCH // 2) as bb:
                for q in range(2):
                    b = bb * 2 + q
                    act.wait_ge(s_xtp, b + 1)
                    act.wait_ge(s_lgp, due(bb * 2))
                    act.copy(xt[q], bank(ps, 2 * q, 2)).then_inc(s_xt, 1)
                    act.wait_ge(put_issued, b + 1)
                    act.activation(g("prob")[:, :, :], g("dif")[:, :, :], ACT.Exp).then_inc(exp_done, 1)
            with act.Fori(0, EXPERTS // 2) as ee:
                for q in range(2):
                    e = ee * 2 + q
                    act.wait_ge(r_tp, due(e + 1))
                    act.wait_ge(h_psum, due(ee * 2))
                    act.copy(rows_t[q], bank(ps, 6)).then_inc(r_t, 1)
                    act.wait_ge(h_psum, due(e + 1))
                    act.wait_ge(y_psum, due(ee * 2))
                    act.activation(hidden[q], bank(ps, 0 + q), ACT.Relu, bias=g("b1")[:, bass.ds(e, 1)]).then_inc(h_done, 1)
                    act.wait_ge(y_done, due(e + 1))
                    act.dma_start(answers[bass.ds(e * CAP, CAP), :].rearrange("(p j) d -> p (j d)", p=P), reply[q]).then_inc(stored[q], 16)

        @block.vector
        def _(dve):
            prime(dve, link, y_done)
            cleared = sem("cleared")
            dve.memset(g("prior")[:, :], 0.0)
            dve.memset(g("prior_b")[:, :], 0.0).then_inc(cleared, 1)
            if tag == "f":
                dve.wait_ge(w_in, 64)
            with dve.Fori(0, BATCH // 2) as bb:
                for q in range(2):
                    b = bb * 2 + q
                    def chained(ins):
                        dve.drain()

                    for i in range(BT):
                        last = dve.bn_stats(g("est")[:, i, :], x[:, bass.ds(b * SEQ + i * D, D)])
                    dve.drain()
                    for i in range(BT):
                        last = dve.bn_aggr(g("emo")[:, i, :], g("est")[:, i, :])
                    dve.drain()
                    dve.tensor_scalar(g("spread")[:, :], g("emo")[:, :, 1], EPS, None, ALU.add).then_inc(s_mo, 1)
                    dve.wait_ge(s_rs, b + 1)
                    dve.wait_ge(put_free, due(bb * 2))
                    for i in range(BT):
                        dve.tensor_scalar(gated[q][:, i * D:(i + 1) * D], x[:, bass.ds(b * SEQ + i * D, D)],
                                          g("emo")[:, i, 0:1], g("ers")[:, i:i + 1], ALU.subtract, ALU.mult).then_inc(s_xn, 1)
                    dve.wait_ge(s_lgp, due(b + 1))
                    lg = ps[:, 4 * HALF:4 * HALF + BT * EXPERTS].rearrange("p (i e) -> p i e", e=EXPERTS)
                    bc = lambda a: a.rearrange("p (i o) -> p i o", o=1).broadcast_to([P, BT, EXPERTS])
                    rank = const[:, C_RANK:C_RANK + EXPERTS].rearrange("p (o e) -> p o e", o=1).broadcast_to([P, BT, EXPERTS])
                    chained(dve.tensor_tensor(g("logit")[:, :, :], lg, g("b_r")[:, :].rearrange("p (o e) -> p o e", o=1).broadcast_to([P, BT, EXPERTS]), ALU.add).then_inc(link, 1))
                    chained(dve.tensor_reduce(g("top")[:, :], g("logit")[:, :, :], AX, ALU.max))
                    dve.tensor_tensor(g("dif")[:, :, :], g("logit")[:, :, :], bc(g("top")[:, :]), ALU.subtract).then_inc(put_issued, 1)
                    chained(dve.tensor_tensor(g("eq")[:, :, :], g("logit")[:, :, :], bc(g("top")[:, :]), ALU.is_equal))
                    chained(dve.tensor_tensor(g("eq")[:, :, :], g("eq")[:, :, :], rank, ALU.mult))
                    chained(dve.tensor_reduce(g("first")[:, :], g("eq")[:, :, :], AX, ALU.max))
                    dve.tensor_tensor(g("eq")[:, :, :], bc(g("first")[:, :]), rank, ALU.is_equal)
                    dve.tensor_tensor(g("onehot")[:, bass.ds(b * BT, BT), :], bc(g("first")[:, :]), rank, ALU.is_equal).then_inc(hot, 1)
                    dve.wait_ge(exp_done, b + 1)
                    chained(dve.tensor_reduce(g("total")[:, :], g("prob")[:, :, :], AX, ALU.add))
                    dve.tensor_scalar(g("base")[:, :], g("first")[:, :], -float(CAP), float(CAP * EXPERTS), ALU.mult, ALU.add)
                    chained(dve.reciprocal(g("gate")[:, :], g("total")[:, :]))
                    dve.tensor_tensor(g("trash")[:, :], const[:, bass.ds(b * BT + C_TOKEN, BT)], g("base")[:, :], ALU.subtract)
                    dve.wait_ge(cum_psum, b + 1)
                    chained(dve.tensor_tensor(g("cum")[:, :, :], ps[:, 5 * HALF:5 * HALF + BT * EXPERTS].rearrange("p (i e) -> p i e", e=EXPERTS),
                                              g("eq")[:, :, :], ALU.mult))
                    dve.tensor_reduce(g("sum8")[:, :], g("eq")[:, :, :].rearrange("p i e -> p e i"), AX, ALU.add)
                    chained(dve.tensor_reduce(g("pos")[:, :], g("cum")[:, :, :], AX, ALU.add))
                    dve.tensor_tensor(g("prior")[:, :], g("prior")[:, :], g("sum8")[:, :], ALU.add)
                    chained(dve.tensor_scalar(g("kept")[:, :], g("pos")[:, :], float(CAP), None, ALU.is_lt))
                    dve.tensor_copy(g("prior_b")[:, :], g("prior")[:, :])
                    dve.tensor_scalar(g("away")[:, :], g("kept")[:, :], -1.0, 1.0, ALU.mult, ALU.add)
                    dve.tensor_tensor(g("weight")[:, bass.ds(b * BT, BT)], g("kept")[:, :], g("gate")[:, :], ALU.mult)
                    chained(dve.tensor_tensor(g("row")[:, :], g("pos")[:, :], g("kept")[:, :], ALU.mult))
                    dve.tensor_tensor(g("trash")[:, :], g("trash")[:, :], g("away")[:, :], ALU.mult)
                    chained(dve.tensor_tensor(g("row")[:, :], g("row")[:, :], g("base")[:, :], ALU.add))
                    dve.tensor_copy(g("get")[:, bass.ds(b * BT, BT)], g("row")[:, :])
                    dve.tensor_tensor(g("put")[:, q, :], g("row")[:, :], g("trash")[:, :], ALU.add)
                    dve.tensor_tensor(gated[q].rearrange("p (i d) -> p i d", d=D), gated[q].rearrange("p (i d) -> p i d", d=D),
                                      g("gate")[:, :].rearrange("p (i o) -> p i o", o=1).broadcast_to([P, BT, D]), ALU.mult).then_inc(put_ready, 1)
            with dve.Fori(0, EXPERTS // 2) as ee:
                for q in range(2):
                    e = ee * 2 + q
                    dve.wait_ge(y_psum, due(e + 1))
                    dve.wait_ge(store_free, due(ee * 2))
                    dve.tensor_tensor(reply[q].rearrange("p (j d) -> p j d", d=D), bank(ps, 2 + q).rearrange("p (j d) -> p j d", d=D),
                                      g("b2")[:, bass.ds(e * D, D)].rearrange("p (o d) -> p o d", o=1).broadcast_to([P, HT, D]),
                                      ALU.add).then_inc(y_done, 1)
            with dve.Fori(0, BATCH // 2) as bb:
                for q in range(2):
                    b = bb * 2 + q
                    dve.wait_ge(got[q], bb * (16 * BT) + 16 * BT)
                    for i in range(BT):
                        last = dve.scalar_tensor_tensor(out=x[:, bass.ds(b * SEQ + i * D, D)], in0=back[q][:, i * D:(i + 1) * D],
                                                        scalar=g("weight")[:, bass.ds(b * BT + i, 1)], in1=x[:, bass.ds(b * SEQ + i * D, D)],
                                                        op0=ALU.mult, op1=ALU.add)
                    last.then_inc(added, 1)

        @block.gpsimd
        def _(pool):
            prime(pool, store_free)
            with pool.Fori(0, BATCH // 2) as bb:
                for q in range(2):
                    pool.wait_ge(s_mo, bb * 2 + (q + 1))
                    pool.tensor_tensor(g("ers")[:, :], g("spread")[:, :], m["neg_half"][:, :], ALU.pow).then_inc(s_rs, 1)
                    pool.wait_ge(put_ready, bb * 2 + (q + 1))
                    pool.wait_ge(zeroed, 16 * 5)
                    standalone(pool, m["passed"])
                    for i in range(BT):
                        pool.indirect_dma_start(out=slots, out_offset=bass.IndirectOffsetOnAxis(g("put")[:, q, i:i + 1], 0),
                                                in_=gated[q][:, i * D:(i + 1) * D], in_offset=None).then_inc(put_done[q], 16)
            with pool.Fori(0, EXPERTS // 2) as ee:
                for q in range(2):
                    pool.wait_ge(stored[q], ee * 16 + 16)
                    pool.sem_inc(store_free, 1)
            for b in range(BATCH):
                if b >= 2:
                    pool.wait_ge(added, b - 1)
                for i in range(BT):
                    pool.indirect_dma_start(out=back[b % 2][:, i * D:(i + 1) * D], out_offset=None, in_=answers,
                                            in_offset=bass.IndirectOffsetOnAxis(g("get")[:, b * BT + i:b * BT + i + 1], 0)).then_inc(got[b % 2], 16)


def conv(nc, k, ps, m, t, taps):
    x, const = m["x"], m["const"]
    ident = const[:, C_ID:C_ID + P]
    PAD = TAPS - 1
    w_in = k.sb("cw_in", [P, 2, D])
    b_in = k.sb("cb_in", [P, 3])
    w_tap = k.sb("cw_tap", [P, 2, TAPS])
    b_tap = k.sb("cb_tap", [P, 3])
    w1, w2, w3 = k.sb("cw1", [TAPS, FW]), k.sb("cw2", [FW, FW]), k.sb("cw3", [FW, D])
    b1, b2 = k.sb("cb1", [FW, 1]), k.sb("cb2", [FW, 1])
    time0 = k.sb("time0", [TAPS, 1])
    col = k.sb("col", [FW, 8])
    row = k.sb("rowh", [1, 3, D])
    fb = k.sb("fb", [P, 1])
    ones_row = k.sb("ones_row", [1, P])
    w_out, b_out = m["w_out"], m["b_out"]
    flipped = k.sb("flipped", [P, 2 * P])
    toep = k.sb("toep", [P, 2 * P])
    flat = lambda i, n: m["big"][i][:, 0:n]
    xn, xt = m["big"][0][:, 0:SEQ], m["big"][0][:, SEQ:2 * SEQ]
    ub = k.sb("ub", [P, 2, PAD + SEQ])
    s0, s2 = m["big"][1][:, 0:SEQ], m["big"][1][:, SEQ:2 * SEQ]
    v, vt = m["big"][2][:, 0:SEQ], m["big"][2][:, SEQ:2 * SEQ]
    z = m["big"][3][:, 0:SEQ]
    mm = {n: k.sem("c_" + n) for n in (
        "w", "pre", "abs", "filt_psum", "filt", "taps_out", "taps_in", "flip_psum", "toep", "stats", "moments", "rstd", "xn",
        "xt_psum", "xt", "u_psum", "u", "tap0", "tap1", "s", "v", "vt_psum", "vt", "y_psum", "yb", "z", "o_psum", "o")}

    with nc.Block() as block:

        @block.sync
        def _(sp):
            ci = t["b_w_in"].rearrange("d (s e) -> d s e", s=3)
            n = 0
            for dst, src in ((w_in[:, :, :], ci[:, 0:3:2, :]), (b_in[:, :], t["b_b_in_t"]),
                             (w_tap[:, :, :], t["b_w_conv"].rearrange("(s e) o j -> e s (o j)", s=3)[:, 0:3:2, :]),
                             (b_tap[:, :], t["b_b_conv_t"]),
                             (w1[:, :], t["b_w1"]), (w2[:, :], t["b_w2"]), (w3[:, :], t["b_w3"]),
                             (b1[:, :], t["b_b1"].rearrange("(f o) -> f o", o=1)), (b2[:, :], t["b_b2"].rearrange("(f o) -> f o", o=1)),
                             (fb[:, :], t["b_filt_bias"].rearrange("(f o) -> f o", o=1)),
                             (row[:, 0, :], t["b_filt_bias"].rearrange("(o f) -> o f", o=1)),
                             (w_out[:, :], t["b_w_out"]), (b_out[:, :], t["b_b_out"].rearrange("(o f) -> o f", o=1))):
                sp.dma_start(dst, src).then_inc(mm["w"], 16)
                n += 1
            assert n == 13
            sp.wait_ge(mm["filt"], 5)
            sp.dma_start(taps[:, P - 1:2 * P - 1], row[:, 2, :]).then_inc(mm["taps_out"], 16)
            sp.wait_ge(mm["taps_out"], 16)
            shifted = bass.AP(tensor=taps.tensor, offset=taps.offset, ap=[[1, P], [1, 2 * P]])
            sp.dma_start(flipped[:, :], shifted).then_inc(mm["taps_in"], 16)

        @block.gpsimd
        def _(pool):
            pool.memset(time0[:, :], 0.0)
            pool.memset(ones_row[:, :], 1.0)
            pool.memset(ub[:, :, 0:PAD], 0.0).then_inc(mm["pre"], 1)
            with pool.Fori(0, BATCH) as b:
                pool.wait_ge(mm["moments"], b + 1)
                pool.tensor_tensor(m["ers"][:, :], m["spread"][:, :], m["neg_half"][:, :], ALU.pow).then_inc(mm["rstd"], 1)
                pool.wait_ge(mm["s"], due(b + 1))
                pool.wait_ge(mm["yb"], due(b))
                pool.tensor_tensor(v, s2, s0, ALU.mult).then_inc(mm["v"], 1)

        @block.tensor
        def _(pe):
            pe.wait_ge(mm["w"], 16 * 13)
            pe.wait_ge(mm["pre"], 1)
            pe.matmul(ps[0:FW, 0:1], w1[:, :], time0[:, :], start=True, stop=True).then_inc(mm["filt_psum"], 1)
            pe.wait_ge(mm["filt"], 2)
            pe.matmul(ps[0:FW, HALF:HALF + 1], w2[:, :], col[:, 3:4], start=True, stop=True).then_inc(mm["filt_psum"], 1)
            pe.wait_ge(mm["filt"], 4)
            pe.matmul(ps[0:1, 2 * HALF:2 * HALF + D], col[:, 7:8], w3[:, :], start=True, stop=True).then_inc(mm["filt_psum"], 1)
            pe.wait_ge(mm["taps_in"], 16)
            pe.matmul(ps[:, 3 * HALF:3 * HALF + 2 * P], const[:, C_FLIP:C_FLIP + P], flipped[:, :], start=True,
                      stop=True).then_inc(mm["flip_psum"], 1)
            pe.wait_ge(mm["toep"], 1)
            with pe.Fori(0, BATCH) as b:
                pe.wait_ge(mm["xn"], b + 1)
                pe.wait_ge(mm["vt"], due(b))
                for i in range(BT):
                    last = pe.transpose(ps[:, i * P:(i + 1) * P], xn[:, i * D:(i + 1) * D], ident)
                last.then_inc(mm["xt_psum"], 1)
                pe.wait_ge(mm["xt"], b + 1)
                pe.wait_ge(mm["o"], due(b))
                for s in range(2):
                    for q in range(2):
                        last = pe.matmul(bank(ps, 2 + 2 * s + q), w_in[:, s, :], xt[:, q * HALF:(q + 1) * HALF], start=True, stop=True)
                last.then_inc(mm["u_psum"], 1)
                pe.wait_ge(mm["v"], b + 1)
                for i in range(BT):
                    last = pe.transpose(ps[:, i * P:(i + 1) * P], v[:, i * P:(i + 1) * P], ident)
                last.then_inc(mm["vt_psum"], 1)
                pe.wait_ge(mm["vt"], due(b + 1))
                for i in range(BT):
                    for j in (i - 1, i):
                        if j >= 0:
                            last = pe.matmul(ps[:, 6 * HALF + i * P:6 * HALF + (i + 1) * P], vt[:, j * D:(j + 1) * D],
                                             toep[:, (i - j) * P:(i - j + 1) * P],
                                             start=i % HT == 0 and j == max(i - 1, 0), stop=i % HT == HT - 1 and j == i)
                last.then_inc(mm["y_psum"], 1)
                pe.wait_ge(mm["z"], due(b + 1))
                for q in range(2):
                    pe.matmul(bank(ps, 2 + q), ones_row[:, :], b_out[:, :].rearrange("p (o d) -> p o d", o=1).broadcast_to([1, HT, D]),
                              start=True, stop=False)
                for i in range(BT):
                    last = pe.matmul(ps[:, 2 * HALF + i * D:2 * HALF + (i + 1) * D], z[:, i * P:(i + 1) * P], w_out[:, :],
                                     start=False, stop=i % HT == HT - 1)
                last.then_inc(mm["o_psum"], 1)

        @block.scalar
        def _(act):
            prime(act, mm["vt"])
            act.wait_ge(mm["w"], 16 * 13)
            for layer in range(2):
                act.wait_ge(mm["filt"], 2 * layer + 1)
                act.activation(col[:, 4 * layer + 1:4 * layer + 2], col[:, 4 * layer:4 * layer + 1], ACT.Exp, scale=-1.0).then_inc(mm["tap0"], 1)
            act.activation(row[:, 1, :], row[:, 0, :], ACT.Abs).then_inc(mm["abs"], 1)
            act.wait_ge(mm["abs"], 1)
            act.activation(row[:, 1, :], row[:, 1, :], ACT.Exp, scale=-0.0).then_inc(mm["tap0"], 1)
            act.wait_ge(mm["flip_psum"], 1)
            act.copy(toep[:, :], ps[:, 3 * HALF:3 * HALF + 2 * P]).then_inc(mm["toep"], 1)
            with act.Fori(0, BATCH) as b:
                act.wait_ge(mm["xt_psum"], b + 1)
                act.copy(xt, bank(ps, 0, 2)).then_inc(mm["xt"], 1)
                act.wait_ge(mm["u_psum"], b + 1)
                act.wait_ge(mm["s"], due(b))
                for s in range(2):
                    last = act.activation(ub[:, s, PAD:], bank(ps, 2 + 2 * s, 2), ACT.Identity, bias=b_in[:, 2 * s:2 * s + 1])
                last.then_inc(mm["u"], 1)
                act.wait_ge(mm["u"], b + 1)
                act.wait_ge(mm["z"], due(b))
                act.activation(s0, ub[:, 0, 0:SEQ], ACT.Identity, scale=w_tap[:, 0, 0:1], bias=b_tap[:, 0:1])
                act.activation(s2, ub[:, 1, 0:SEQ], ACT.Identity, scale=w_tap[:, 1, 0:1], bias=b_tap[:, 2:3]).then_inc(mm["tap1"], 1)
                act.wait_ge(mm["vt_psum"], b + 1)
                act.copy(vt, bank(ps, 0, 2)).then_inc(mm["vt"], 1)

        @block.vector
        def _(dve):
            prime(dve, mm["o"], mm["yb"], mm["s"], mm["z"])
            dve.wait_ge(mm["w"], 16 * 13)
            link = k.sem("c_link")
            for layer, bias in ((0, b1), (1, b2)):
                c0 = 4 * layer
                dve.wait_ge(mm["filt_psum"], layer + 1)
                dve.tensor_tensor(col[:, c0:c0 + 1], ps[0:FW, layer * HALF:layer * HALF + 1], bias[:, :], ALU.add).then_inc(mm["filt"], 1)
                dve.wait_ge(mm["tap0"], layer + 1)
                dve.tensor_scalar(col[:, c0 + 1:c0 + 2], col[:, c0 + 1:c0 + 2], 1.0, None, ALU.add).then_inc(link, 1)
                dve.wait_ge(link, 2 * layer + 1)
                dve.reciprocal(col[:, c0 + 2:c0 + 3], col[:, c0 + 1:c0 + 2]).then_inc(link, 1)
                dve.wait_ge(link, 2 * layer + 2)
                dve.tensor_tensor(col[:, c0 + 3:c0 + 4], col[:, c0:c0 + 1], col[:, c0 + 2:c0 + 3], ALU.mult).then_inc(mm["filt"], 1)
            dve.wait_ge(mm["tap0"], 3)
            dve.wait_ge(mm["filt_psum"], 3)
            dve.tensor_tensor(row[:, 2, :], ps[0:1, 2 * HALF:2 * HALF + D], row[:, 1, :], ALU.mult).then_inc(mm["filt"], 1)
            with dve.Fori(0, BATCH) as b:
                for i in range(BT):
                    last = dve.bn_stats(m["est"][:, i, :], x[:, bass.ds(b * SEQ + i * D, D)])
                dve.drain()
                for i in range(BT):
                    last = dve.bn_aggr(m["emo"][:, i, :], m["est"][:, i, :])
                dve.drain()
                dve.tensor_scalar(m["spread"][:, :], m["emo"][:, :, 1], EPS, None, ALU.add).then_inc(mm["moments"], 1)
                dve.wait_ge(mm["rstd"], b + 1)
                for i in range(BT):
                    last = dve.tensor_scalar(xn[:, i * D:(i + 1) * D], x[:, bass.ds(b * SEQ + i * D, D)],
                                             m["emo"][:, i, 0:1], m["ers"][:, i:i + 1], ALU.subtract, ALU.mult)
                last.then_inc(mm["xn"], 1)
                dve.wait_ge(mm["tap1"], b + 1)
                for j in (1, 2):
                    for s, dst in enumerate((s0, s2)):
                        last = dve.scalar_tensor_tensor(out=dst, in0=ub[:, s, j:j + SEQ], scalar=w_tap[:, s, j:j + 1], in1=dst,
                                                        op0=ALU.mult, op1=ALU.add)
                    last.then_inc(link if j == 1 else mm["s"], 1)
                    if j == 1:
                        dve.wait_ge(link, b + 5)
                dve.wait_ge(mm["y_psum"], b + 1)
                dve.scalar_tensor_tensor(out=z, in0=v, scalar=fb[:, 0:1], in1=bank(ps, 6, 2), op0=ALU.mult, op1=ALU.add).then_inc(mm["yb"], 1)
                dve.wait_ge(mm["yb"], due(b + 1))
                dve.tensor_tensor(z, z, s0, ALU.mult).then_inc(mm["z"], 1)
                dve.wait_ge(mm["o_psum"], b + 1)
                dve.tensor_tensor(x[:, bass.ds(b * SEQ, SEQ)], x[:, bass.ds(b * SEQ, SEQ)], bank(ps, 2, 2), ALU.add).then_inc(mm["o"], 1)


def kernel(**inputs):
    import concourse.bacc as bacc
    from concourse.bass_utils import run_bass_kernel_spmd as run

    nc = bacc.Bacc("TRN2", target_bir_lowering=False, num_devices=1)
    a = {n.removeprefix("L0_").replace("attn_a_", "a_").replace("attn_b_", "b_").replace("ffn_", "f_"): np.asarray(v)
         for n, v in inputs.items()}
    a["x"] = a.pop("a_x")
    a["a_A_log_p"] = a["a_A_log"].reshape(GROUPS, GROUP, STATES).transpose(2, 1, 0).reshape(P, GROUPS)
    a["f_b1_t"] = a.pop("f_b1").T
    a["b_b_in_t"] = a.pop("b_b_in").reshape(3, D).T
    a["b_b_conv_t"] = a.pop("b_b_conv").reshape(3, D).T
    a["table"] = constant_table()
    arrays, t = {}, {}
    for n, v in a.items():
        v = np.ascontiguousarray(v)
        arrays["in_" + n] = v
        t[n] = nc.dram_tensor("in_" + n, v.shape, mybir.dt.from_np(v.dtype), kind="ExternalInput").ap()
    t["out"] = nc.dram_tensor("out", (BATCH, SEQ, D), F32, kind="ExternalOutput").ap()
    build(nc, t)
    return run(nc, [arrays], core_ids=[0]).results[0]["out"]
```

```python
from contextlib import ExitStack

import numpy as np

import concourse.bass as bass
from concourse import mybir

F32 = mybir.dt.float32
BF16 = mybir.dt.bfloat16
I32 = mybir.dt.int32
ALU = mybir.AluOpType
ACT = mybir.ActivationFunctionType
AX = mybir.AxisListType.X

P = 128
BATCH, SEQ, D = 4, 1024, 128
TOKENS = BATCH * SEQ
TILES = TOKENS // P
BT = SEQ // P
HALF = SEQ // 2
HT = HALF // P
STATES = 16
RANK = 64
GROUP = P // STATES
GROUPS = D // GROUP
PARTS = 3
QUARTER = 32
QG = QUARTER // GROUP
EXPERTS = 8
CAP = TOKENS // EXPERTS
TAPS = 3
FW = 64
DT_MIN, DT_MAX = 0.001, 0.1
EPS = 1e-5

C_ID, C_FLIP, C_TRI = 0, P, 2 * P
C_SEL = 3 * P
C_RED = C_SEL + QG * P
C_RANK = C_RED + QG * QUARTER
C_TOKEN = C_RANK + EXPERTS
C_END = C_TOKEN + TILES


def constant_table():
    t = np.zeros((P, C_END), np.float32)
    r = np.arange(P)
    t[r, C_ID + r] = 1.0
    t[r, C_FLIP + P - 1 - r] = 1.0
    t[:, C_TRI:C_TRI + P] = r[:, None] <= r[None, :]
    for s in range(QG):
        for part in range(PARTS):
            for p in range(P):
                t[part * QUARTER + s * GROUP + p % GROUP, C_SEL + s * P + p] = 1.0
    for s in range(QG):
        t[r, C_RED + s * QUARTER + s * GROUP + r % GROUP] = 1.0
    t[:, C_RANK:C_RANK + EXPERTS] = EXPERTS - np.arange(EXPERTS)
    t[:, C_TOKEN:C_TOKEN + TILES] = TOKENS + np.arange(TILES)[None, :] * P + r[:, None]
    return t


CREDIT = 2 * GROUPS


class Plan:

    ENGINES = ("sync", "tensor", "vector", "scalar", "gpsimd")

    def __init__(self, nc, ctx, memory, tag=""):
        self.nc, self.ctx, self.memory = nc, ctx, memory
        self.stages = {e: [] for e in self.ENGINES}
        self.owned = {e: [] for e in self.ENGINES}
        self.passed = {e: self.dma_sem("passed_" + e + tag) for e in ("sync", "gpsimd")}

    def sb(self, name, shape, dt=F32):
        return self.memory.enter_context(self.nc.sbuf_tensor(name, shape, dt))

    def dma_sem(self, name):
        return self.ctx.enter_context(self.nc.semaphore(name))

    def sem(self, owner, name):
        s = self.dma_sem(name)
        self.owned[owner].append(s)
        return s

    def sems(self, owner, names):
        return [self.sem(owner, n) for n in names.split()]

    def on(self, engine):
        return self.stages[engine].append

    def run(self):
        with self.nc.Block() as block:
            for name in self.ENGINES:
                def program(eng, name=name):
                    for s in self.owned[name]:
                        eng.sem_inc(s, CREDIT)
                    for stage in self.stages[name]:
                        stage(eng)
                {"sync": block.sync, "tensor": block.tensor, "vector": block.vector, "scalar": block.scalar,
                 "gpsimd": block.gpsimd}[name](program)


def need(eng, sem, count):
    eng.wait_ge(sem, count + CREDIT)


def alone(plan, eng, name):
    eng.sem_inc(plan.passed[name], 1)


def bank(ps, i, n=1):
    return ps[:, i * HALF:(i + n) * HALF]


def build(nc, t):
    with ExitStack() as ctx:
        ps = ctx.enter_context(nc.psum_tensor("ps", [P, 8 * HALF], F32))
        plan = Plan(nc, ctx, ctx)
        m = {"x": plan.sb("x", [P, TOKENS]),
             "const": plan.sb("const", [P, C_END]),
             "tri": plan.sb("tri", [P, P], BF16), "ones": plan.sb("ones", [P, P], BF16),
             "neg_half": plan.sb("neg_half", [P, TILES]),
             "stats": plan.sb("stats", [P, BT, 6]), "moments": plan.sb("moments", [P, BT, 2]),
             "spread": plan.sb("spread", [P, 3, TILES]), "neg_mean": plan.sb("neg_mean", [P, 3, TILES]),
             "rstd": plan.sb("rstd", [P, 3, TILES]), "shift": plan.sb("shift", [P, 3, TILES]),
             "slots": nc.dram_tensor("slots", (2 * TOKENS, D), F32).ap(),
             "answers": nc.dram_tensor("answers", (TOKENS, D), F32).ap(),
             "steps": nc.dram_tensor("steps", (P, BATCH * PARTS * SEQ), BF16).ap(),
             "taps": nc.dram_tensor("taps", (1, 4 * P), F32).ap()}
        with ExitStack() as early:
            plan.memory = early
            m["zeroed"] = plan.dma_sem("zeroed")
            project(plan, ps, m, t)
            step(plan, ps, m, t)
            scan(plan, ps, m, t)
            plan.run()
        plan2 = Plan(nc, ctx, ctx, "2")
        mixtures_and_conv(plan2, ps, m, t)
        plan2.run()


def project(plan, ps, m, t):
    x, const = m["x"], m["const"]
    sb = plan.sb
    ident = const[:, C_ID:C_ID + P]
    m["states"] = states = sb("states", [P, GROUPS * SEQ])
    m["exp_z"], m["sp"] = exp_z, relu_z = states[:, GROUPS * SEQ - 2 * TOKENS:GROUPS * SEQ - TOKENS], states[:, GROUPS * SEQ - TOKENS:]
    m["inp"], m["c_rows"], m["u"] = inp, c_rows, u = sb("inp", [P, TOKENS]), sb("c_rows", [P, TOKENS]), sb("u", [P, TOKENS])
    zero = sb("zero", [P, 1024])
    w_in, w_x, w_dt, b_dt = sb("w_in", [P, D]), sb("w_x", [P, RANK + 2 * STATES]), sb("w_dt", [RANK, D]), sb("b_dt", [P, 1])
    w_in_t = sb("w_in_t", [P, D])
    w_low = sb("w_low", [RANK, D])
    w_z = sb("w_z", [P, D])
    w_b, w_c = sb("w_b", [P, P]), sb("w_c", [P, P])
    stats, moments = sb("in_stats", [P, 2, HT, 6]), sb("in_moments", [P, 2, HT, 2])
    spread, rstd = sb("in_spread", [P, 2, HT]), sb("in_rstd", [P, 2, HT])
    m["scratch"] = scratch = sb("scratch", [P, 3 * SEQ])
    xn, xn_t, abs_z = (scratch[:, i * SEQ:(i + 1) * SEQ].rearrange("p (q s) -> p q s", q=2) for i in range(3))

    x_in = [plan.dma_sem(f"x_in{b}") for b in range(BATCH)]
    weights_in, consts_in = plan.dma_sem("weights_in"), plan.dma_sem("consts_in")
    zero_made, half_made, rstd_done = plan.sems("gpsimd", "zero_made half_made rstd_done")
    tri_made, moments_done, xn_ready, z_taken = plan.sems("vector", "tri_made moments_done xn_ready z_taken")
    fold_psum, xt_psum, z_psum, u_psum, b_psum, c_psum = plan.sems("tensor", "fold_psum xt_psum z_psum u_psum b_psum c_psum")
    fold_done, xt_ready, abs_done, u_taken, b_taken, c_taken, exp_done = plan.sems(
        "scalar", "fold_done xt_ready abs_done u_taken b_taken c_taken exp_done")
    m["exp_done"] = exp_done

    @plan.on("sync")
    def _(sp):
        for b in range(BATCH):
            sp.dma_start(x[:, b * SEQ:(b + 1) * SEQ].rearrange("p (i d) -> p i d", d=D),
                         t["x"][b:b + 1, :, :].rearrange("b (i p) d -> p (b i) d", p=P)).then_inc(x_in[b], 16)
        need(sp, zero_made, 1)
        for i in range(4):
            sp.dma_start(m["slots"][i * 1024:(i + 1) * 1024, :].rearrange("(p j) d -> p (j d)", p=P),
                         zero[:, :]).then_inc(m["zeroed"], 16)
        sp.dma_start(m["taps"][:, :], zero[0:1, 0:4 * P]).then_inc(m["zeroed"], 16)

    @plan.on("gpsimd")
    def _(pool):
        pool.memset(m["neg_half"][:, :], -0.5).then_inc(half_made, 1)
        pool.memset(m["ones"][:, :], 1.0)
        pool.memset(zero[:, :], 0.0).then_inc(zero_made, 1)
        need(pool, half_made, 1)
        with pool.Fori(0, BATCH) as b:
            for q in range(2):
                need(pool, moments_done, b * 2 + (q + 1))
                pool.tensor_tensor(rstd[:, q, :], spread[:, q, :], m["neg_half"][:, 0:HT], ALU.pow).then_inc(rstd_done, 1)

    @plan.on("scalar")
    def _(act):
        act.dma_start(const[:, :], t["table"]).then_inc(consts_in, 16)
        act.dma_start(w_in[:, :], t["a_w_in"]).then_inc(weights_in, 16)
        act.dma_start(w_x[:, :], t["a_w_x"]).then_inc(weights_in, 16)
        act.dma_start(w_dt[:, :], t["a_w_dt"]).then_inc(weights_in, 16)
        act.dma_start(b_dt[:, :], t["a_b_dt"].rearrange("(d o) -> d o", o=1)).then_inc(weights_in, 16)
        need(act, fold_psum, 1)
        act.copy(w_in_t[:, :], ps[:, 0:D]).then_inc(fold_done, 1)
        need(act, fold_psum, 2)
        act.copy(w_low[:, :], ps[0:RANK, HALF:HALF + D])
        act.copy(w_b[:, :], ps[:, 2 * HALF:2 * HALF + P])
        act.copy(w_c[:, :], ps[:, 3 * HALF:3 * HALF + P]).then_inc(fold_done, 1)
        need(act, fold_psum, 3)
        act.copy(w_z[:, :], ps[:, 4 * HALF:4 * HALF + D]).then_inc(fold_done, 1)
        with act.Fori(0, BATCH) as b:
            for q in range(2):
                need(act, xt_psum, b * 2 + (q + 1))
                need(act, c_psum, b * 2 + q - 1)
                act.copy(xn_t[:, q, :], bank(ps, q)).then_inc(xt_ready, 1)
            for q in range(2):
                cols = bass.ds(b * SEQ + q * HALF, HALF)
                need(act, z_psum, b * 2 + (q + 1))
                act.activation(abs_z[:, q, :], bank(ps, 2), ACT.Abs, bias=b_dt[:, 0:1]).then_inc(abs_done, 1)
                need(act, u_psum, b * 2 + (q + 1))
                act.copy(u[:, cols], bank(ps, 3)).then_inc(u_taken, 1)
                need(act, b_psum, b * 2 + (q + 1))
                act.copy(inp[:, cols], bank(ps, 4)).then_inc(b_taken, 1)
                need(act, c_psum, b * 2 + (q + 1))
                act.copy(c_rows[:, cols], bank(ps, 5)).then_inc(c_taken, 1)
                need(act, abs_done, b * 2 + (q + 1))
                act.activation(exp_z[:, cols], abs_z[:, q, :], ACT.Exp, scale=-1.0).then_inc(exp_done, 1)

    @plan.on("vector")
    def _(dve):
        dve.wait_ge(consts_in, 16)
        dve.tensor_copy(m["tri"][:, :], const[:, C_TRI:C_TRI + P])
        dve.tensor_copy(m["sel"][:, :], const[:, C_SEL:C_SEL + QG * P])
        dve.tensor_copy(m["red"][:, :], const[:, C_RED:C_RED + QG * QUARTER]).then_inc(tri_made, 1)
        dve.wait_ge(weights_in, 16 * 4)

        def statistics(b, q):
            for i in range(HT):
                dve.bn_stats(stats[:, q, i, :], x[:, bass.ds(b * SEQ + (q * HT + i) * D, D)])
            dve.drain()
            for i in range(HT):
                dve.bn_aggr(moments[:, q, i, :], stats[:, q, i, :])
            dve.drain()
            dve.tensor_scalar(spread[:, q, :], moments[:, q, :, 1], EPS, None, ALU.add).then_inc(moments_done, 1)

        def normalize(b, q):
            need(dve, rstd_done, b * 2 + (q + 1))
            need(dve, xt_psum, b * 2 + q - 1)
            for i in range(HT):
                last = dve.tensor_scalar(xn[:, q, i * D:(i + 1) * D], x[:, bass.ds(b * SEQ + (q * HT + i) * D, D)],
                                         moments[:, q, i, 0:1], rstd[:, q, i:i + 1], ALU.subtract, ALU.mult)
            last.then_inc(xn_ready, 1)

        for b in range(BATCH):
            dve.wait_ge(x_in[b], 16)
            if b == 0:
                statistics(0, 0)
                normalize(0, 0)
                statistics(0, 1)
                normalize(0, 1)
        with dve.Fori(0, BATCH - 1) as b:
            for q in range(2):
                statistics(b + 1, q)
                need(dve, abs_done, b * 2 + (q + 1))
                dve.tensor_scalar(relu_z[:, bass.ds(b * SEQ + q * HALF, HALF)], bank(ps, 2), b_dt[:, 0:1], 0.0,
                                  ALU.add, ALU.max).then_inc(z_taken, 1)
                normalize(b + 1, q)
        for q in range(2):
            need(dve, abs_done, (BATCH - 1) * 2 + q + 1)
            dve.tensor_scalar(relu_z[:, (BATCH - 1) * SEQ + q * HALF:(BATCH - 1) * SEQ + (q + 1) * HALF], bank(ps, 2),
                              b_dt[:, 0:1], 0.0, ALU.add, ALU.max).then_inc(z_taken, 1)

    @plan.on("tensor")
    def _(pe):
        pe.wait_ge(consts_in, 16)
        pe.wait_ge(weights_in, 16 * 4)
        pe.transpose(ps[:, 0:D], w_in[:, :], ident).then_inc(fold_psum, 1)
        need(pe, fold_done, 1)
        rep = lambda a: a.rearrange("p (n o) -> p n o", o=1).broadcast_to([P, STATES, GROUP])
        pe.matmul(ps[0:RANK, HALF:HALF + D], w_x[:, 0:RANK], w_in_t[:, :], start=True, stop=True)
        pe.matmul(ps[:, 2 * HALF:2 * HALF + P], w_in_t[:, :], rep(w_x[:, RANK:RANK + STATES]), start=True, stop=True)
        pe.matmul(ps[:, 3 * HALF:3 * HALF + P], w_in_t[:, :], rep(w_x[:, RANK + STATES:]), start=True,
                  stop=True).then_inc(fold_psum, 1)
        need(pe, fold_done, 2)
        pe.matmul(ps[:, 4 * HALF:4 * HALF + D], w_low[:, :], w_dt[:, :], start=True, stop=True).then_inc(fold_psum, 1)
        need(pe, fold_done, 3)

        def transpose(b, q):
            need(pe, xn_ready, b * 2 + (q + 1))
            need(pe, xt_ready, b * 2 + q - 1)
            for i in range(HT):
                last = pe.transpose(ps[:, q * HALF + i * P:q * HALF + (i + 1) * P], xn[:, q, i * D:(i + 1) * D], ident)
            last.then_inc(xt_psum, 1)

        def products(b, q):
            need(pe, xt_ready, b * 2 + (q + 1))
            for w, at, full, taken in ((w_z, 2, z_psum, z_taken), (w_in, 3, u_psum, u_taken),
                                       (w_b, 4, b_psum, b_taken), (w_c, 5, c_psum, c_taken)):
                need(pe, taken, b * 2 + q)
                pe.matmul(bank(ps, at), w[:, :], xn_t[:, q, :], start=True, stop=True).then_inc(full, 1)

        with pe.Fori(0, BATCH) as b:
            for q in range(2):
                transpose(b, q)
            for q in range(2):
                products(b, q)


def step(plan, ps, m, t):
    sp_all, exp_z, inp, u = m["sp"], m["exp_z"], m["inp"], m["u"]
    sb = plan.sb
    a_neg = sb("a_neg", [P, STATES])
    a_range, a_min = sb("a_range", [P, P]), sb("a_min", [P, P])
    a_p = sb("a_p", [P, GROUPS])
    m["scale_p"], m["bias_p"] = scale_p, bias_p = sb("scale_p", [P, GROUPS]), sb("bias_p", [P, GROUPS])
    m["sel"], m["red"] = sb("sel", [P, QG * P], BF16), sb("red", [P, QG * QUARTER])
    part = sb("part", [P, 2, PARTS * SEQ], BF16)
    rest = m["scratch"][:, 0:2 * SEQ].rearrange("p (q s) -> p q s", q=2)
    spu = m["scratch"][:, 2 * SEQ:]
    m["stack"] = stack = sb("stack", [PARTS * QUARTER, QUARTER // GROUP, TOKENS], BF16)
    a_in, steps_out = plan.dma_sem("a_in"), plan.dma_sem("steps_out")
    m["stacked"] = stacked = [plan.dma_sem(f"stacked{b}") for b in range(BATCH)]
    a_exp, ln_done, hi_done, mid_done = plan.sems("scalar", "a_exp ln_done hi_done mid_done")
    a_made, sp_done, lo_done, inp_done = plan.sems("vector", "a_made sp_done lo_done inp_done")
    rest_done, spu_done = plan.sems("gpsimd", "rest_done spu_done")
    q_psum = plan.sem("tensor", "q_psum")
    parts_free = plan.sem("sync", "parts_free")

    @plan.on("sync")
    def _(sp):
        for b in range(BATCH):
            need(sp, lo_done, b + 1)
            sp.dma_start(m["steps"][:, b * PARTS * SEQ:(b + 1) * PARTS * SEQ],
                         part[:, b % 2, :]).then_inc(steps_out, 16)
            sp.wait_ge(steps_out, b * 16 + 16)
            sp.sem_inc(parts_free, 1)
            for a in range(PARTS):
                sp.dma_start(stack[a * QUARTER:(a + 1) * QUARTER, :, b * SEQ:(b + 1) * SEQ],
                             m["steps"][:, (b * PARTS + a) * SEQ:(b * PARTS + a + 1) * SEQ].rearrange(
                                 "(q r) s -> r q s", r=QUARTER)).then_inc(stacked[b], 16)

    @plan.on("scalar")
    def _(act):
        act.dma_start(a_neg[:, :], t["a_A_log"]).then_inc(a_in, 16)
        act.dma_start(a_p[:, :], t["a_A_log_p"]).then_inc(a_in, 16)
        act.wait_ge(a_in, 32)
        act.activation(a_neg[:, :], a_neg[:, :], ACT.Exp)
        act.activation(a_p[:, :], a_p[:, :], ACT.Exp).then_inc(a_exp, 1)

        for b in range(BATCH):
            cols = slice(b * SEQ, (b + 1) * SEQ)
            need(act, m["exp_done"], b * 2 + 2)
            act.activation(exp_z[:, cols], exp_z[:, cols], ACT.Ln, bias=1.0).then_inc(ln_done, 1)
        with act.Fori(0, BATCH // 2) as bb:
            for q in range(2):
                need(act, sp_done, bb * 2 + (q + 1))
                need(act, parts_free, bb * 2 + q - 1)
                act.copy(part[:, q, 0:SEQ], sp_all[:, bass.ds((bb * 2 + q) * SEQ, SEQ)]).then_inc(hi_done, 1)
            for q in range(2):
                need(act, rest_done, bb * 2 + (q + 1))
                act.copy(part[:, q, SEQ:2 * SEQ], rest[:, q, :]).then_inc(mid_done, 1)

    @plan.on("vector")
    def _(dve):
        need(dve, a_exp, 1)
        dve.tensor_scalar(a_neg[:, :], a_neg[:, :], -1.0, None, ALU.mult)
        dve.tensor_scalar(scale_p[:, :], a_p[:, :], -(DT_MAX - DT_MIN), None, ALU.mult)
        dve.tensor_scalar(bias_p[:, :], a_p[:, :], -DT_MIN, None, ALU.mult)
        dve.drain()
        rep = a_neg[:, :].rearrange("p (n o) -> p n o", o=1).broadcast_to([P, STATES, GROUP])
        dve.tensor_scalar(a_range[:, :].rearrange("p (n j) -> p n j", j=GROUP), rep, DT_MAX - DT_MIN, None, ALU.mult)
        dve.tensor_scalar(a_min[:, :].rearrange("p (n j) -> p n j", j=GROUP), rep, DT_MIN, None, ALU.mult).then_inc(a_made, 1)
        for b in range(BATCH):
            cols = slice(b * SEQ, (b + 1) * SEQ)
            need(dve, ln_done, b + 1)
            dve.tensor_tensor(sp_all[:, cols], sp_all[:, cols], exp_z[:, cols], ALU.add).then_inc(sp_done, 1)
        with dve.Fori(0, BATCH // 2) as bb:
            for q in range(2):
                cols = bass.ds((bb * 2 + q) * SEQ, SEQ)
                need(dve, mid_done, bb * 2 + (q + 1))
                dve.tensor_tensor(part[:, q, 2 * SEQ:], rest[:, q, :], part[:, q, SEQ:2 * SEQ], ALU.subtract).then_inc(lo_done, 1)
                need(dve, q_psum, bb * 2 + (q + 1))
                dve.tensor_tensor(inp[:, cols], inp[:, cols], bank(ps, 6, 2), ALU.mult).then_inc(inp_done, 1)

    @plan.on("gpsimd")
    def _(pool):
        with pool.Fori(0, BATCH // 2) as bb:
            for q in range(2):
                cols = bass.ds((bb * 2 + q) * SEQ, SEQ)
                need(pool, hi_done, bb * 2 + (q + 1))
                need(pool, lo_done, bb * 2 + q - 1)
                alone(plan, pool, "gpsimd")
                pool.tensor_tensor(rest[:, q, :], sp_all[:, cols], part[:, q, 0:SEQ], ALU.subtract).then_inc(rest_done, 1)
                need(pool, q_psum, bb * 2 + q)
                alone(plan, pool, "gpsimd")
                pool.tensor_tensor(spu[:, :], sp_all[:, cols], u[:, cols], ALU.mult).then_inc(spu_done, 1)

    @plan.on("tensor")
    def _(pe):
        need(pe, a_made, 1)
        with pe.Fori(0, BATCH) as b:
            need(pe, spu_done, b + 1)
            need(pe, inp_done, b)
            for q in range(2):
                pe.matmul(bank(ps, 6 + q), a_range[:, :], spu[:, q * HALF:(q + 1) * HALF], start=True, stop=False)
                last = pe.matmul(bank(ps, 6 + q), a_min[:, :], u[:, bass.ds(b * SEQ + q * HALF, HALF)], start=False, stop=True)
            last.then_inc(q_psum, 1)


ON_DVE = (2, 5, 8, 11, 14)
SLOTS = [u % 3 for u in range(GROUPS - 1)] + [1]
QUARTERS = D // QUARTER
LAG = 7
LAST_SUM = (GROUPS - 1 + LAG) % GROUPS


def before(u, same):
    j = u - 1
    while not same(j % GROUPS):
        j -= 1
    return j


def upto(u, on_dve):
    mine = [v for v in range(GROUPS) if (v in ON_DVE) == on_dve]
    return (u // GROUPS) * len(mine) + sum(1 for v in mine if v <= u % GROUPS)


def scan(plan, ps, m, t):
    x, const, u_all = m["x"], m["const"], m["u"]
    inp, c_rows, sel, red, stack = m["inp"], m["c_rows"], m["sel"], m["red"], m["stack"]
    ident = const[:, C_ID:C_ID + P]
    h = m["states"]
    y_t = m["scratch"][:, 0:SEQ]
    skip, warm = plan.sb("skip", [P, 1]), plan.sb("warm", [P, 1])
    skip_in = plan.dma_sem("skip_in")
    dt_psum, summed, y_psum = plan.sems("tensor", "dt_psum summed y_psum")
    decay_ready = plan.sem("scalar", "decay_ready")
    scanned, prod_dve, y_taken, x_added = plan.sems("vector", "scanned prod_dve y_taken x_added")
    prod_pool = plan.sem("gpsimd", "prod_pool")
    n_dve, n_pool = len(ON_DVE), GROUPS - len(ON_DVE)
    group = lambda u: QG * (u % QUARTERS) + u // QUARTERS
    slot = lambda u: bank(ps, 2 * SLOTS[u], 2)

    def need_products(eng, b, u):
        need(eng, prod_dve, b * n_dve + upto(u, True))
        need(eng, prod_pool, b * n_pool + upto(u, False))

    @plan.on("sync")
    def _(sp):
        sp.dma_start(skip[:, :], t["a_Dp"].rearrange("(d o) -> d o", o=1)).then_inc(skip_in, 16)

    @plan.on("tensor")
    def _(pe):
        def broadcast(b, u):
            need(pe, scanned, b * GROUPS + before(u, lambda v: SLOTS[v] == SLOTS[u]) + 1)
            g = group(u)
            for q in range(2):
                last = pe.matmul(bank(ps, 2 * SLOTS[u] + q), sel[0:PARTS * QUARTER, (g % QG) * P:(g % QG + 1) * P],
                                 stack[:, g // QG, bass.ds(b * SEQ + q * HALF, HALF)], start=True, stop=True)
            last.then_inc(dt_psum, 1)

        def state_sum(b, r):
            need_products(pe, b, QUARTERS * r + QUARTERS - 1)
            if r == 0:
                need(pe, x_added, b)
            for q in range(2):
                for c in range(QUARTERS):
                    last = pe.matmul(ps[c * QUARTER:(c + 1) * QUARTER, (6 + q) * HALF:(7 + q) * HALF],
                                     red[:, r * QUARTER:(r + 1) * QUARTER],
                                     h[:, (QUARTERS * r + c) * SEQ + q * HALF:(QUARTERS * r + c) * SEQ + (q + 1) * HALF],
                                     start=r == 0, stop=r == QG - 1)
            last.then_inc(summed, 1)

        def back_to_tokens(b):
            need(pe, y_taken, b + 1)
            for i in range(BT):
                last = pe.transpose(ps[:, 6 * HALF + i * P:6 * HALF + (i + 1) * P], y_t[:, i * P:(i + 1) * P], ident)
            last.then_inc(y_psum, 1)

        def row(b, behind):
            for u in range(GROUPS):
                broadcast(b, u)
                r, late = divmod(u - LAG - QUARTERS + 1, QUARTERS)
                if u == LAST_SUM + 3 and behind:
                    back_to_tokens(b - 1)
                if late == 0 and (r >= 0 or behind):
                    state_sum(b if r >= 0 else b - 1, r % QG)

        for b in range(BATCH):
            pe.wait_ge(m["stacked"][b], 16 * PARTS)
            if b == 0:
                row(0, False)
        with pe.Fori(1, BATCH) as b:
            row(b, True)
        for r in range(QG):
            if QUARTERS * r + QUARTERS - 1 + LAG >= GROUPS:
                state_sum(BATCH - 1, r)
        back_to_tokens(BATCH - 1)

    @plan.on("scalar")
    def _(act):
        act.activation(warm[:, :], m["bias_p"][:, 0:1], ACT.Exp)
        with act.Fori(0, BATCH) as b:
            for u in range(GROUPS):
                need(act, dt_psum, b * GROUPS + (u + 1))
                act.activation(slot(u), slot(u), ACT.Exp, scale=m["scale_p"][:, group(u):group(u) + 1],
                               bias=m["bias_p"][:, group(u):group(u) + 1]).then_inc(decay_ready, 1)

    def multiply(eng, done, b, u):
        need(eng, scanned, b * GROUPS + (u + 1))
        if eng is plan.nc.gpsimd:
            alone(plan, eng, "gpsimd")
        eng.tensor_tensor(h[:, u * SEQ:(u + 1) * SEQ], h[:, u * SEQ:(u + 1) * SEQ], c_rows[:, bass.ds(b * SEQ, SEQ)],
                          ALU.mult).then_inc(done, 1)

    @plan.on("vector")
    def _(dve):
        dve.wait_ge(skip_in, 16)

        def take_sums(b):
            need(dve, summed, b * QG + QG)
            dve.scalar_tensor_tensor(out=y_t[:, :], in0=u_all[:, bass.ds(b * SEQ, SEQ)], scalar=skip[:, 0:1],
                                     in1=bank(ps, 6, 2), op0=ALU.mult, op1=ALU.add).then_inc(y_taken, 1)

        def add_to_x(b):
            need(dve, y_psum, b + 1)
            cols = bass.ds(b * SEQ, SEQ)
            dve.tensor_tensor(x[:, cols], x[:, cols], bank(ps, 6, 2), ALU.add).then_inc(x_added, 1)
            dve.drain()
            statistics(dve, m, 0, b)

        def row(b, behind):
            for u in range(GROUPS):
                need(dve, decay_ready, b * GROUPS + (u + 1))
                need(dve, summed, b * QG + (u - GROUPS) // QUARTERS + 1)
                dve.tensor_tensor_scan(h[:, u * SEQ:(u + 1) * SEQ], slot(u), inp[:, bass.ds(b * SEQ, SEQ)], 0.0,
                                       ALU.mult, ALU.add).then_inc(scanned, 1)
                if u - 1 in ON_DVE:
                    multiply(dve, prod_dve, b, u - 1)
                if behind and u == LAST_SUM - 1:
                    take_sums(b - 1)
                if behind and u == LAST_SUM + 2:
                    add_to_x(b - 1)

        row(0, False)
        with dve.Fori(1, BATCH) as b:
            row(b, True)
        take_sums(BATCH - 1)
        add_to_x(BATCH - 1)

    @plan.on("gpsimd")
    def _(pool):
        with pool.Fori(0, BATCH) as b:
            for u in range(GROUPS):
                if u not in ON_DVE:
                    multiply(pool, prod_pool, b, u)




def late_memory(plan, m, t):
    sb = plan.sb
    for name, shape, dt in (
            ("w_r", [P, EXPERTS], F32), ("b_r", [P, EXPERTS], F32), ("b1", [P, EXPERTS], F32), ("b2", [P, EXPERTS * D], F32),
            ("rx", [P, 2, SEQ], F32), ("rx_t", [P, 2, SEQ], F32), ("gated", [P, 2, SEQ], F32), ("back", [P, BATCH, SEQ], F32),
            ("logit", [P, BT, EXPERTS], F32), ("top", [P, BT], F32), ("below", [P, 2, BT, EXPERTS], F32),
            ("prob", [P, 2, BT, EXPERTS], F32), ("ranked", [P, BT, EXPERTS], F32), ("first", [P, 2, BT], F32),
            ("onehot", [P, 2, BT, EXPERTS], BF16), ("own", [P, EXPERTS], F32), ("prior", [P, 2, EXPERTS], BF16),
            ("total", [P, BT], F32), ("gate", [P, 2, BT], F32), ("cum", [P, BT, EXPERTS], F32), ("pos", [P, BT], F32),
            ("kept", [P, BT], F32), ("inside", [P, BT], F32), ("row", [P, BT], F32), ("offset", [P, BT], F32),
            ("weight", [P, TILES], F32), ("put", [P, 2, BT], I32), ("get", [P, TILES], I32),
            ("e_w1", [P, 4, D], F32), ("e_w2", [P, 4, D], F32), ("rows", [P, 4, HALF], F32), ("rows_t", [P, 2, HALF], F32),
            ("hidden", [P, 2, HALF], F32), ("reply", [P, EXPERTS, HALF], F32)):
        m[name] = sb(name, shape, dt)
    m["router_in"] = plan.dma_sem("router_in")

    @plan.on("sync")
    def _(sp):
        for dst, src in ((m["w_r"], t["f_Wr"]), (m["b_r"], t["f_br"].rearrange("(o e) -> o e", o=1).broadcast_to([P, EXPERTS])),
                         (m["b1"], t["f_b1_t"]),
                         (m["b2"], t["f_b2"].rearrange("(o e) d -> o (e d)", o=1).broadcast_to([P, EXPERTS * D]))):
            sp.dma_start(dst[:, :], src).then_inc(m["router_in"], 16)


def statistics(dve, m, use, b):
    tiles = bass.ds(b * BT, BT) if not isinstance(b, int) else slice(b * BT, (b + 1) * BT)
    for i in range(BT):
        dve.bn_stats(m["stats"][:, i, :], m["x"][:, bass.ds(b * SEQ + i * D, D)])
    dve.drain()
    for i in range(BT):
        dve.bn_aggr(m["moments"][:, i, :], m["stats"][:, i, :])
    dve.drain()
    dve.tensor_scalar(m["spread"][:, use, tiles], m["moments"][:, :, 1], EPS, None, ALU.add)
    return dve.tensor_scalar(m["neg_mean"][:, use, tiles], m["moments"][:, :, 0], -1.0, None, ALU.mult)


def deviations(pool, m, use, first, rows, chained, count):
    tiles = slice(first * BT, (first + rows) * BT)
    pool.tensor_tensor(m["rstd"][:, use, tiles], m["spread"][:, use, tiles], m["neg_half"][:, 0:rows * BT],
                       ALU.pow).then_inc(chained, 1)
    need(pool, chained, count)
    return pool.tensor_tensor(m["shift"][:, use, tiles], m["neg_mean"][:, use, tiles], m["rstd"][:, use, tiles], ALU.mult)


def normalize(act, m, use, b, dst, done):
    for i in range(BT):
        tile = b * BT + i
        act.activation(dst[:, i * D:(i + 1) * D], m["x"][:, tile * D:(tile + 1) * D], ACT.Identity,
                       scale=m["rstd"][:, use, tile:tile + 1], bias=m["shift"][:, use, tile:tile + 1]).then_inc(done, 1)


class Router:

    TRANSPOSED, LOGITS, COUNTS = 0, 6, 7

    def __init__(self, plan, ps, m, tr):
        self.plan, self.ps, self.m, self.tr = plan, ps, m, tr
        self.moments = plan.sem("vector", "r_moments")
        self.rstd = plan.sem("gpsimd", "r_rstd")
        self.normal, self.xt, self.exp, self.gated = plan.sems("scalar", "r_normal r_xt r_exp r_gated")
        self.logit_psum, self.count_psum = plan.sems("tensor", "r_logit_psum r_count_psum")
        self.logit_read, self.below, self.hot, self.gate, self.placed = plan.sems(
            "vector", "r_logit_read r_below r_hot r_gate r_placed")
        self.put_done = [plan.dma_sem(f"put{b}") for b in range(BATCH)]

    def scattered(self, n):
        return self.put_done[n % BATCH], (n // BATCH + 1) * 16 * BT

    def normalize(self, act, n):
        m = self.m
        need(act, self.rstd, 1 if n < BATCH else n - BATCH + 2)
        need(act, self.tr.full, self.tr.at("r", n - 2))
        need(act, self.gated, (n - 1) * BT)
        normalize(act, m, 0 if n < BATCH else 2, n % BATCH, m["rx"][:, n % 2, :], self.normal)

    def transpose(self, pe, n):
        self.tr.transpose(pe, "r", n, self.m["rx"][:, n % 2, :], self.normal, n * BT + 1)

    def copy(self, act, n):
        need(act, self.logit_psum, n - 1)
        self.tr.copy(act, "r", n, self.m["rx_t"][:, n % 2, :])

    def logits(self, pe, n):
        self.tr.need_copy(pe, "r", n)
        need(pe, self.logit_read, n)
        for i in range(BT):
            last = pe.matmul(self.ps[:, self.LOGITS * HALF + i * EXPERTS:self.LOGITS * HALF + (i + 1) * EXPERTS],
                             self.m["rx_t"][:, n % 2, i * P:(i + 1) * P], self.m["w_r"][:, :], start=True, stop=True)
        last.then_inc(self.logit_psum, 1)

    def choose(self, dve, n):
        m, q = self.m, n % 2
        wide = lambda a: a.rearrange("p (i o) -> p i o", o=1).broadcast_to([P, BT, EXPERTS])
        same = lambda a: a.rearrange("p (o e) -> p o e", o=1).broadcast_to([P, BT, EXPERTS])
        rank = same(m["const"][:, C_RANK:C_RANK + EXPERTS])
        need(dve, self.logit_psum, n + 1)
        dve.tensor_tensor(m["logit"][:, :, :], bank(self.ps, self.LOGITS)[:, 0:BT * EXPERTS].rearrange("p (i e) -> p i e", e=EXPERTS),
                          same(m["b_r"][:, :]), ALU.add).then_inc(self.logit_read, 1)
        dve.drain()
        dve.tensor_reduce(m["top"][:, :], m["logit"][:, :, :], AX, ALU.max)
        dve.drain()
        need(dve, self.exp, n - 1)
        dve.tensor_tensor(m["below"][:, q, :, :], m["logit"][:, :, :], wide(m["top"][:, :]), ALU.subtract).then_inc(self.below, 1)
        dve.drain()
        dve.scalar_tensor_tensor(out=m["ranked"][:, :, :], in0=m["below"][:, q, :, :], scalar=0.0, in1=rank,
                                 op0=ALU.is_equal, op1=ALU.mult)
        dve.drain()
        dve.tensor_reduce(m["first"][:, q, :], m["ranked"][:, :, :], AX, ALU.max)
        dve.drain()
        need(dve, self.count_psum, n - 1)
        dve.tensor_tensor(m["onehot"][:, q, :, :], wide(m["first"][:, q, :]), rank, ALU.is_equal).then_inc(self.hot, 1)
        if n % BATCH < BATCH - 1:
            dve.drain()
            dve.tensor_reduce(m["own"][:, :], m["onehot"][:, q, :, :].rearrange("p i e -> p e i"), AX, ALU.add)
            dve.drain()
            need(dve, self.count_psum, n)
            dve.tensor_tensor(m["prior"][:, 1 - q, :], m["prior"][:, q, :], m["own"][:, :], ALU.add)

    def probabilities(self, act, n):
        need(act, self.below, n + 1)
        need(act, self.placed, n - 1)
        act.activation(self.m["prob"][:, n % 2, :, :], self.m["below"][:, n % 2, :, :], ACT.Exp).then_inc(self.exp, 1)

    def count(self, pe, n):
        m, q, at = self.m, n % 2, self.COUNTS * HALF
        need(pe, self.hot, n + 1)
        need(pe, self.placed, n)
        counts = self.ps[:, at:at + BT * EXPERTS]
        pe.matmul(counts, m["tri"][:, :], m["onehot"][:, q, :, :].rearrange("p i e -> p (i e)"), start=True, stop=False)
        for i in range(BT - 1):
            pe.matmul(self.ps[:, at + (i + 1) * EXPERTS:at + BT * EXPERTS], m["ones"][:, :],
                      m["onehot"][:, q, i:i + 1, :].broadcast_to([P, BT - 1 - i, EXPERTS]), start=False, stop=False)
        pe.matmul(counts, m["ones"][:, :], m["prior"][:, q:q + 1, :].broadcast_to([P, BT, EXPERTS]),
                  start=False, stop=True).then_inc(self.count_psum, 1)

    def place(self, dve, n):
        m, q, b = self.m, n % 2, n % BATCH
        token = m["const"][:, C_TOKEN + b * BT:C_TOKEN + (b + 1) * BT]
        need(dve, self.exp, n + 1)
        dve.tensor_reduce(m["total"][:, :], m["prob"][:, q, :, :], AX, ALU.add)
        dve.drain()
        need(dve, self.gated, (n - 1) * BT)
        dve.reciprocal(m["gate"][:, q, :], m["total"][:, :]).then_inc(self.gate, 1)
        need(dve, self.count_psum, n + 1)
        dve.tensor_tensor(m["cum"][:, :, :], bank(self.ps, self.COUNTS)[:, 0:BT * EXPERTS].rearrange("p (i e) -> p i e", e=EXPERTS),
                          m["onehot"][:, q, :, :], ALU.mult)
        dve.drain()
        dve.tensor_reduce(m["pos"][:, :], m["cum"][:, :, :], AX, ALU.add)
        dve.drain()
        dve.tensor_scalar(m["kept"][:, :], m["pos"][:, :], float(CAP), None, ALU.is_lt)
        dve.scalar_tensor_tensor(out=m["inside"][:, :], in0=m["pos"][:, :], scalar=float(CAP), in1=m["pos"][:, :],
                                 op0=ALU.is_lt, op1=ALU.mult)
        dve.drain()
        dve.scalar_tensor_tensor(out=m["row"][:, :], in0=m["first"][:, q, :], scalar=-float(CAP), in1=m["inside"][:, :],
                                 op0=ALU.mult, op1=ALU.add)
        if n >= BATCH and b == 0:
            for s in self.fetched:
                dve.wait_ge(s, 16 * BT)
        dve.tensor_tensor(m["weight"][:, b * BT:(b + 1) * BT], m["kept"][:, :], m["gate"][:, q, :], ALU.mult)
        dve.drain()
        dve.tensor_scalar(m["get"][:, b * BT:(b + 1) * BT], m["row"][:, :], float(EXPERTS * CAP), None, ALU.add)
        dve.scalar_tensor_tensor(out=m["offset"][:, :], in0=m["row"][:, :], scalar=float(EXPERTS * CAP), in1=token,
                                 op0=ALU.add, op1=ALU.subtract)
        dve.drain()
        dve.tensor_tensor(m["offset"][:, :], m["offset"][:, :], m["kept"][:, :], ALU.mult)
        dve.drain()
        if n >= 2:
            dve.wait_ge(*self.scattered(n - 2))
        dve.tensor_tensor(m["put"][:, q, :], m["offset"][:, :], token, ALU.add).then_inc(self.placed, 1)

    def gate_rows(self, act, n):
        m, q = self.m, n % 2
        need(act, self.gate, n + 1)
        if n >= 2:
            act.wait_ge(*self.scattered(n - 2))
        for i in range(BT):
            act.activation(m["gated"][:, q, i * D:(i + 1) * D], m["rx"][:, q, i * D:(i + 1) * D], ACT.Copy,
                           scale=m["gate"][:, q, i:i + 1]).then_inc(self.gated, 1)

    def scatter(self, pool, n):
        m, q = self.m, n % 2
        need(pool, self.placed, n + 1)
        if n == 0:
            pool.wait_ge(m["zeroed"], 16 * 5)
        for i in range(BT):
            need(pool, self.gated, n * BT + i + 1)
            pool.indirect_dma_start(out=m["slots"], out_offset=bass.IndirectOffsetOnAxis(m["put"][:, q, i:i + 1], 0),
                                    in_=m["gated"][:, q, i * D:(i + 1) * D], in_offset=None).then_inc(self.put_done[n % BATCH], 16)


class Transposer:

    def __init__(self, plan, ps, m, order):
        self.ps, self.m, self.order = ps, m, order
        self.full, self.left = plan.sem("tensor", "tr_full"), plan.sem("scalar", "tr_left")

    def at(self, who, n):
        return 2 * (self.order.index((who, n)) + 1) if n >= 0 else 0

    def transpose(self, pe, who, n, src, ready, first):
        at = self.at(who, n)
        for i in range(BT):
            if i % HT == 0:
                need(pe, self.left, at - 3 + i // HT)
            need(pe, ready, first + (i if who != "v" else 0))
            last = pe.transpose(self.ps[:, i * P:(i + 1) * P], src[:, i * D:(i + 1) * D], self.m["const"][:, C_ID:C_ID + P])
            if i % HT == HT - 1:
                last.then_inc(self.full, 1)

    def copy(self, act, who, n, dst):
        at = self.at(who, n)
        for h in range(2):
            need(act, self.full, at - 1 + h)
            act.copy(dst[:, h * HALF:(h + 1) * HALF], bank(self.ps, h)).then_inc(self.left, 1)

    def need_copy(self, pe, who, n, h=1):
        need(pe, self.left, self.at(who, n) - 1 + h)


class Experts:

    ROWS, HIDDEN, REPLY = 0, 2, 4
    PAIRS = EXPERTS // 2

    def __init__(self, plan, ps, m, t, router):
        self.plan, self.ps, self.m, self.t, self.router = plan, ps, m, t, router
        self.rows_psum, self.hidden_psum, self.reply_psum = plan.sems("tensor", "e_rows_psum e_hidden_psum e_reply_psum")
        self.rows_t, self.hidden = plan.sems("scalar", "e_rows_t e_hidden")
        self.reply = plan.sem("vector", "e_reply")
        self.w_in = [plan.dma_sem(f"e_w_in{k}") for k in range(2)]
        self.rows_in = [plan.dma_sem(f"e_rows_in{k}") for k in range(2)]
        self.stored = plan.dma_sem("e_stored")

    def load_weights(self, sp, layer, pair):
        e, k = 2 * pair, pair % 2
        need(sp, self.reply_psum, layer * EXPERTS + e - 2)
        for w, src in (("e_w1", "f_W1"), ("e_w2", "f_W2")):
            sp.dma_start(self.m[w][:, 2 * k:2 * k + 2, :], self.t[src][e:e + 2, :, :].rearrange("e d f -> d e f")).then_inc(self.w_in[k], 16)

    def load_rows(self, sp, layer, pair):
        e, k = 2 * pair, pair % 2
        need(sp, self.rows_psum, layer * EXPERTS + e - 2)
        sp.dma_start(self.m["rows"][:, 2 * k:2 * k + 2, :],
                     self.m["slots"][e * CAP:(e + 2) * CAP, :].rearrange("(e p j) d -> p e (j d)", e=2, p=P)).then_inc(self.rows_in[k], 16)

    def store(self, sp, layer, pair):
        e = 2 * pair
        need(sp, self.reply, layer * EXPERTS + e + 2)
        sp.dma_start(self.m["answers"][e * CAP:(e + 2) * CAP, :].rearrange("(e p j) d -> p e (j d)", e=2, p=P),
                     self.m["reply"][:, e:e + 2, :]).then_inc(self.stored, 16)

    def sync(self, sp, layer):
        for pair in range(2):
            self.load_weights(sp, layer, pair)
        for b in range(BATCH):
            sp.wait_ge(*self.router.scattered(layer * BATCH + b))
        for pair in range(2):
            self.load_rows(sp, layer, pair)
        for pair in range(2, self.PAIRS):
            self.load_rows(sp, layer, pair)
            self.load_weights(sp, layer, pair)
            self.store(sp, layer, pair - 2)
        for pair in range(self.PAIRS - 2, self.PAIRS):
            self.store(sp, layer, pair)

    def tensor(self, pe, layer):
        m, ps, ident = self.m, self.ps, self.m["const"][:, C_ID:C_ID + P]
        with pe.Fori(0, self.PAIRS // 2) as c:
            for k in range(2):
                e = c * 4 + (layer * EXPERTS + 2 * k)
                pe.wait_ge(self.rows_in[k], c * 16 + (layer * (self.PAIRS // 2) + 1) * 16)
                for q in range(2):
                    need(pe, self.rows_t, e + (q - 1))
                    for j in range(HT):
                        last = pe.transpose(ps[:, (self.ROWS + q) * HALF + j * P:(self.ROWS + q) * HALF + (j + 1) * P],
                                            m["rows"][:, 2 * k + q, j * D:(j + 1) * D], ident)
                    last.then_inc(self.rows_psum, 1)
                pe.wait_ge(self.w_in[k], c * 32 + (layer * (self.PAIRS // 2) + 1) * 32)
                for q in range(2):
                    need(pe, self.rows_t, e + (q + 1))
                    need(pe, self.hidden, e + (q - 1))
                    pe.matmul(bank(ps, self.HIDDEN + q), m["e_w1"][:, 2 * k + q, :], m["rows_t"][:, q, :], start=True,
                              stop=True).then_inc(self.hidden_psum, 1)
                for q in range(2):
                    need(pe, self.hidden, e + (q + 1))
                    need(pe, self.reply, e + (q - 1))
                    for j in range(HT):
                        last = pe.matmul(ps[:, (self.REPLY + q) * HALF + j * D:(self.REPLY + q) * HALF + (j + 1) * D],
                                         m["hidden"][:, q, j * P:(j + 1) * P], m["e_w2"][:, 2 * k + q, :], start=True, stop=True)
                    last.then_inc(self.reply_psum, 1)

    def scalar(self, act, layer):
        m, ps = self.m, self.ps
        with act.Fori(0, self.PAIRS) as c:
            e = c * 2 + layer * EXPERTS
            for q in range(2):
                need(act, self.rows_psum, e + (q + 1))
                need(act, self.hidden_psum, e + (q - 1))
                act.copy(m["rows_t"][:, q, :], bank(ps, self.ROWS + q)).then_inc(self.rows_t, 1)
            for q in range(2):
                need(act, self.hidden_psum, e + (q + 1))
                need(act, self.reply_psum, e + (q - 1))
                act.activation(m["hidden"][:, q, :], bank(ps, self.HIDDEN + q), ACT.Relu,
                               bias=m["b1"][:, bass.ds(c * 2 + q, 1)]).then_inc(self.hidden, 1)

    def vector(self, dve, layer):
        m, ps = self.m, self.ps
        if layer:
            dve.wait_ge(self.stored, 16 * self.PAIRS)
        with dve.Fori(0, self.PAIRS) as c:
            for q in range(2):
                need(dve, self.reply_psum, c * 2 + (layer * EXPERTS + q + 1))
                dve.tensor_tensor(m["reply"][:, bass.ds(c * 2 + q, 1), :].rearrange("p o (j d) -> p (o j) d", d=D),
                                  bank(ps, self.REPLY + q).rearrange("p (j d) -> p j d", d=D),
                                  m["b2"][:, bass.ds(c * (2 * D) + q * D, D)].rearrange("p (o d) -> p o d", o=1).broadcast_to([P, HT, D]),
                                  ALU.add).then_inc(self.reply, 1)


class Answers:

    def __init__(self, plan, m, experts):
        self.m, self.experts = m, experts
        self.got = [plan.dma_sem(f"got{b}") for b in range(BATCH)]
        self.added = plan.sem("vector", "a_added")

    def fetch(self, pool, layer, b):
        m = self.m
        if b == 0:
            pool.wait_ge(self.experts.stored, (layer + 1) * 16 * Experts.PAIRS)
        need(pool, self.added, (layer - 1) * BATCH + b + 1)
        for i in range(BT):
            pool.indirect_dma_start(out=m["back"][:, b, i * D:(i + 1) * D], out_offset=None, in_=m["answers"],
                                    in_offset=bass.IndirectOffsetOnAxis(m["get"][:, b * BT + i:b * BT + i + 1], 0)).then_inc(self.got[b], 16)

    def add(self, dve, layer, b):
        m = self.m
        dve.wait_ge(self.got[b], (layer + 1) * 16 * BT)
        for i in range(BT):
            tile = b * BT + i
            last = dve.scalar_tensor_tensor(out=m["x"][:, tile * D:(tile + 1) * D], in0=m["back"][:, b, i * D:(i + 1) * D],
                                            scalar=m["weight"][:, tile:tile + 1], in1=m["x"][:, tile * D:(tile + 1) * D],
                                            op0=ALU.mult, op1=ALU.add)
        last.then_inc(self.added, 1)


class Conv:

    U0, Y, U2, OUT = 2, 2, 4, 4
    PAD = TAPS - 1

    def __init__(self, plan, ps, m, t, tr):
        self.plan, self.ps, self.m, self.t, self.tr = plan, ps, m, t, tr
        sb = plan.sb
        self.w_in, self.w_out = sb("c_w_in", [P, 2, D]), sb("c_w_out", [P, D])
        self.b_in, self.b_tap, self.w_tap = sb("c_b_in", [P, 3]), sb("c_b_tap", [P, 3]), sb("c_w_tap", [P, 2, TAPS])
        self.w1, self.w2, self.w3 = sb("c_w1", [TAPS, FW]), sb("c_w2", [FW, FW]), sb("c_w3", [FW, D])
        self.b1, self.b2, self.b_out = sb("c_b1", [FW, 1]), sb("c_b2", [FW, 1]), sb("c_b_out", [1, D])
        self.time0, self.ones_row, self.filt_bias = sb("time0", [TAPS, 1]), sb("ones_row", [1, P]), sb("filt_bias", [P, 1])
        self.col, self.row = sb("mlp_col", [FW, 2, 4]), sb("mlp_row", [1, 3, D])
        self.flipped, self.toep = sb("flipped", [P, 2 * P]), sb("toep", [P, 2 * P])
        self.xn, self.xt = sb("c_xn", [P, 2, SEQ]), sb("c_xt", [P, 2, SEQ])
        self.u = sb("c_u", [P, 2, 2, self.PAD + SEQ])
        self.s, self.v, self.vt, self.z = sb("c_s", [P, 2, 2, SEQ]), sb("c_v", [P, 2, SEQ]), sb("c_vt", [P, 2, SEQ]), sb("c_z", [P, 2, SEQ])
        self.weights_in, self.taps_out, self.taps_in = plan.dma_sem("c_weights_in"), plan.dma_sem("taps_out"), plan.dma_sem("taps_in")
        self.cleared, self.rstd, self.v_done = plan.sems("gpsimd", "c_cleared c_rstd c_v")
        self.mlp_psum, self.flip_psum, self.u_psum, self.y_psum, self.o_psum = plan.sems(
            "tensor", "c_mlp_psum c_flip_psum c_u_psum c_y_psum c_o_psum")
        self.mlp_exp, self.row_abs, self.toep_done, self.normal, self.u_done, self.s_first = plan.sems(
            "scalar", "c_mlp_exp c_row_abs c_toep c_normal c_u c_s_first")
        self.mlp, self.moments, self.s_done, self.y_read, self.z_done, self.x_done = plan.sems(
            "vector", "c_mlp c_moments c_s c_y_read c_z c_x")

    def load(self, sp):
        t, by_one = self.t, lambda a: a.rearrange("(f o) -> f o", o=1)
        loads = ((self.w_in[:, :, :], t["b_w_in"].rearrange("d (s e) -> d s e", s=3)[:, 0:3:2, :]), (self.b_in[:, :], t["b_b_in_t"]),
                 (self.w_tap[:, :, :], t["b_w_conv"].rearrange("(s e) o j -> e s (o j)", s=3)[:, 0:3:2, :]),
                 (self.b_tap[:, :], t["b_b_conv_t"]), (self.w1[:, :], t["b_w1"]), (self.w2[:, :], t["b_w2"]),
                 (self.w3[:, :], t["b_w3"]), (self.b1[:, :], by_one(t["b_b1"])), (self.b2[:, :], by_one(t["b_b2"])),
                 (self.filt_bias[:, :], by_one(t["b_filt_bias"])),
                 (self.row[:, 0, :], t["b_filt_bias"].rearrange("(o f) -> o f", o=1)),
                 (self.w_out[:, :], t["b_w_out"]), (self.b_out[:, :], t["b_b_out"].rearrange("(o f) -> o f", o=1)))
        self.n_weights = 16 * len(loads)
        for dst, src in loads:
            sp.dma_start(dst, src).then_inc(self.weights_in, 16)

    def filter_sync(self, sp):
        taps = self.m["taps"]
        sp.wait_ge(self.m["zeroed"], 16 * 5)
        need(sp, self.mlp, 5)
        sp.dma_start(taps[:, P - 1:2 * P - 1], self.row[:, 2, :]).then_inc(self.taps_out, 16)
        sp.wait_ge(self.taps_out, 16)
        shifted = bass.AP(tensor=taps.tensor, offset=taps.offset, ap=[[1, P], [1, 2 * P]])
        sp.dma_start(self.flipped[:, :], shifted).then_inc(self.taps_in, 16)

    def clear(self, pool):
        pool.memset(self.time0[:, :], 0.0)
        pool.memset(self.ones_row[:, :], 1.0)
        pool.memset(self.u[:, :, :, 0:self.PAD], 0.0).then_inc(self.cleared, 1)

    def filter_tensor(self, pe):
        at = lambda i: slice((2 + i) * HALF, (2 + i) * HALF + 1)
        pe.wait_ge(self.weights_in, self.n_weights)
        need(pe, self.cleared, 1)
        pe.matmul(self.ps[0:FW, at(0)], self.w1[:, :], self.time0[:, :], start=True, stop=True).then_inc(self.mlp_psum, 1)
        need(pe, self.mlp, 2)
        pe.matmul(self.ps[0:FW, at(1)], self.w2[:, :], self.col[:, 0, 3:4], start=True, stop=True).then_inc(self.mlp_psum, 1)
        need(pe, self.mlp, 4)
        pe.matmul(self.ps[0:1, 4 * HALF:4 * HALF + D], self.col[:, 1, 3:4], self.w3[:, :], start=True, stop=True).then_inc(self.mlp_psum, 1)

    def toeplitz_tensor(self, pe):
        pe.wait_ge(self.taps_in, 16)
        pe.matmul(self.ps[:, 5 * HALF:5 * HALF + 2 * P], self.m["const"][:, C_FLIP:C_FLIP + P], self.flipped[:, :], start=True,
                  stop=True).then_inc(self.flip_psum, 1)

    def filter_scalar(self, act):
        act.wait_ge(self.weights_in, self.n_weights)
        act.activation(self.row[:, 1, :], self.row[:, 0, :], ACT.Abs).then_inc(self.row_abs, 1)
        for layer in range(2):
            need(act, self.mlp, 2 * layer + 1)
            act.activation(self.col[:, layer, 1:2], self.col[:, layer, 0:1], ACT.Exp, scale=-1.0).then_inc(self.mlp_exp, 1)
        need(act, self.row_abs, 1)
        act.activation(self.row[:, 1, :], self.row[:, 1, :], ACT.Exp, scale=-0.0).then_inc(self.mlp_exp, 1)

    def toeplitz_scalar(self, act):
        need(act, self.flip_psum, 1)
        act.copy(self.toep[:, :], self.ps[:, 5 * HALF:5 * HALF + 2 * P]).then_inc(self.toep_done, 1)

    def filter_vector(self, dve):
        dve.wait_ge(self.weights_in, self.n_weights)
        for layer, bias in ((0, self.b1), (1, self.b2)):
            c = lambda i: self.col[:, layer, i:i + 1]
            need(dve, self.mlp_psum, layer + 1)
            dve.tensor_tensor(c(0), self.ps[0:FW, (2 + layer) * HALF:(2 + layer) * HALF + 1], bias[:, :], ALU.add).then_inc(self.mlp, 1)
            need(dve, self.mlp_exp, layer + 1)
            dve.tensor_scalar(c(1), c(1), 1.0, None, ALU.add)
            dve.drain()
            dve.reciprocal(c(2), c(1))
            dve.drain()
            dve.tensor_tensor(c(3), c(0), c(2), ALU.mult).then_inc(self.mlp, 1)
        need(dve, self.mlp_exp, 3)
        need(dve, self.mlp_psum, 3)
        dve.tensor_tensor(self.row[:, 2, :], self.ps[0:1, 4 * HALF:4 * HALF + D], self.row[:, 1, :], ALU.mult).then_inc(self.mlp, 1)

    def normalize(self, act, b):
        need(act, self.rstd, b + 1)
        need(act, self.tr.full, self.tr.at("c", b - 2))
        normalize(act, self.m, 1, b, self.xn[:, b % 2, :], self.normal)

    def transpose(self, pe, b):
        self.tr.transpose(pe, "c", b, self.xn[:, b % 2, :], self.normal, b * BT + 1)

    def copy(self, act, b):
        need(act, self.u_psum, 2 * b - 2)
        self.tr.copy(act, "c", b, self.xt[:, b % 2, :])

    def streams(self, pe, b):
        for s, at in enumerate((self.U0, self.U2)):
            if s == 0:
                need(pe, self.y_read, b - 1)
            else:
                need(pe, self.x_done, b - 2)
            for q in range(2):
                self.tr.need_copy(pe, "c", b, q)
                last = pe.matmul(bank(self.ps, at + q), self.w_in[:, s, :], self.xt[:, b % 2, q * HALF:(q + 1) * HALF],
                                 start=True, stop=True)
            last.then_inc(self.u_psum, 1)

    def first_tap(self, act, b):
        q = b % 2
        for s, at in enumerate((self.U0, self.U2)):
            need(act, self.u_psum, 2 * b + s + 1)
            need(act, self.s_done, 2 * b - 2 + s)
            act.activation(self.u[:, q, s, self.PAD:], bank(self.ps, at, 2), ACT.Identity,
                           bias=self.b_in[:, 2 * s:2 * s + 1]).then_inc(self.u_done, 1)
        for s in range(2):
            need(act, self.u_done, 2 * b + s + 1)
            need(act, self.z_done, b - 1)
            act.activation(self.s[:, q, s, :], self.u[:, q, s, 0:SEQ], ACT.Identity, scale=self.w_tap[:, s, 0:1],
                           bias=self.b_tap[:, 2 * s:2 * s + 1]).then_inc(self.s_first, 1)

    def taps(self, dve, b):
        q = b % 2
        for j in range(1, TAPS):
            for s in range(2):
                if j == 1:
                    need(dve, self.s_first, 2 * b + s + 1)
                last = dve.scalar_tensor_tensor(out=self.s[:, q, s, :], in0=self.u[:, q, s, j:j + SEQ],
                                                scalar=self.w_tap[:, s, j:j + 1], in1=self.s[:, q, s, :],
                                                op0=ALU.mult, op1=ALU.add)
                if j == TAPS - 1:
                    last.then_inc(self.s_done, 1)
            if j < TAPS - 1:
                dve.drain()

    def product(self, pool, b):
        q = b % 2
        need(pool, self.s_done, 2 * b + 2)
        need(pool, self.y_read, b - 1)
        pool.tensor_tensor(self.v[:, q, :], self.s[:, q, 1, :], self.s[:, q, 0, :], ALU.mult).then_inc(self.v_done, 1)

    def v_transpose(self, pe, b):
        self.tr.transpose(pe, "v", b, self.v[:, b % 2, :], self.v_done, b + 1)

    def v_copy(self, act, b):
        need(act, self.y_psum, b - 1)
        self.tr.copy(act, "v", b, self.vt[:, b % 2, :])

    def long_conv(self, pe, b):
        need(pe, self.toep_done, 1)
        need(pe, self.u_done, min(2 * b + 3, 2 * BATCH - 1))
        need(pe, self.y_read, b)
        for i in range(BT):
            self.tr.need_copy(pe, "v", b, i // HT)
            for j in (i - 1, i):
                if j >= 0:
                    last = pe.matmul(self.ps[:, self.Y * HALF + i * P:self.Y * HALF + (i + 1) * P],
                                     self.vt[:, b % 2, j * D:(j + 1) * D], self.toep[:, (i - j) * P:(i - j + 1) * P],
                                     start=i % HT == 0 and j == max(i - 1, 0), stop=i % HT == HT - 1 and j == i)
        last.then_inc(self.y_psum, 1)

    def gate_y(self, dve, b):
        q = b % 2
        need(dve, self.y_psum, b + 1)
        need(dve, self.o_psum, b - 1)
        need(dve, self.v_done, b + 1)
        dve.scalar_tensor_tensor(out=self.z[:, q, :], in0=self.v[:, q, :], scalar=self.filt_bias[:, 0:1],
                                 in1=bank(self.ps, self.Y, 2), op0=ALU.mult, op1=ALU.add).then_inc(self.y_read, 1)
        dve.drain()
        dve.tensor_tensor(self.z[:, q, :], self.z[:, q, :], self.s[:, q, 0, :], ALU.mult).then_inc(self.z_done, 1)

    def output(self, pe, b):
        need(pe, self.z_done, b + 1)
        need(pe, self.u_done, min(2 * (b + 2) + 2, 2 * BATCH))
        need(pe, self.x_done, b)
        for q in range(2):
            pe.matmul(bank(self.ps, self.OUT + q), self.ones_row[:, :],
                      self.b_out[:, :].rearrange("p (o d) -> p o d", o=1).broadcast_to([1, HT, D]), start=True, stop=False)
        for i in range(BT):
            last = pe.matmul(self.ps[:, self.OUT * HALF + i * D:self.OUT * HALF + (i + 1) * D], self.z[:, b % 2, i * P:(i + 1) * P],
                             self.w_out[:, :], start=False, stop=i % HT == HT - 1)
        last.then_inc(self.o_psum, 1)

    def add(self, dve, b):
        x = self.m["x"][:, b * SEQ:(b + 1) * SEQ]
        need(dve, self.o_psum, b + 1)
        dve.tensor_tensor(x, x, bank(self.ps, self.OUT, 2), ALU.add).then_inc(self.x_done, 1)
        dve.drain()


def row_steps(*steps):
    for k in range(BATCH + max(lag for _, lag in steps)):
        for step_of, lag in steps:
            if 0 <= k - lag < BATCH:
                step_of(k - lag)


def mixtures_and_conv(plan, ps, m, t):
    late_memory(plan, m, t)
    order = [("r", b) for b in range(BATCH)]
    row_steps((lambda b: order.append(("c", b)), 1), (lambda b: order.append(("v", b)), 2),
              (lambda b: order.append(("r", BATCH + b)), 3))
    tr = Transposer(plan, ps, m, order)
    router = Router(plan, ps, m, tr)
    experts = Experts(plan, ps, m, t, router)
    answers = Answers(plan, m, experts)
    router.fetched = answers.got
    conv = Conv(plan, ps, m, t, tr)
    r_pow, c_pow = plan.sems("gpsimd", "r_pow c_pow")
    out_done = plan.dma_sem("out_done")
    second = lambda b: BATCH + b

    @plan.on("sync")
    def _(sp):
        conv.load(sp)
        conv.filter_sync(sp)
        experts.sync(sp, 0)
        experts.sync(sp, 1)
        for b in range(BATCH):
            need(sp, answers.added, BATCH + b + 1)
            sp.dma_start(t["out"][b:b + 1, :, :].rearrange("b (i p) d -> p (b i) d", p=P),
                         m["x"][:, b * SEQ:(b + 1) * SEQ].rearrange("p (i d) -> p i d", d=D)).then_inc(out_done, 16)
        sp.wait_ge(out_done, 16 * BATCH)

    @plan.on("tensor")
    def _(pe):
        pe.wait_ge(m["router_in"], 16 * 4)
        row_steps((lambda b: router.transpose(pe, b), 0), (lambda b: router.count(pe, b), 1), (lambda b: router.logits(pe, b), 0))
        conv.filter_tensor(pe)
        conv.toeplitz_tensor(pe)
        experts.tensor(pe, 0)
        row_steps((lambda b: conv.transpose(pe, b), 1), (lambda b: conv.streams(pe, b), 1),
                  (lambda b: conv.output(pe, b), 3), (lambda b: router.count(pe, second(b)), 4),
                  (lambda b: conv.v_transpose(pe, b), 2), (lambda b: conv.long_conv(pe, b), 2),
                  (lambda b: router.transpose(pe, second(b)), 3), (lambda b: router.logits(pe, second(b)), 3))
        experts.tensor(pe, 1)

    @plan.on("scalar")
    def _(act):
        row_steps((lambda b: router.normalize(act, b), 0), (lambda b: router.probabilities(act, b), 1),
                  (lambda b: router.copy(act, b), 0), (lambda b: router.gate_rows(act, b), 1))
        conv.filter_scalar(act)
        conv.toeplitz_scalar(act)
        experts.scalar(act, 0)
        row_steps((lambda b: conv.normalize(act, b), 1), (lambda b: conv.copy(act, b), 1),
                  (lambda b: router.probabilities(act, second(b)), 4), (lambda b: conv.first_tap(act, b), 1),
                  (lambda b: conv.v_copy(act, b), 2), (lambda b: router.gate_rows(act, second(b)), 4),
                  (lambda b: router.normalize(act, second(b)), 3), (lambda b: router.copy(act, second(b)), 3))
        experts.scalar(act, 1)

    @plan.on("vector")
    def _(dve):
        dve.memset(m["prior"][:, :, :], 0.0)
        dve.wait_ge(m["router_in"], 16 * 4)
        row_steps((lambda b: router.choose(dve, b), 1), (lambda b: router.place(dve, b), 1))
        need(dve, router.count_psum, BATCH)
        dve.memset(m["prior"][:, 0, :], 0.0)
        conv.filter_vector(dve)
        experts.vector(dve, 0)

        def fetched(b):
            answers.add(dve, 0, b)
            dve.drain()
            statistics(dve, m, 1, b).then_inc(conv.moments, 1)

        def convolved(b):
            conv.add(dve, b)
            statistics(dve, m, 2, b).then_inc(router.moments, 1)

        row_steps((lambda b: conv.gate_y(dve, b), 3), (lambda b: router.choose(dve, second(b)), 4),
                  (lambda b: conv.taps(dve, b), 2), (convolved, 3), (lambda b: router.place(dve, second(b)), 4), (fetched, 0))
        experts.vector(dve, 1)
        for b in range(BATCH):
            answers.add(dve, 1, b)

    @plan.on("gpsimd")
    def _(pool):
        deviations(pool, m, 0, 0, BATCH, r_pow, 1).then_inc(router.rstd, 1)
        conv.clear(pool)
        for b in range(BATCH):
            router.scatter(pool, b)

        def conv_rstd(b):
            need(pool, conv.moments, b + 1)
            deviations(pool, m, 1, b, 1, c_pow, b + 1).then_inc(conv.rstd, 1)

        def router_rstd(b):
            need(pool, router.moments, b + 1)
            deviations(pool, m, 2, b, 1, r_pow, b + 2).then_inc(router.rstd, 1)

        answers.fetch(pool, 0, 0)
        row_steps((lambda b: answers.fetch(pool, 0, b + 1) if b + 1 < BATCH else None, 0), (conv_rstd, 0),
                  (lambda b: conv.product(pool, b), 2), (router_rstd, 3), (lambda b: router.scatter(pool, second(b)), 4))
        for b in range(BATCH):
            answers.fetch(pool, 1, b)


def kernel(**inputs):
    import concourse.bacc as bacc
    from concourse.bass_utils import run_bass_kernel_spmd as run

    nc = bacc.Bacc("TRN2", target_bir_lowering=False, num_devices=1)
    a = {n.removeprefix("L0_").replace("attn_a_", "a_").replace("attn_b_", "b_").replace("ffn_", "f_"): np.asarray(v)
         for n, v in inputs.items()}
    a["x"] = a.pop("a_x")
    a["a_A_log_p"] = a["a_A_log"].reshape(GROUPS, GROUP, STATES).transpose(2, 1, 0).reshape(P, GROUPS)
    a["f_b1_t"] = a.pop("f_b1").T
    a["b_b_in_t"] = a.pop("b_b_in").reshape(3, D).T
    a["b_b_conv_t"] = a.pop("b_b_conv").reshape(3, D).T
    a["table"] = constant_table()
    arrays, t = {}, {}
    for n, v in a.items():
        v = np.ascontiguousarray(v)
        arrays["in_" + n] = v
        t[n] = nc.dram_tensor("in_" + n, v.shape, mybir.dt.from_np(v.dtype), kind="ExternalInput").ap()
    t["out"] = nc.dram_tensor("out", (BATCH, SEQ, D), F32, kind="ExternalOutput").ap()
    build(nc, t)
    return run(nc, [arrays], core_ids=[0]).results[0]["out"]
```

```python
from contextlib import ExitStack

import numpy as np

import concourse.bass as bass
from concourse import mybir

F32 = mybir.dt.float32
BF16 = mybir.dt.bfloat16
I32 = mybir.dt.int32
ALU = mybir.AluOpType
ACT = mybir.ActivationFunctionType
AX = mybir.AxisListType.X

P = 128
BATCH, SEQ, D = 4, 1024, 128
TOKENS = BATCH * SEQ
TILES = TOKENS // P
BT = SEQ // P
HALF = SEQ // 2
HT = HALF // P
STATES = 16
RANK = 64
GROUP = P // STATES
GROUPS = D // GROUP
PARTS = 3
QUARTER = 32
QG = QUARTER // GROUP
EXPERTS = 8
CAP = TOKENS // EXPERTS
TAPS = 3
FW = 64
DT_MIN, DT_MAX = 0.001, 0.1
EPS = 1e-5
WIDE = D + 1
PREPARED = 16 * (3 * BATCH + 3)

C_ID, C_FLIP, C_TRI = 0, P, 2 * P
C_SEL = 3 * P
C_RED = C_SEL + QG * P
C_RANK = C_RED + QG * QUARTER
C_TOKEN = C_RANK + EXPERTS
C_SLOT = C_TOKEN + TILES
C_END = C_SLOT + TILES


def constant_table():
    t = np.zeros((P, C_END), np.float32)
    r = np.arange(P)
    t[r, C_ID + r] = 1.0
    t[r, C_FLIP + P - 1 - r] = 1.0
    t[:, C_TRI:C_TRI + P] = r[:, None] <= r[None, :]
    for s in range(QG):
        for part in range(PARTS):
            for p in range(P):
                t[part * QUARTER + s * GROUP + p % GROUP, C_SEL + s * P + p] = 1.0
    for s in range(QG):
        t[r, C_RED + s * QUARTER + s * GROUP + r % GROUP] = 1.0
    t[:, C_RANK:C_RANK + EXPERTS] = EXPERTS - np.arange(EXPERTS)
    t[:, C_TOKEN:C_TOKEN + TILES] = TOKENS + np.arange(TILES)[None, :] * P + r[:, None]
    t[:, C_SLOT:C_SLOT + TILES] = np.arange(TILES)[None, :] * P + r[:, None]
    return t


CREDIT = 2 * GROUPS


class Plan:

    ENGINES = ("sync", "tensor", "vector", "scalar", "gpsimd")

    def __init__(self, nc, ctx, memory, tag=""):
        self.nc, self.ctx, self.memory = nc, ctx, memory
        self.stages = {e: [] for e in self.ENGINES}
        self.owned = {e: [] for e in self.ENGINES}
        self.passed = {e: self.dma_sem("passed_" + e + tag) for e in ("sync", "gpsimd")}

    def sb(self, name, shape, dt=F32):
        return self.memory.enter_context(self.nc.sbuf_tensor(name, shape, dt))

    def dma_sem(self, name):
        return self.ctx.enter_context(self.nc.semaphore(name))

    def sem(self, owner, name):
        s = self.dma_sem(name)
        self.owned[owner].append(s)
        return s

    def sems(self, owner, names):
        return [self.sem(owner, n) for n in names.split()]

    def on(self, engine):
        return self.stages[engine].append

    def run(self):
        with self.nc.Block() as block:
            for name in self.ENGINES:
                def program(eng, name=name):
                    for s in self.owned[name]:
                        eng.sem_inc(s, CREDIT)
                    for stage in self.stages[name]:
                        stage(eng)
                {"sync": block.sync, "tensor": block.tensor, "vector": block.vector, "scalar": block.scalar,
                 "gpsimd": block.gpsimd}[name](program)


def need(eng, sem, count):
    eng.wait_ge(sem, count + CREDIT)


def alone(plan, eng, name):
    eng.sem_inc(plan.passed[name], 1)


def bank(ps, i, n=1):
    return ps[:, i * HALF:(i + n) * HALF]


def build(nc, t):
    with ExitStack() as ctx:
        ps = ctx.enter_context(nc.psum_tensor("ps", [P, 8 * HALF], F32))
        plan = Plan(nc, ctx, ctx)
        m = {"x": plan.sb("x", [P, TOKENS]),
             "const": plan.sb("const", [P, C_END]),
             "tri": plan.sb("tri", [P, P], BF16), "ones": plan.sb("ones", [P, P], BF16),
             "neg_half": plan.sb("neg_half", [P, TILES]),
             "w_r": plan.sb("w_r", [P, EXPERTS]), "b_r": plan.sb("b_r", [P, EXPERTS]),
             "stats": plan.sb("stats", [P, BT, 6]), "moments": plan.sb("moments", [P, BT, 2]),
             "spread": plan.sb("spread", [P, 3, TILES]), "neg_mean": plan.sb("neg_mean", [P, 3, TILES]),
             "rstd": plan.sb("rstd", [P, 3, TILES]), "shift": plan.sb("shift", [P, 3, TILES]),
             "slots": [nc.dram_tensor(f"slots{i}", (2 * TOKENS, WIDE), F32).ap() for i in range(2)],
             "answers": nc.dram_tensor("answers", (2 * TOKENS, D), F32).ap(),
             "steps": nc.dram_tensor("steps", (P, BATCH * PARTS * SEQ), BF16).ap(),
             "taps": nc.dram_tensor("taps", (1, 4 * P), F32).ap()}
        with ExitStack() as early:
            plan.memory = early
            m["prepared"] = plan.dma_sem("prepared")
            m["skip"], m["skip_in"] = plan.sb("skip", [P, 1]), plan.dma_sem("skip_in")
            project(plan, ps, m, t)
            scan(plan, ps, m, t)
            plan.run()
        plan2 = Plan(nc, ctx, ctx, "2")
        mixtures_and_conv(plan2, ps, m, t)
        plan2.run()


def project(plan, ps, m, t):
    x, const = m["x"], m["const"]
    sb = plan.sb
    ident = const[:, C_ID:C_ID + P]
    m["states"] = states = sb("states", [P, GROUPS * SEQ])
    exp_z, sp_all = states[:, GROUPS * SEQ - 2 * TOKENS:GROUPS * SEQ - TOKENS], states[:, GROUPS * SEQ - TOKENS:]
    m["inp"], m["c_rows"], m["u"] = inp, c_rows, u = sb("inp", [P, TOKENS]), sb("c_rows", [P, TOKENS]), sb("u", [P, TOKENS])
    zero = sb("zero", [P, BT * WIDE])
    w_in, w_x, w_dt, b_dt = sb("w_in", [P, D]), sb("w_x", [P, RANK + 2 * STATES]), sb("w_dt", [RANK, D]), sb("b_dt", [P, 1])
    w_in_t = sb("w_in_t", [P, D])
    w_low = sb("w_low", [RANK, D])
    w_z = sb("w_z", [P, D])
    w_b, w_c = sb("w_b", [P, P]), sb("w_c", [P, P])
    stats, moments = sb("in_stats", [P, 2, HT, 6]), sb("in_moments", [P, 2, HT, 2])
    spread, rstd = sb("in_spread", [P, 2, HT]), sb("in_rstd", [P, 2, HT])
    m["scratch"] = scratch = sb("scratch", [P, 2 * SEQ])
    xn, xn_t = (scratch[:, i * SEQ:(i + 1) * SEQ].rearrange("p (q s) -> p q s", q=2) for i in range(2))
    a_neg = sb("a_neg", [P, STATES])
    a_range = sb("a_range", [P, P])
    a_p = sb("a_p", [P, GROUPS])
    m["scale_p"], m["bias_p"] = scale_p, bias_p = sb("scale_p", [P, GROUPS]), sb("bias_p", [P, GROUPS])
    m["sel"], m["red"] = sb("sel", [P, QG * P], BF16), sb("red", [P, QG * QUARTER])
    part, rest = sb("part", [P, PARTS * SEQ], BF16), sb("rest", [P, SEQ])
    dtu = sb("dtu", [P, SEQ])
    m["stack"] = stack = sb("stack", [PARTS * QUARTER, QUARTER // GROUP, TOKENS], BF16)

    x_in = [plan.dma_sem(f"x_in{b}") for b in range(BATCH)]
    weights_in, ident_in, consts_in, a_in = (plan.dma_sem(n) for n in ("weights_in", "ident_in", "consts_in", "a_in"))
    steps_out = plan.dma_sem("steps_out")
    m["stacked"] = stacked = [plan.dma_sem(f"stacked{b}") for b in range(BATCH)]
    zero_made, half_made, rstd_done, rest_done = plan.sems("gpsimd", "zero_made half_made rstd_done rest_done")
    moments_done, xn_ready, z_taken, a_made, sp_done, dtu_done, lo_done, inp_done = plan.sems(
        "vector", "moments_done xn_ready z_taken a_made sp_done dtu_done lo_done inp_done")
    fold_psum, xt_psum, z_psum, u_psum, b_psum, c_psum, q_psum = plan.sems(
        "tensor", "fold_psum xt_psum z_psum u_psum b_psum c_psum q_psum")
    fold_done, xt_ready, abs_done, u_taken, b_taken, c_taken, a_exp, ln_done, hi_done, mid_done = plan.sems(
        "scalar", "fold_done xt_ready abs_done u_taken b_taken c_taken a_exp ln_done hi_done mid_done")
    parts_free = plan.sem("sync", "parts_free")
    m["late"] = late = {}

    @plan.on("sync")
    def _(sp):
        for b in range(BATCH):
            sp.dma_start(x[:, b * SEQ:(b + 1) * SEQ].rearrange("p (i d) -> p i d", d=D),
                         t["x"][b:b + 1, :, :].rearrange("b (i p) d -> p (b i) d", p=P)).then_inc(x_in[b], 16)
        sp.dma_start(a_neg[:, :], t["a_A_log"]).then_inc(a_in, 16)
        sp.dma_start(a_p[:, :], t["a_A_log_p"]).then_inc(a_in, 16)
        sp.dma_start(m["skip"][:, :], t["a_Dp"].rearrange("(d o) -> d o", o=1)).then_inc(m["skip_in"], 16)
        sp.dma_start(m["w_r"][:, :], t["f_Wr"]).then_inc(m["prepared"], 16)
        sp.dma_start(m["b_r"][:, :], t["f_br"].rearrange("(o e) -> o e", o=1).broadcast_to([P, EXPERTS])).then_inc(m["prepared"], 16)
        need(sp, zero_made, 1)

        def clear(dst, b):
            wide = dst.shape[1]
            sp.dma_start(dst[b * SEQ:(b + 1) * SEQ, :].rearrange("(p j) d -> p (j d)", p=P),
                         zero[:, 0:BT * wide]).then_inc(m["prepared"], 16)

        sp.dma_start(m["taps"][:, :], zero[0:1, 0:4 * P]).then_inc(m["prepared"], 16)
        for b in range(BATCH):
            need(sp, lo_done, b + 1)
            sp.dma_start(m["steps"][:, b * PARTS * SEQ:(b + 1) * PARTS * SEQ], part[:, :]).then_inc(steps_out, 16)
            sp.wait_ge(steps_out, b * 16 + 16)
            sp.sem_inc(parts_free, 1)
            for a in range(PARTS):
                sp.dma_start(stack[a * QUARTER:(a + 1) * QUARTER, :, b * SEQ:(b + 1) * SEQ],
                             m["steps"][:, (b * PARTS + a) * SEQ:(b * PARTS + a + 1) * SEQ].rearrange(
                                 "(q r) s -> r q s", r=QUARTER)).then_inc(stacked[b], 16)
        for dst in m["slots"] + [m["answers"][TOKENS:, :]]:
            for b in range(BATCH):
                clear(dst, b)
        sp.wait_ge(m["prepared"], PREPARED)

    @plan.on("gpsimd")
    def _(pool):
        pool.memset(m["neg_half"][:, :], -0.5).then_inc(half_made, 1)
        pool.memset(m["ones"][:, :], 1.0)
        pool.memset(zero[:, :], 0.0).then_inc(zero_made, 1)
        need(pool, half_made, 1)

        def remainder(b):
            need(pool, hi_done, b + 1)
            need(pool, lo_done, b)
            alone(plan, pool, "gpsimd")
            pool.tensor_tensor(rest[:, :], sp_all[:, bass.ds(b * SEQ, SEQ)], part[:, 0:SEQ], ALU.subtract).then_inc(rest_done, 1)

        def deviation(b):
            for q in range(2):
                need(pool, moments_done, b * 2 + (q + 1))
                pool.tensor_tensor(rstd[:, q, :], spread[:, q, :], m["neg_half"][:, 0:HT], ALU.pow).then_inc(rstd_done, 1)

        deviation(0)
        deviation(1)
        with pool.Fori(1, BATCH - 1) as b:
            for q in range(2):
                need(pool, moments_done, b * 2 + (q + 3))
                pool.tensor_tensor(rstd[:, q, :], spread[:, q, :], m["neg_half"][:, 0:HT], ALU.pow).then_inc(rstd_done, 1)
            remainder(b - 1)
        remainder(BATCH - 2)
        remainder(BATCH - 1)

    @plan.on("scalar")
    def _(act):
        act.dma_start(w_in[:, :], t["a_w_in"]).then_inc(weights_in, 16)
        act.dma_start(const[:, 0:P], t["table"][:, 0:P]).then_inc(ident_in, 16)
        act.dma_start(w_x[:, :], t["a_w_x"]).then_inc(weights_in, 16)
        act.dma_start(w_dt[:, :], t["a_w_dt"]).then_inc(weights_in, 16)
        act.dma_start(b_dt[:, :], t["a_b_dt"].rearrange("(d o) -> d o", o=1)).then_inc(weights_in, 16)
        act.dma_start(const[:, P:], t["table"][:, P:]).then_inc(consts_in, 16)
        need(act, fold_psum, 1)
        act.copy(w_in_t[:, :], ps[:, 0:D]).then_inc(fold_done, 1)
        need(act, fold_psum, 2)
        act.copy(w_low[:, :], ps[0:RANK, HALF:HALF + D])
        act.copy(w_b[:, :], ps[:, 2 * HALF:2 * HALF + P])
        act.copy(w_c[:, :], ps[:, 3 * HALF:3 * HALF + P]).then_inc(fold_done, 1)
        need(act, fold_psum, 3)
        act.copy(w_z[:, :], ps[:, 4 * HALF:4 * HALF + D]).then_inc(fold_done, 1)

        def logarithm(b):
            act.drain()
            cols = bass.ds(b * SEQ, SEQ)
            act.activation(exp_z[:, cols], exp_z[:, cols], ACT.Ln, bias=1.0).then_inc(ln_done, 1)

        def first_part(b):
            need(act, sp_done, b + 1)
            need(act, parts_free, b)
            act.copy(part[:, 0:SEQ], sp_all[:, bass.ds(b * SEQ, SEQ)]).then_inc(hi_done, 1)

        def second_part(b):
            need(act, rest_done, b + 1)
            act.copy(part[:, SEQ:2 * SEQ], rest[:, :]).then_inc(mid_done, 1)

        def tokens(b):
            for q in range(2):
                need(act, xt_psum, b * 2 + (q + 1))
                need(act, c_psum, b * 2 + q - 1)
                act.copy(xn_t[:, q, :], bank(ps, q)).then_inc(xt_ready, 1)

        def projections(b, q):
            cols = bass.ds(b * SEQ + q * HALF, HALF)
            need(act, z_psum, b * 2 + (q + 1))
            act.activation(exp_z[:, cols], bank(ps, 2), ACT.Abs, bias=b_dt[:, 0:1]).then_inc(abs_done, 1)
            need(act, u_psum, b * 2 + (q + 1))
            act.copy(u[:, cols], bank(ps, 3)).then_inc(u_taken, 1)
            need(act, b_psum, b * 2 + (q + 1))
            act.copy(inp[:, cols], bank(ps, 4)).then_inc(b_taken, 1)
            need(act, c_psum, b * 2 + (q + 1))
            act.copy(c_rows[:, cols], bank(ps, 5)).then_inc(c_taken, 1)

        def exponential(b):
            cols = bass.ds(b * SEQ, SEQ)
            act.drain()
            act.activation(exp_z[:, cols], exp_z[:, cols], ACT.Exp, scale=-1.0)

        tokens(0)
        projections(0, 0)
        projections(0, 1)
        tokens(1)
        act.wait_ge(a_in, 32)
        act.activation(a_neg[:, :], a_neg[:, :], ACT.Exp)
        act.activation(a_p[:, :], a_p[:, :], ACT.Exp).then_inc(a_exp, 1)
        exponential(0)
        logarithm(0)
        projections(1, 0)
        with act.Fori(1, BATCH - 1) as b:
            projections(b, 1)
            first_part(b - 1)
            tokens(b + 1)
            exponential(b)
            projections(b + 1, 0)
            second_part(b - 1)
            logarithm(b)
        projections(BATCH - 1, 1)
        first_part(BATCH - 2)
        exponential(BATCH - 1)
        second_part(BATCH - 2)
        logarithm(BATCH - 1)
        late["scalar"] = {1: lambda: first_part(BATCH - 1), 3: lambda: second_part(BATCH - 1)}

    @plan.on("vector")
    def _(dve):
        def statistics_of(b, q):
            for i in range(HT):
                dve.bn_stats(stats[:, q, i, :], x[:, bass.ds(b * SEQ + (q * HT + i) * D, D)])
            dve.drain()
            for i in range(HT):
                dve.bn_aggr(moments[:, q, i, :], stats[:, q, i, :])
            dve.drain()
            dve.tensor_scalar(spread[:, q, :], moments[:, q, :, 1], EPS, None, ALU.add).then_inc(moments_done, 1)

        def normalize(b, q):
            need(dve, rstd_done, b * 2 + (q + 1))
            need(dve, xt_psum, b * 2 + q - 1)
            for i in range(HT):
                last = dve.tensor_scalar(xn[:, q, i * D:(i + 1) * D], x[:, bass.ds(b * SEQ + (q * HT + i) * D, D)],
                                         moments[:, q, i, 0:1], rstd[:, q, i:i + 1], ALU.subtract, ALU.mult)
            last.then_inc(xn_ready, 1)

        def positive(b, q):
            need(dve, abs_done, b * 2 + (q + 1))
            dve.tensor_scalar(sp_all[:, bass.ds(b * SEQ + q * HALF, HALF)], bank(ps, 2), b_dt[:, 0:1], 0.0,
                              ALU.add, ALU.max).then_inc(z_taken, 1)

        def softplus(b):
            cols = bass.ds(b * SEQ, SEQ)
            dve.drain()
            need(dve, ln_done, b + 1)
            dve.tensor_tensor(sp_all[:, cols], sp_all[:, cols], exp_z[:, cols], ALU.add).then_inc(sp_done, 1)

        def step_times_u(b):
            cols = bass.ds(b * SEQ, SEQ)
            dve.drain()
            need(dve, q_psum, b)
            need(dve, u_taken, b * 2 + 2)
            dve.scalar_tensor_tensor(out=dtu[:, :], in0=sp_all[:, cols], scalar=DT_MIN / (DT_MAX - DT_MIN), in1=u[:, cols],
                                     op0=ALU.add, op1=ALU.mult).then_inc(dtu_done, 1)

        def third_part(b):
            need(dve, mid_done, b + 1)
            dve.tensor_tensor(part[:, 2 * SEQ:], rest[:, :], part[:, SEQ:2 * SEQ], ALU.subtract).then_inc(lo_done, 1)

        def input_rows(b):
            cols = bass.ds(b * SEQ, SEQ)
            need(dve, q_psum, b + 1)
            dve.tensor_tensor(inp[:, cols], inp[:, cols], bank(ps, 6, 2), ALU.mult).then_inc(inp_done, 1)

        dve.wait_ge(x_in[0], 16)
        for q in range(2):
            statistics_of(0, q)
        for q in range(2):
            normalize(0, q)
        dve.wait_ge(consts_in, 16)
        dve.tensor_copy(m["tri"][:, :], const[:, C_TRI:C_TRI + P])
        dve.tensor_copy(m["sel"][:, :], const[:, C_SEL:C_SEL + QG * P])
        dve.tensor_copy(m["red"][:, :], const[:, C_RED:C_RED + QG * QUARTER])
        dve.wait_ge(x_in[1], 16)
        dve.wait_ge(weights_in, 16 * 4)
        for q in range(2):
            statistics_of(1, q)
            positive(0, q)
            normalize(1, q)
        positive(1, 0)
        need(dve, a_exp, 1)
        dve.tensor_scalar(a_neg[:, :], a_neg[:, :], -1.0, None, ALU.mult)
        dve.tensor_scalar(scale_p[:, :], a_p[:, :], -(DT_MAX - DT_MIN), None, ALU.mult)
        dve.tensor_scalar(bias_p[:, :], a_p[:, :], -DT_MIN, None, ALU.mult)
        dve.drain()
        rep = a_neg[:, :].rearrange("p (n o) -> p n o", o=1).broadcast_to([P, STATES, GROUP])
        dve.tensor_scalar(a_range[:, :].rearrange("p (n j) -> p n j", j=GROUP), rep, DT_MAX - DT_MIN, None,
                          ALU.mult).then_inc(a_made, 1)
        for b in range(BATCH):
            if b > 0:
                positive(b, 1)
            if b + 2 < BATCH:
                dve.wait_ge(x_in[b + 2], 16)
                statistics_of(b + 2, 0)
                statistics_of(b + 2, 1)
            if 0 < b < BATCH - 1:
                positive(b + 1, 0)
            if b + 2 < BATCH:
                normalize(b + 2, 0)
                normalize(b + 2, 1)
            if b > 0:
                third_part(b - 1)
                input_rows(b - 1)
            softplus(b)
            step_times_u(b)
        late["vector"] = {3: lambda: third_part(BATCH - 1), 4: lambda: input_rows(BATCH - 1)}

    @plan.on("tensor")
    def _(pe):
        pe.wait_ge(ident_in, 16)
        pe.wait_ge(weights_in, 16 * 4)
        pe.transpose(ps[:, 0:D], w_in[:, :], ident).then_inc(fold_psum, 1)
        need(pe, fold_done, 1)
        rep = lambda a: a.rearrange("p (n o) -> p n o", o=1).broadcast_to([P, STATES, GROUP])
        pe.matmul(ps[0:RANK, HALF:HALF + D], w_x[:, 0:RANK], w_in_t[:, :], start=True, stop=True)
        pe.matmul(ps[:, 2 * HALF:2 * HALF + P], w_in_t[:, :], rep(w_x[:, RANK:RANK + STATES]), start=True, stop=True)
        pe.matmul(ps[:, 3 * HALF:3 * HALF + P], w_in_t[:, :], rep(w_x[:, RANK + STATES:]), start=True,
                  stop=True).then_inc(fold_psum, 1)
        need(pe, fold_done, 2)
        pe.matmul(ps[:, 4 * HALF:4 * HALF + D], w_low[:, :], w_dt[:, :], start=True, stop=True).then_inc(fold_psum, 1)
        need(pe, fold_done, 3)

        def transpose(b, q):
            need(pe, xn_ready, b * 2 + (q + 1))
            need(pe, xt_ready, b * 2 + q - 1)
            for i in range(HT):
                last = pe.transpose(ps[:, q * HALF + i * P:q * HALF + (i + 1) * P], xn[:, q, i * D:(i + 1) * D], ident)
            last.then_inc(xt_psum, 1)

        def products(b, q):
            need(pe, xt_ready, b * 2 + (q + 1))
            for w, at, full, taken in ((w_z, 2, z_psum, z_taken), (w_in, 3, u_psum, u_taken),
                                       (w_b, 4, b_psum, b_taken), (w_c, 5, c_psum, c_taken)):
                need(pe, taken, b * 2 + q)
                pe.matmul(bank(ps, at), w[:, :], xn_t[:, q, :], start=True, stop=True).then_inc(full, 1)

        def step_products(b):
            need(pe, dtu_done, b + 1)
            need(pe, inp_done, b)
            for q in range(2):
                last = pe.matmul(bank(ps, 6 + q), a_range[:, :], dtu[:, q * HALF:(q + 1) * HALF], start=True, stop=True)
            last.then_inc(q_psum, 1)

        for q in range(2):
            transpose(0, q)
        for q in range(2):
            products(0, q)
        for q in range(2):
            transpose(1, q)
        with pe.Fori(1, BATCH - 1) as b:
            for q in range(2):
                products(b, q)
            for q in range(2):
                transpose(b + 1, q)
            step_products(b - 1)
        for q in range(2):
            products(BATCH - 1, q)
        step_products(BATCH - 2)
        need(pe, c_taken, 2 * BATCH)
        need(pe, z_taken, 2 * BATCH)
        late["tensor"] = {3: lambda: step_products(BATCH - 1)}


ON_DVE = (1, 3, 6, 12, 14)
SLOTS = [u % 3 for u in range(GROUPS - 1)] + [1]
QUARTERS = D // QUARTER
LAG = 7
LAST_SUM = (GROUPS - 1 + LAG) % GROUPS
AHEAD = 1


def before(u, same):
    j = u - 1
    while not same(j % GROUPS):
        j -= 1
    return j


def upto(u, on_dve):
    mine = [v for v in range(GROUPS) if (v in ON_DVE) == on_dve]
    return (u // GROUPS) * len(mine) + sum(1 for v in mine if v <= u % GROUPS)


def scan(plan, ps, m, t):
    x, const, u_all = m["x"], m["const"], m["u"]
    inp, c_rows, sel, red, stack = m["inp"], m["c_rows"], m["sel"], m["red"], m["stack"]
    ident = const[:, C_ID:C_ID + P]
    h = m["states"]
    y_t = m["scratch"][:, 0:SEQ]
    skip, skip_in = m["skip"], m["skip_in"]
    warm = plan.sb("warm", [P, 1])
    dt_psum, summed, y_psum = plan.sems("tensor", "dt_psum summed y_psum")
    decay_ready = plan.sem("scalar", "decay_ready")
    scanned, prod_dve, y_taken, x_added, row_moments = plan.sems("vector", "scanned prod_dve y_taken x_added row_moments")
    prod_pool, row_pow = plan.sems("gpsimd", "prod_pool row_pow")
    n_dve, n_pool = len(ON_DVE), GROUPS - len(ON_DVE)
    group = lambda u: QG * (u % QUARTERS) + u // QUARTERS
    slot = lambda u: bank(ps, 2 * SLOTS[u], 2)

    def need_products(eng, b, u):
        need(eng, prod_dve, b * n_dve + upto(u, True))
        need(eng, prod_pool, b * n_pool + upto(u, False))

    @plan.on("tensor")
    def _(pe):
        def broadcast(b, u):
            need(pe, scanned, b * GROUPS + before(u, lambda v: SLOTS[v] == SLOTS[u]) + 1)
            g = group(u)
            for q in range(2):
                last = pe.matmul(bank(ps, 2 * SLOTS[u] + q), sel[0:PARTS * QUARTER, (g % QG) * P:(g % QG + 1) * P],
                                 stack[:, g // QG, bass.ds(b * SEQ + q * HALF, HALF)], start=True, stop=True)
            last.then_inc(dt_psum, 1)

        def state_sum(b, r, q):
            need_products(pe, b, QUARTERS * r + QUARTERS - 1)
            if r == 0:
                need(pe, x_added, 2 * b + (q - 1))
            for c in range(QUARTERS):
                last = pe.matmul(ps[c * QUARTER:(c + 1) * QUARTER, (6 + q) * HALF:(7 + q) * HALF],
                                 red[:, r * QUARTER:(r + 1) * QUARTER],
                                 h[:, (QUARTERS * r + c) * SEQ + q * HALF:(QUARTERS * r + c) * SEQ + (q + 1) * HALF],
                                 start=r == 0, stop=r == QG - 1)
            last.then_inc(summed, 1)

        def back_to_tokens(b, q):
            need(pe, y_taken, 2 * b + (q + 1))
            for i in range(q * HT, (q + 1) * HT):
                last = pe.transpose(ps[:, 6 * HALF + i * P:6 * HALF + (i + 1) * P], y_t[:, i * P:(i + 1) * P], ident)
            last.then_inc(y_psum, 1)

        def row(b, behind):
            for u in range(GROUPS):
                if not behind and u in m["late"]["tensor"]:
                    m["late"]["tensor"][u]()
                broadcast(b, u)
                r, late = divmod(u - LAG - QUARTERS + 1, QUARTERS)
                if u - LAST_SUM - 2 in (0, 1) and behind:
                    back_to_tokens(b - 1, u - LAST_SUM - 2)
                if late in (0, 1) and (r >= 0 or behind):
                    state_sum(b if r >= 0 else b - 1, r % QG, late)

        for b in range(BATCH):
            pe.wait_ge(m["stacked"][b], 16 * PARTS)
            if b == 0:
                row(0, False)
        with pe.Fori(1, BATCH) as b:
            row(b, True)
        for r in range(QG):
            for q in range(2):
                if QUARTERS * r + QUARTERS - 1 + LAG + q >= GROUPS:
                    state_sum(BATCH - 1, r, q)
        for q in range(2):
            back_to_tokens(BATCH - 1, q)

    @plan.on("scalar")
    def _(act):
        act.activation(warm[:, :], m["bias_p"][:, 0:1], ACT.Exp)
        def row(b, behind):
            for u in range(GROUPS):
                if not behind and u in m["late"]["scalar"]:
                    m["late"]["scalar"][u]()
                need(act, dt_psum, b * GROUPS + (u + 1))
                act.activation(slot(u), slot(u), ACT.Exp, scale=m["scale_p"][:, group(u):group(u) + 1],
                               bias=m["bias_p"][:, group(u):group(u) + 1]).then_inc(decay_ready, 1)

        row(0, False)
        with act.Fori(1, BATCH) as b:
            row(b, True)

    def multiply(eng, done, b, u):
        need(eng, scanned, b * GROUPS + (u + 1))
        if eng is plan.nc.gpsimd:
            alone(plan, eng, "gpsimd")
        eng.tensor_tensor(h[:, u * SEQ:(u + 1) * SEQ], h[:, u * SEQ:(u + 1) * SEQ], c_rows[:, bass.ds(b * SEQ, SEQ)],
                          ALU.mult).then_inc(done, 1)

    @plan.on("vector")
    def _(dve):
        dve.wait_ge(skip_in, 16)

        def take_sums(b, q):
            need(dve, summed, 2 * QG * b + (2 * QG - 1 + q))
            dve.scalar_tensor_tensor(out=y_t[:, q * HALF:(q + 1) * HALF], in0=u_all[:, bass.ds(b * SEQ + q * HALF, HALF)],
                                     scalar=skip[:, 0:1], in1=bank(ps, 6 + q), op0=ALU.mult, op1=ALU.add).then_inc(y_taken, 1)

        def add_to_x(b, q):
            need(dve, y_psum, 2 * b + (q + 1))
            cols = bass.ds(b * SEQ + q * HALF, HALF)
            dve.tensor_tensor(x[:, cols], x[:, cols], bank(ps, 6 + q), ALU.add).then_inc(x_added, 1)

        def row(b, behind):
            for u in range(GROUPS):
                if not behind and u in m["late"]["vector"]:
                    m["late"]["vector"][u]()
                need(dve, decay_ready, b * GROUPS + (u + 1))
                need(dve, summed, 2 * (b * QG + ((u - GROUPS) // QUARTERS + 1)))
                dve.tensor_tensor_scan(h[:, u * SEQ:(u + 1) * SEQ], slot(u), inp[:, bass.ds(b * SEQ, SEQ)], 0.0,
                                       ALU.mult, ALU.add).then_inc(scanned, 1)
                if u - 1 in ON_DVE:
                    multiply(dve, prod_dve, b, u - 1)
                step = u + AHEAD - LAST_SUM
                if behind and step in (0, 1):
                    take_sums(b - 1, step)
                if behind and step in (2, 3):
                    add_to_x(b - 1, step - 2)
                if behind and step in (4, 5):
                    dve.drain()
                    statistics(dve, m, 0, b - 1, (step - 4) * HT, HT).then_inc(row_moments, 1)

        row(0, False)
        with dve.Fori(1, BATCH) as b:
            row(b, True)
        for q in range(2):
            take_sums(BATCH - 1, q)
        for q in range(2):
            add_to_x(BATCH - 1, q)
            dve.drain()
            statistics(dve, m, 0, BATCH - 1, q * HT, HT)

    @plan.on("gpsimd")
    def _(pool):
        with pool.Fori(0, BATCH) as b:
            for u in range(GROUPS):
                if u not in ON_DVE:
                    multiply(pool, prod_pool, b, u)
        need(pool, row_moments, 2 * (BATCH - 1))
        deviations(pool, m, 0, 0, BATCH - 1, row_pow, 1)




def late_memory(plan, m, t):
    sb = plan.sb
    for name, shape, dt in (
            ("b1", [P, EXPERTS], F32), ("b2", [P, EXPERTS * D], F32),
            ("rx", [P, 2, SEQ], F32), ("rx_t", [P, 2, SEQ], F32), ("gated", [P, 2, BT, WIDE], F32), ("back", [P, BATCH, SEQ], F32),
            ("logit", [P, BT, EXPERTS], F32), ("top", [P, BT], F32), ("below", [P, 2, BT, EXPERTS], F32),
            ("prob", [P, 2, BT, EXPERTS], F32), ("ranked", [P, BT, EXPERTS], F32), ("first", [P, 2, BT], F32),
            ("onehot", [P, 2, BT, EXPERTS], BF16), ("own", [P, EXPERTS], F32), ("prior", [P, 2, EXPERTS], BF16),
            ("total", [P, BT], F32), ("gate", [P, 2, BT], F32), ("cum", [P, BT, EXPERTS], F32), ("pos", [P, BT], F32),
            ("kept", [P, BT], F32), ("inside", [P, BT], F32), ("row", [P, BT], F32), ("offset", [P, BT], F32),
            ("weight", [P, TILES], F32), ("put", [P, 2, BT], I32),
            ("e_w1", [P, 4, D], F32), ("e_w2", [P, 4, D], F32), ("home", [P, EXPERTS, HT], I32), ("unfilled", [P, HT], F32), ("rows", [P, 4, HT, WIDE], F32), ("rows_t", [P, 2, HALF], F32),
            ("hidden", [P, 2, HALF], F32), ("reply", [P, EXPERTS, HALF], F32)):
        m[name] = sb(name, shape, dt)
    m["biases_in"] = plan.dma_sem("biases_in")

    @plan.on("sync")
    def _(sp):
        sp.dma_start(m["b1"][:, :], t["f_b1_t"]).then_inc(m["biases_in"], 16)
        sp.dma_start(m["b2"][:, :], t["f_b2"].rearrange("(o e) d -> o (e d)", o=1).broadcast_to([P, EXPERTS * D])).then_inc(m["biases_in"], 16)


def statistics(dve, m, use, b, first=0, tiles=BT):
    to = bass.ds(b * BT + first, tiles)
    for i in range(tiles):
        dve.bn_stats(m["stats"][:, first + i, :], m["x"][:, bass.ds(b * SEQ + (first + i) * D, D)])
    dve.drain()
    for i in range(tiles):
        dve.bn_aggr(m["moments"][:, first + i, :], m["stats"][:, first + i, :])
    dve.drain()
    dve.tensor_scalar(m["spread"][:, use, to], m["moments"][:, first:first + tiles, 1], EPS, None, ALU.add)
    return dve.tensor_scalar(m["neg_mean"][:, use, to], m["moments"][:, first:first + tiles, 0], -1.0, None, ALU.mult)


def deviations(pool, m, use, first, rows, chained, count):
    tiles = slice(first * BT, (first + rows) * BT)
    pool.tensor_tensor(m["rstd"][:, use, tiles], m["spread"][:, use, tiles], m["neg_half"][:, 0:rows * BT],
                       ALU.pow).then_inc(chained, 1)
    need(pool, chained, count)
    return pool.tensor_tensor(m["shift"][:, use, tiles], m["neg_mean"][:, use, tiles], m["rstd"][:, use, tiles], ALU.mult)


class Router:

    TRANSPOSED, LOGITS, COUNTS = 0, 6, 7

    def __init__(self, plan, ps, m, tr):
        self.plan, self.ps, self.m, self.tr = plan, ps, m, tr
        self.moments = plan.sem("vector", "r_moments")
        self.rstd = plan.sem("gpsimd", "r_rstd")
        self.exp, self.gated = plan.sems("scalar", "r_exp r_gated")
        self.logit_psum, self.count_psum = plan.sems("tensor", "r_logit_psum r_count_psum")
        self.normal, self.logit_read, self.below, self.hot, self.gate, self.placed = plan.sems(
            "vector", "r_normal r_logit_read r_below r_hot r_gate r_placed")
        self.put_done = [plan.dma_sem(f"put{b}") for b in range(BATCH)]

    def scattered(self, n):
        return self.put_done[n % BATCH], (n // BATCH + 1) * 16 * BT

    def normalize(self, dve, n):
        m, use = self.m, 0 if n < BATCH else 2
        if n >= BATCH - 1:
            need(dve, self.rstd, n - BATCH + 2)
        need(dve, self.tr.full, self.tr.at("r", n - 2))
        need(dve, self.gated, (n - 1) * BT)
        for i in range(BT):
            tile = n % BATCH * BT + i
            dve.tensor_scalar(m["rx"][:, n % 2, i * D:(i + 1) * D], m["x"][:, tile * D:(tile + 1) * D],
                              m["rstd"][:, use, tile:tile + 1], m["shift"][:, use, tile:tile + 1],
                              ALU.mult, ALU.add).then_inc(self.normal, 1)

    def transpose(self, pe, n):
        self.tr.transpose(pe, "r", n, self.m["rx"][:, n % 2, :], self.normal, n * BT + 1)

    def copy(self, act, n):
        need(act, self.logit_psum, n - 1)
        self.tr.copy(act, "r", n, self.m["rx_t"][:, n % 2, :])

    def logits(self, pe, n):
        self.tr.need_copy(pe, "r", n)
        need(pe, self.logit_read, n)
        for i in range(BT):
            last = pe.matmul(self.ps[:, self.LOGITS * HALF + i * EXPERTS:self.LOGITS * HALF + (i + 1) * EXPERTS],
                             self.m["rx_t"][:, n % 2, i * P:(i + 1) * P], self.m["w_r"][:, :], start=True, stop=True)
        last.then_inc(self.logit_psum, 1)

    def choose(self, dve, n):
        m, q = self.m, n % 2
        wide = lambda a: a.rearrange("p (i o) -> p i o", o=1).broadcast_to([P, BT, EXPERTS])
        same = lambda a: a.rearrange("p (o e) -> p o e", o=1).broadcast_to([P, BT, EXPERTS])
        rank = same(m["const"][:, C_RANK:C_RANK + EXPERTS])
        need(dve, self.logit_psum, n + 1)
        dve.tensor_tensor(m["logit"][:, :, :], bank(self.ps, self.LOGITS)[:, 0:BT * EXPERTS].rearrange("p (i e) -> p i e", e=EXPERTS),
                          same(m["b_r"][:, :]), ALU.add).then_inc(self.logit_read, 1)
        dve.drain()
        dve.tensor_reduce(m["top"][:, :], m["logit"][:, :, :], AX, ALU.max)
        dve.drain()
        need(dve, self.exp, n - 1)
        dve.tensor_tensor(m["below"][:, q, :, :], m["logit"][:, :, :], wide(m["top"][:, :]), ALU.subtract).then_inc(self.below, 1)
        dve.drain()
        dve.scalar_tensor_tensor(out=m["ranked"][:, :, :], in0=m["below"][:, q, :, :], scalar=0.0, in1=rank,
                                 op0=ALU.is_equal, op1=ALU.mult)
        dve.drain()
        dve.tensor_reduce(m["first"][:, q, :], m["ranked"][:, :, :], AX, ALU.max)
        dve.drain()
        need(dve, self.count_psum, n - 1)
        dve.tensor_tensor(m["onehot"][:, q, :, :], wide(m["first"][:, q, :]), rank, ALU.is_equal).then_inc(self.hot, 1)
        if n % BATCH < BATCH - 1:
            dve.drain()
            dve.tensor_reduce(m["own"][:, :], m["onehot"][:, q, :, :].rearrange("p i e -> p e i"), AX, ALU.add)
            dve.drain()
            need(dve, self.count_psum, n)
            dve.tensor_tensor(m["prior"][:, 1 - q, :], m["prior"][:, q, :], m["own"][:, :], ALU.add)

    def probabilities(self, act, n):
        need(act, self.below, n + 1)
        need(act, self.placed, n - 1)
        act.activation(self.m["prob"][:, n % 2, :, :], self.m["below"][:, n % 2, :, :], ACT.Exp).then_inc(self.exp, 1)

    def count(self, pe, n):
        m, q, at = self.m, n % 2, self.COUNTS * HALF
        need(pe, self.hot, n + 1)
        need(pe, self.placed, n)
        counts = self.ps[:, at:at + BT * EXPERTS]
        pe.matmul(counts, m["tri"][:, :], m["onehot"][:, q, :, :].rearrange("p i e -> p (i e)"), start=True, stop=False)
        for i in range(BT - 1):
            pe.matmul(self.ps[:, at + (i + 1) * EXPERTS:at + BT * EXPERTS], m["ones"][:, :],
                      m["onehot"][:, q, i:i + 1, :].broadcast_to([P, BT - 1 - i, EXPERTS]), start=False, stop=False)
        pe.matmul(counts, m["ones"][:, :], m["prior"][:, q:q + 1, :].broadcast_to([P, BT, EXPERTS]),
                  start=False, stop=True).then_inc(self.count_psum, 1)

    def place(self, dve, n):
        m, q, b = self.m, n % 2, n % BATCH
        token = m["const"][:, C_TOKEN + b * BT:C_TOKEN + (b + 1) * BT]
        need(dve, self.exp, n + 1)
        dve.tensor_reduce(m["total"][:, :], m["prob"][:, q, :, :], AX, ALU.add)
        dve.drain()
        need(dve, self.gated, (n - 1) * BT)
        dve.reciprocal(m["gate"][:, q, :], m["total"][:, :]).then_inc(self.gate, 1)
        need(dve, self.count_psum, n + 1)
        dve.tensor_tensor(m["cum"][:, :, :], bank(self.ps, self.COUNTS)[:, 0:BT * EXPERTS].rearrange("p (i e) -> p i e", e=EXPERTS),
                          m["onehot"][:, q, :, :], ALU.mult)
        dve.drain()
        dve.tensor_reduce(m["pos"][:, :], m["cum"][:, :, :], AX, ALU.add)
        dve.drain()
        dve.tensor_scalar(m["kept"][:, :], m["pos"][:, :], float(CAP), None, ALU.is_lt)
        dve.scalar_tensor_tensor(out=m["inside"][:, :], in0=m["pos"][:, :], scalar=float(CAP), in1=m["pos"][:, :],
                                 op0=ALU.is_lt, op1=ALU.mult)
        dve.drain()
        dve.scalar_tensor_tensor(out=m["row"][:, :], in0=m["first"][:, q, :], scalar=-float(CAP), in1=m["inside"][:, :],
                                 op0=ALU.mult, op1=ALU.add)
        dve.tensor_tensor(m["weight"][:, b * BT:(b + 1) * BT], m["kept"][:, :], m["gate"][:, q, :], ALU.mult)
        dve.drain()
        dve.scalar_tensor_tensor(out=m["offset"][:, :], in0=m["row"][:, :], scalar=float(EXPERTS * CAP), in1=token,
                                 op0=ALU.add, op1=ALU.subtract)
        dve.drain()
        dve.tensor_tensor(m["offset"][:, :], m["offset"][:, :], m["kept"][:, :], ALU.mult)
        dve.drain()
        if n >= 2:
            dve.wait_ge(*self.scattered(n - 2))
        dve.tensor_copy(m["gated"][:, q, :, D], token)
        dve.tensor_tensor(m["put"][:, q, :], m["offset"][:, :], token, ALU.add).then_inc(self.placed, 1)

    def gate_rows(self, act, n):
        m, q = self.m, n % 2
        need(act, self.gate, n + 1)
        if n >= 2:
            act.wait_ge(*self.scattered(n - 2))
        for i in range(BT):
            act.activation(m["gated"][:, q, i, 0:D], m["rx"][:, q, i * D:(i + 1) * D], ACT.Copy,
                           scale=m["gate"][:, q, i:i + 1]).then_inc(self.gated, 1)

    def scatter(self, pool, n):
        m, q = self.m, n % 2
        need(pool, self.placed, n + 1)
        for i in range(BT):
            need(pool, self.gated, n * BT + i + 1)
            pool.indirect_dma_start(out=m["slots"][n // BATCH], out_offset=bass.IndirectOffsetOnAxis(m["put"][:, q, i:i + 1], 0),
                                    in_=m["gated"][:, q, i, :], in_offset=None).then_inc(self.put_done[n % BATCH], 16)


class Transposer:

    def __init__(self, plan, ps, m, order):
        self.ps, self.m, self.order = ps, m, order
        self.full, self.left = plan.sem("tensor", "tr_full"), plan.sem("scalar", "tr_left")

    def at(self, who, n):
        return 2 * (self.order.index((who, n)) + 1) if n >= 0 else 0

    def transpose(self, pe, who, n, src, ready, first):
        at = self.at(who, n)
        for i in range(BT):
            if i % HT == 0:
                need(pe, self.left, at - 3 + i // HT)
            need(pe, ready, first + (i if who != "v" else 0))
            last = pe.transpose(self.ps[:, i * P:(i + 1) * P], src[:, i * D:(i + 1) * D], self.m["const"][:, C_ID:C_ID + P])
            if i % HT == HT - 1:
                last.then_inc(self.full, 1)

    def copy(self, act, who, n, dst):
        at = self.at(who, n)
        for h in range(2):
            need(act, self.full, at - 1 + h)
            act.copy(dst[:, h * HALF:(h + 1) * HALF], bank(self.ps, h)).then_inc(self.left, 1)

    def need_copy(self, pe, who, n, h=1):
        need(pe, self.left, self.at(who, n) - 1 + h)


class Experts:

    ROWS, HIDDEN, REPLY = 0, 2, 4
    PAIRS = EXPERTS // 2

    def __init__(self, plan, ps, m, t, router):
        self.plan, self.ps, self.m, self.t, self.router = plan, ps, m, t, router
        self.rows_psum, self.hidden_psum, self.reply_psum = plan.sems("tensor", "e_rows_psum e_hidden_psum e_reply_psum")
        self.rows_t, self.hidden = plan.sems("scalar", "e_rows_t e_hidden")
        self.reply, self.home = plan.sems("vector", "e_reply e_home")
        self.w_in = [plan.dma_sem(f"e_w_in{k}") for k in range(2)]
        self.rows_in = [plan.dma_sem(f"e_rows_in{i}") for i in range(4)]
        self.sent = plan.dma_sem("e_sent")
        self.all_sent = 16 * EXPERTS * HT

    def load_weights(self, sp, layer, pair):
        e, k = 2 * pair, pair % 2
        need(sp, self.reply_psum, layer * EXPERTS + e - 2)
        for w, src in (("e_w1", "f_W1"), ("e_w2", "f_W2")):
            sp.dma_start(self.m[w][:, 2 * k:2 * k + 2, :], self.t[src][e:e + 2, :, :].rearrange("e d f -> d e f")).then_inc(self.w_in[k], 16)

    def load_rows(self, sp, layer, pair):
        for e in (2 * pair, 2 * pair + 1):
            i = e % 4
            need(sp, self.rows_psum, layer * EXPERTS + e - 3)
            need(sp, self.home, layer * EXPERTS + e - 3)
            sp.dma_start(self.m["rows"][:, i, :, :].rearrange("p j d -> p (j d)"),
                         self.m["slots"][layer][e * CAP:(e + 1) * CAP, :].rearrange("(p j) d -> p (j d)", p=P)).then_inc(self.rows_in[i], 16)

    def sync(self, sp, layer):
        for pair in range(2):
            self.load_weights(sp, layer, pair)
        for b in range(BATCH):
            sp.wait_ge(*self.router.scattered(layer * BATCH + b))
        for pair in range(2):
            self.load_rows(sp, layer, pair)
        for pair in range(2, self.PAIRS):
            self.load_rows(sp, layer, pair)
            self.load_weights(sp, layer, pair)

    def tensor(self, pe, layer):
        m, ps, ident = self.m, self.ps, self.m["const"][:, C_ID:C_ID + P]
        turn = layer * (EXPERTS // 4) + 1
        with pe.Fori(0, EXPERTS // 4) as c:
            def transpose(i):
                pe.wait_ge(self.rows_in[i], c * 16 + turn * 16)
                need(pe, self.rows_t, c * 4 + (layer * EXPERTS + i - 1))
                at = (self.ROWS + i % 2) * HALF
                for j in range(HT):
                    last = pe.transpose(ps[:, at + j * P:at + (j + 1) * P], m["rows"][:, i, j, 0:D], ident)
                last.then_inc(self.rows_psum, 1)

            def first(i):
                e = c * 4 + (layer * EXPERTS + i)
                if i % 2 == 0:
                    pe.wait_ge(self.w_in[i // 2], c * 32 + turn * 32)
                need(pe, self.rows_t, e + 1)
                need(pe, self.hidden, e - 1)
                pe.matmul(bank(ps, self.HIDDEN + i % 2), m["e_w1"][:, i, :], m["rows_t"][:, i % 2, :], start=True,
                          stop=True).then_inc(self.hidden_psum, 1)

            def second(i):
                e = c * 4 + (layer * EXPERTS + i)
                need(pe, self.hidden, e + 1)
                need(pe, self.reply, e - 1)
                at = (self.REPLY + i % 2) * HALF
                for j in range(HT):
                    last = pe.matmul(ps[:, at + j * D:at + (j + 1) * D], m["hidden"][:, i % 2, j * P:(j + 1) * P],
                                     m["e_w2"][:, i, :], start=True, stop=True)
                last.then_inc(self.reply_psum, 1)

            transpose(0)
            for i in range(4):
                first(i)
                if i < 3:
                    transpose(i + 1)
                second(i)

    def scalar(self, act, layer):
        m, ps = self.m, self.ps
        if layer == 0:
            act.wait_ge(m["biases_in"], 32)
        with act.Fori(0, EXPERTS // 4) as c:
            def rows(i):
                e = c * 4 + (layer * EXPERTS + i)
                need(act, self.rows_psum, e + 1)
                need(act, self.hidden_psum, e - 1)
                act.copy(m["rows_t"][:, i % 2, :], bank(ps, self.ROWS + i % 2)).then_inc(self.rows_t, 1)

            def hide(i):
                e = c * 4 + (layer * EXPERTS + i)
                need(act, self.hidden_psum, e + 1)
                need(act, self.reply_psum, e - 1)
                act.activation(m["hidden"][:, i % 2, :], bank(ps, self.HIDDEN + i % 2), ACT.Relu,
                               bias=m["b1"][:, bass.ds(c * 4 + i, 1)]).then_inc(self.hidden, 1)

            rows(0)
            for i in range(4):
                hide(i)
                if i < 3:
                    rows(i + 1)

    def vector(self, dve, layer):
        m, ps = self.m, self.ps
        if layer == 0:
            dve.wait_ge(m["biases_in"], 32)
        else:
            dve.wait_ge(self.sent, self.all_sent)
        with dve.Fori(0, EXPERTS // 4) as c:
            for i in range(4):
                e = c * 4 + i
                dve.drain()
                dve.wait_ge(self.rows_in[i], c * 16 + (layer * (EXPERTS // 4) + 1) * 16)
                carried = m["rows"][:, i, :, D]
                own = m["const"][:, bass.ds(c * (4 * HT) + (C_SLOT + i * HT), HT)]
                dve.scalar_tensor_tensor(out=m["unfilled"][:, :], in0=carried, scalar=0.0, in1=own, op0=ALU.is_equal, op1=ALU.mult)
                dve.drain()
                dve.tensor_tensor(m["home"][:, bass.ds(e, 1), :].rearrange("p o j -> p (o j)"), carried, m["unfilled"][:, :],
                                  ALU.add).then_inc(self.home, 1)
                need(dve, self.reply_psum, c * 4 + (layer * EXPERTS + i + 1))
                dve.tensor_tensor(m["reply"][:, bass.ds(e, 1), :].rearrange("p o (j d) -> p (o j) d", d=D),
                                  bank(ps, self.REPLY + i % 2).rearrange("p (j d) -> p j d", d=D),
                                  m["b2"][:, bass.ds(e * D, D)].rearrange("p (o d) -> p o d", o=1).broadcast_to([P, HT, D]),
                                  ALU.add).then_inc(self.reply, 1)

    def gpsimd(self, pool, layer):
        m = self.m
        for e in range(EXPERTS):
            need(pool, self.reply, layer * EXPERTS + e + 1)
            for j in range(HT):
                pool.indirect_dma_start(out=m["answers"], out_offset=bass.IndirectOffsetOnAxis(m["home"][:, e, j:j + 1], 0),
                                        in_=m["reply"][:, e, j * D:(j + 1) * D], in_offset=None).then_inc(self.sent, 16)


class Answers:

    def __init__(self, plan, m, experts):
        self.m, self.experts = m, experts
        self.got = [plan.dma_sem(f"got{b}") for b in range(BATCH)]
        self.added = plan.sem("vector", "a_added")

    def fetch(self, sp, layer):
        sp.wait_ge(self.experts.sent, (layer + 1) * self.experts.all_sent)
        for b in range(BATCH):
            need(sp, self.added, (layer - 1) * BATCH + b + 1)
            sp.dma_start(self.m["back"][:, b, :].rearrange("p (i d) -> p i d", d=D),
                         self.m["answers"][TOKENS + b * SEQ:TOKENS + (b + 1) * SEQ, :].rearrange("(i p) d -> p i d", p=P)).then_inc(self.got[b], 16)

    def add(self, dve, layer, b):
        m = self.m
        dve.wait_ge(self.got[b], (layer + 1) * 16)
        for i in range(BT):
            tile = b * BT + i
            last = dve.scalar_tensor_tensor(out=m["x"][:, tile * D:(tile + 1) * D], in0=m["back"][:, b, i * D:(i + 1) * D],
                                            scalar=m["weight"][:, tile:tile + 1], in1=m["x"][:, tile * D:(tile + 1) * D],
                                            op0=ALU.mult, op1=ALU.add)
        last.then_inc(self.added, 1)


class Conv:

    U0, Y, U2, OUT = 2, 2, 4, 4
    PAD = TAPS - 1

    def __init__(self, plan, ps, m, t, tr):
        self.plan, self.ps, self.m, self.t, self.tr = plan, ps, m, t, tr
        sb = plan.sb
        self.w_in, self.w_out = sb("c_w_in", [P, 2, D]), sb("c_w_out", [P, D])
        self.b_in, self.b_tap, self.w_tap = sb("c_b_in", [P, 3]), sb("c_b_tap", [P, 3]), sb("c_w_tap", [P, 2, TAPS])
        self.w1, self.w2, self.w3 = sb("c_w1", [TAPS, FW]), sb("c_w2", [FW, FW]), sb("c_w3", [FW, D])
        self.b1, self.b2, self.b_out = sb("c_b1", [FW, 1]), sb("c_b2", [FW, 1]), sb("c_b_out", [P, D])
        self.time0, self.filt_bias = sb("time0", [TAPS, 1]), sb("filt_bias", [P, 1])
        self.col, self.row = sb("mlp_col", [FW, 2, 4]), sb("mlp_row", [1, 3, D])
        self.flipped, self.toep = sb("flipped", [P, 2 * P]), sb("toep", [P, 2 * P])
        self.xn, self.xt = sb("c_xn", [P, 2, SEQ]), sb("c_xt", [P, 2, SEQ])
        self.u = sb("c_u", [P, 2, 2, self.PAD + SEQ])
        self.s, self.v, self.vt, self.z = sb("c_s", [P, 2, 2, SEQ]), sb("c_v", [P, 2, SEQ]), sb("c_vt", [P, 2, SEQ]), sb("c_z", [P, 2, SEQ])
        self.weights_in, self.taps_out, self.taps_in = plan.dma_sem("c_weights_in"), plan.dma_sem("taps_out"), plan.dma_sem("taps_in")
        self.cleared, self.rstd, self.v_done, self.biased = plan.sems("gpsimd", "c_cleared c_rstd c_v c_biased")
        self.mlp_psum, self.flip_psum, self.u_psum, self.y_psum, self.o_psum = plan.sems(
            "tensor", "c_mlp_psum c_flip_psum c_u_psum c_y_psum c_o_psum")
        self.mlp_exp, self.row_abs, self.toep_done, self.normal, self.u_done, self.s_first = plan.sems(
            "scalar", "c_mlp_exp c_row_abs c_toep c_normal c_u c_s_first")
        self.mlp, self.moments, self.s_done, self.y_read, self.z_done, self.x_done = plan.sems(
            "vector", "c_mlp c_moments c_s c_y_read c_z c_x")

    def load(self, sp):
        t, by_one = self.t, lambda a: a.rearrange("(f o) -> f o", o=1)
        loads = ((self.w_in[:, :, :], t["b_w_in"].rearrange("d (s e) -> d s e", s=3)[:, 0:3:2, :]), (self.b_in[:, :], t["b_b_in_t"]),
                 (self.w_tap[:, :, :], t["b_w_conv"].rearrange("(s e) o j -> e s (o j)", s=3)[:, 0:3:2, :]),
                 (self.b_tap[:, :], t["b_b_conv_t"]), (self.w1[:, :], t["b_w1"]), (self.w2[:, :], t["b_w2"]),
                 (self.w3[:, :], t["b_w3"]), (self.b1[:, :], by_one(t["b_b1"])), (self.b2[:, :], by_one(t["b_b2"])),
                 (self.filt_bias[:, :], by_one(t["b_filt_bias"])),
                 (self.row[:, 0, :], t["b_filt_bias"].rearrange("(o f) -> o f", o=1)),
                 (self.w_out[:, :], t["b_w_out"]), (self.b_out[:, :], t["b_b_out"].rearrange("(o f) -> o f", o=1).broadcast_to([P, D])))
        self.n_weights = 16 * len(loads)
        for dst, src in loads:
            sp.dma_start(dst, src).then_inc(self.weights_in, 16)

    def filter_sync(self, sp):
        taps = self.m["taps"]
        need(sp, self.mlp, 5)
        sp.dma_start(taps[:, P - 1:2 * P - 1], self.row[:, 2, :]).then_inc(self.taps_out, 16)
        sp.wait_ge(self.taps_out, 16)
        shifted = bass.AP(tensor=taps.tensor, offset=taps.offset, ap=[[1, P], [1, 2 * P]])
        sp.dma_start(self.flipped[:, :], shifted).then_inc(self.taps_in, 16)

    def clear(self, pool):
        pool.memset(self.time0[:, :], 0.0)
        pool.memset(self.u[:, :, :, 0:self.PAD], 0.0).then_inc(self.cleared, 1)

    def filter_tensor(self, pe):
        at = lambda i: slice((2 + i) * HALF, (2 + i) * HALF + 1)
        pe.wait_ge(self.weights_in, self.n_weights)
        need(pe, self.cleared, 1)
        pe.matmul(self.ps[0:FW, at(0)], self.w1[:, :], self.time0[:, :], start=True, stop=True).then_inc(self.mlp_psum, 1)
        need(pe, self.mlp, 2)
        pe.matmul(self.ps[0:FW, at(1)], self.w2[:, :], self.col[:, 0, 3:4], start=True, stop=True).then_inc(self.mlp_psum, 1)
        need(pe, self.mlp, 4)
        pe.matmul(self.ps[0:1, 4 * HALF:4 * HALF + D], self.col[:, 1, 3:4], self.w3[:, :], start=True, stop=True).then_inc(self.mlp_psum, 1)

    def toeplitz_tensor(self, pe):
        pe.wait_ge(self.taps_in, 16)
        pe.matmul(self.ps[:, 5 * HALF:5 * HALF + 2 * P], self.m["const"][:, C_FLIP:C_FLIP + P], self.flipped[:, :], start=True,
                  stop=True).then_inc(self.flip_psum, 1)

    def filter_scalar(self, act):
        act.wait_ge(self.weights_in, self.n_weights)
        act.activation(self.row[:, 1, :], self.row[:, 0, :], ACT.Abs).then_inc(self.row_abs, 1)
        for layer in range(2):
            need(act, self.mlp, 2 * layer + 1)
            act.activation(self.col[:, layer, 1:2], self.col[:, layer, 0:1], ACT.Exp, scale=-1.0).then_inc(self.mlp_exp, 1)
        need(act, self.row_abs, 1)
        act.activation(self.row[:, 1, :], self.row[:, 1, :], ACT.Exp, scale=-0.0).then_inc(self.mlp_exp, 1)

    def toeplitz_scalar(self, act):
        need(act, self.flip_psum, 1)
        act.copy(self.toep[:, :], self.ps[:, 5 * HALF:5 * HALF + 2 * P]).then_inc(self.toep_done, 1)

    def filter_vector(self, dve):
        dve.wait_ge(self.weights_in, self.n_weights)
        for layer, bias in ((0, self.b1), (1, self.b2)):
            c = lambda i: self.col[:, layer, i:i + 1]
            need(dve, self.mlp_psum, layer + 1)
            dve.tensor_tensor(c(0), self.ps[0:FW, (2 + layer) * HALF:(2 + layer) * HALF + 1], bias[:, :], ALU.add).then_inc(self.mlp, 1)
            need(dve, self.mlp_exp, layer + 1)
            dve.tensor_scalar(c(1), c(1), 1.0, None, ALU.add)
            dve.drain()
            dve.reciprocal(c(2), c(1))
            dve.drain()
            dve.tensor_tensor(c(3), c(0), c(2), ALU.mult).then_inc(self.mlp, 1)
        need(dve, self.mlp_exp, 3)
        need(dve, self.mlp_psum, 3)
        dve.tensor_tensor(self.row[:, 2, :], self.ps[0:1, 4 * HALF:4 * HALF + D], self.row[:, 1, :], ALU.mult).then_inc(self.mlp, 1)

    def normalize(self, act, b):
        need(act, self.rstd, b + 1)
        need(act, self.tr.full, self.tr.at("c", b - 2))
        for i in range(BT):
            tile = b * BT + i
            act.activation(self.xn[:, b % 2, i * D:(i + 1) * D], self.m["x"][:, tile * D:(tile + 1) * D], ACT.Identity,
                           scale=self.m["rstd"][:, 1, tile:tile + 1], bias=self.m["shift"][:, 1, tile:tile + 1]).then_inc(self.normal, 1)

    def transpose(self, pe, b):
        self.tr.transpose(pe, "c", b, self.xn[:, b % 2, :], self.normal, b * BT + 1)

    def copy(self, act, b):
        need(act, self.u_psum, 2 * b - 2)
        self.tr.copy(act, "c", b, self.xt[:, b % 2, :])

    def streams(self, pe, b):
        for s, at in enumerate((self.U0, self.U2)):
            if s == 0:
                need(pe, self.y_read, b - 1)
            else:
                need(pe, self.x_done, b - 1)
            for q in range(2):
                self.tr.need_copy(pe, "c", b, q)
                last = pe.matmul(bank(self.ps, at + q), self.w_in[:, s, :], self.xt[:, b % 2, q * HALF:(q + 1) * HALF],
                                 start=True, stop=True)
            last.then_inc(self.u_psum, 1)

    def take_streams(self, act, b):
        q = b % 2
        for s, at in enumerate((self.U0, self.U2)):
            need(act, self.u_psum, 2 * b + s + 1)
            need(act, self.s_done, 2 * b - 2 + s)
            act.activation(self.u[:, q, s, self.PAD:], bank(self.ps, at, 2), ACT.Identity,
                           bias=self.b_in[:, 2 * s:2 * s + 1]).then_inc(self.u_done, 1)

    def first_tap(self, act, b):
        q = b % 2
        for s in range(2):
            need(act, self.u_done, 2 * b + s + 1)
            need(act, self.z_done, b - 1)
            act.activation(self.s[:, q, s, :], self.u[:, q, s, 0:SEQ], ACT.Identity, scale=self.w_tap[:, s, 0:1],
                           bias=self.b_tap[:, 2 * s:2 * s + 1]).then_inc(self.s_first, 1)

    def taps(self, dve, b):
        q = b % 2
        for j in range(1, TAPS):
            for s in range(2):
                if j == 1:
                    need(dve, self.s_first, 2 * b + s + 1)
                last = dve.scalar_tensor_tensor(out=self.s[:, q, s, :], in0=self.u[:, q, s, j:j + SEQ],
                                                scalar=self.w_tap[:, s, j:j + 1], in1=self.s[:, q, s, :],
                                                op0=ALU.mult, op1=ALU.add)
                if j == TAPS - 1:
                    last.then_inc(self.s_done, 1)
            if j < TAPS - 1:
                dve.drain()

    def product(self, pool, b):
        q = b % 2
        need(pool, self.s_done, 2 * b + 2)
        need(pool, self.y_read, b - 1)
        pool.tensor_tensor(self.v[:, q, :], self.s[:, q, 1, :], self.s[:, q, 0, :], ALU.mult).then_inc(self.v_done, 1)

    def bias(self, pool, b):
        x = self.m["x"][:, b * SEQ:(b + 1) * SEQ].rearrange("p (i d) -> p i d", d=D)
        if b == 0:
            pool.wait_ge(self.weights_in, self.n_weights)
        need(pool, self.normal, (b + 1) * BT)
        pool.tensor_tensor(x, x, self.b_out[:, :].rearrange("p (o d) -> p o d", o=1).broadcast_to([P, BT, D]),
                           ALU.add).then_inc(self.biased, 1)

    def v_transpose(self, pe, b):
        self.tr.transpose(pe, "v", b, self.v[:, b % 2, :], self.v_done, b + 1)

    def v_copy(self, act, b):
        need(act, self.y_psum, b - 1)
        self.tr.copy(act, "v", b, self.vt[:, b % 2, :])

    def long_conv(self, pe, b):
        need(pe, self.toep_done, 1)
        need(pe, self.u_done, min(2 * b + 3, 2 * BATCH - 1))
        need(pe, self.y_read, b)
        for h in range(2):
            self.tr.need_copy(pe, "v", b, h)
            first = h * HT
            steps = [(first, 2), (first + 2, 2), (first + 1, 2), (first + HT - 1, 1)] + ([(first - 1, 0)] if h else [])
            for j, tiles in steps:
                y0, t0, n = (j, 0, tiles) if tiles else (j + 1, 1, 1)
                last = pe.matmul(self.ps[:, self.Y * HALF + y0 * P:self.Y * HALF + (y0 + n) * P],
                                 self.vt[:, b % 2, j * D:(j + 1) * D], self.toep[:, t0 * P:(t0 + n) * P],
                                 start=j == first, stop=(j, tiles) == steps[-1])
        last.then_inc(self.y_psum, 1)

    def gate_y(self, dve, b):
        q = b % 2
        need(dve, self.y_psum, b + 1)
        need(dve, self.o_psum, b - 1)
        need(dve, self.v_done, b + 1)
        dve.scalar_tensor_tensor(out=self.z[:, q, :], in0=self.v[:, q, :], scalar=self.filt_bias[:, 0:1],
                                 in1=bank(self.ps, self.Y, 2), op0=ALU.mult, op1=ALU.add).then_inc(self.y_read, 1)
        dve.drain()
        dve.tensor_tensor(self.z[:, q, :], self.z[:, q, :], self.s[:, q, 0, :], ALU.mult).then_inc(self.z_done, 1)

    def output(self, pe, b):
        need(pe, self.z_done, b + 1)
        need(pe, self.u_done, min(2 * (b + 1) + 2, 2 * BATCH))
        need(pe, self.x_done, b)
        for i in range(BT):
            last = pe.matmul(self.ps[:, self.OUT * HALF + i * D:self.OUT * HALF + (i + 1) * D], self.z[:, b % 2, i * P:(i + 1) * P],
                             self.w_out[:, :], start=True, stop=True)
        last.then_inc(self.o_psum, 1)

    def add(self, dve, b):
        x = self.m["x"][:, b * SEQ:(b + 1) * SEQ]
        need(dve, self.o_psum, b + 1)
        need(dve, self.biased, b + 1)
        dve.tensor_tensor(x, x, bank(self.ps, self.OUT, 2), ALU.add).then_inc(self.x_done, 1)
        dve.drain()


def row_steps(*steps):
    for k in range(BATCH + max(lag for _, lag in steps)):
        for step_of, lag in steps:
            if 0 <= k - lag < BATCH:
                step_of(k - lag)


def mixtures_and_conv(plan, ps, m, t):
    late_memory(plan, m, t)
    order = [("r", b) for b in range(BATCH)]
    row_steps((lambda b: order.append(("c", b)), 0), (lambda b: order.append(("v", b)), 1),
              (lambda b: order.append(("r", BATCH + b)), 2))
    tr = Transposer(plan, ps, m, order)
    router = Router(plan, ps, m, tr)
    experts = Experts(plan, ps, m, t, router)
    answers = Answers(plan, m, experts)
    conv = Conv(plan, ps, m, t, tr)
    r_pow, c_pow = plan.sems("gpsimd", "r_pow c_pow")
    out_done = plan.dma_sem("out_done")
    second = lambda b: BATCH + b

    @plan.on("sync")
    def _(sp):
        conv.load(sp)
        conv.filter_sync(sp)
        for layer in range(2):
            experts.sync(sp, layer)
            answers.fetch(sp, layer)
        for b in range(BATCH):
            need(sp, answers.added, BATCH + b + 1)
            sp.dma_start(t["out"][b:b + 1, :, :].rearrange("b (i p) d -> p (b i) d", p=P),
                         m["x"][:, b * SEQ:(b + 1) * SEQ].rearrange("p (i d) -> p i d", d=D)).then_inc(out_done, 16)
        sp.wait_ge(out_done, 16 * BATCH)

    @plan.on("tensor")
    def _(pe):
        row_steps((lambda b: router.transpose(pe, b), 0), (lambda b: router.count(pe, b), 1), (lambda b: router.logits(pe, b), 0))
        conv.filter_tensor(pe)
        conv.toeplitz_tensor(pe)
        experts.tensor(pe, 0)
        row_steps((lambda b: conv.output(pe, b), 2),
                  (lambda b: conv.transpose(pe, b), 0), (lambda b: conv.streams(pe, b), 0),
                  (lambda b: conv.v_transpose(pe, b), 1), (lambda b: router.count(pe, second(b)), 3),
                  (lambda b: conv.long_conv(pe, b), 1),
                  (lambda b: router.transpose(pe, second(b)), 2), (lambda b: router.logits(pe, second(b)), 2))
        experts.tensor(pe, 1)

    @plan.on("scalar")
    def _(act):
        row_steps((lambda b: router.probabilities(act, b), 1),
                  (lambda b: router.copy(act, b), 0), (lambda b: router.gate_rows(act, b), 1))
        conv.filter_scalar(act)
        conv.toeplitz_scalar(act)
        experts.scalar(act, 0)
        row_steps((lambda b: conv.normalize(act, b), 0), (lambda b: conv.copy(act, b), 0), (lambda b: conv.take_streams(act, b), 0),
                  (lambda b: conv.v_copy(act, b), 1), (lambda b: router.probabilities(act, second(b)), 3),
                  (lambda b: conv.first_tap(act, b), 0), (lambda b: router.gate_rows(act, second(b)), 3),
                  (lambda b: router.copy(act, second(b)), 2))
        experts.scalar(act, 1)

    @plan.on("vector")
    def _(dve):
        dve.memset(m["prior"][:, :, :], 0.0)
        row_steps((lambda b: router.normalize(dve, b), 0), (lambda b: router.choose(dve, b), 1), (lambda b: router.place(dve, b), 1))
        need(dve, router.count_psum, BATCH)
        dve.memset(m["prior"][:, 0, :], 0.0)
        conv.filter_vector(dve)
        experts.vector(dve, 0)

        def fetched(b):
            answers.add(dve, 0, b)
            dve.drain()
            statistics(dve, m, 1, b).then_inc(conv.moments, 1)

        def convolved(b):
            conv.add(dve, b)
            statistics(dve, m, 2, b).then_inc(router.moments, 1)

        for b in range(BATCH):
            fetched(b)
        row_steps((lambda b: conv.taps(dve, b), 1), (convolved, 2),
                  (lambda b: router.choose(dve, second(b)), 3), (lambda b: router.normalize(dve, second(b)), 2),
                  (lambda b: router.place(dve, second(b)), 3), (lambda b: conv.gate_y(dve, b), 1))
        experts.vector(dve, 1)
        for b in range(BATCH):
            answers.add(dve, 1, b)

    @plan.on("gpsimd")
    def _(pool):
        deviations(pool, m, 0, BATCH - 1, 1, r_pow, 1).then_inc(router.rstd, 1)
        conv.clear(pool)
        for b in range(BATCH):
            router.scatter(pool, b)

        def conv_rstd(b):
            need(pool, conv.moments, b + 1)
            deviations(pool, m, 1, b, 1, c_pow, b + 1).then_inc(conv.rstd, 1)

        def router_rstd(b):
            need(pool, router.moments, b + 1)
            deviations(pool, m, 2, b, 1, r_pow, b + 2).then_inc(router.rstd, 1)

        experts.gpsimd(pool, 0)
        for b in range(BATCH):
            conv_rstd(b)
        row_steps((lambda b: conv.product(pool, b), 1), (router_rstd, 2), (lambda b: router.scatter(pool, second(b)), 3),
                  (lambda b: conv.bias(pool, b), 0))
        experts.gpsimd(pool, 1)


def kernel(**inputs):
    import concourse.bacc as bacc
    from concourse.bass_utils import run_bass_kernel_spmd as run

    nc = bacc.Bacc("TRN2", target_bir_lowering=False, num_devices=1)
    a = {n.removeprefix("L0_").replace("attn_a_", "a_").replace("attn_b_", "b_").replace("ffn_", "f_"): np.asarray(v)
         for n, v in inputs.items()}
    a["x"] = a.pop("a_x")
    a["a_A_log_p"] = a["a_A_log"].reshape(GROUPS, GROUP, STATES).transpose(2, 1, 0).reshape(P, GROUPS)
    a["f_b1_t"] = a.pop("f_b1").T
    a["b_b_in_t"] = a.pop("b_b_in").reshape(3, D).T
    a["b_b_conv_t"] = a.pop("b_b_conv").reshape(3, D).T
    a["table"] = constant_table()
    arrays, t = {}, {}
    for n, v in a.items():
        v = np.ascontiguousarray(v)
        arrays["in_" + n] = v
        t[n] = nc.dram_tensor("in_" + n, v.shape, mybir.dt.from_np(v.dtype), kind="ExternalInput").ap()
    t["out"] = nc.dram_tensor("out", (BATCH, SEQ, D), F32, kind="ExternalOutput").ap()
    build(nc, t)
    return run(nc, [arrays], core_ids=[0]).results[0]["out"]
```
